# Optimizing a Trainium2 kernel written in Bass

```python
import numpy as np
import jax
import jax.numpy as jnp

def _softmax(x, axis=-1):
    return jax.nn.softmax(x, axis=axis)

def _gelu(x):
    return jax.nn.gelu(x, approximate=True)

def _silu(x):
    return jax.nn.silu(x)

def _sigmoid(x):
    return jax.nn.sigmoid(x)

def _layernorm(x, axis=-1, eps=1e-05):
    m = jnp.mean(x, axis=axis, keepdims=True)
    v = jnp.var(x, axis=axis, keepdims=True)
    return (x - m) / jnp.sqrt(v + eps)

def _scatter_add(tgt, idx, src, axis=0):
    return tgt.at[idx].add(src)

def _segment_sum(src, seg, n):
    return jax.ops.segment_sum(src, seg, n)
kernel_name = 'mk_gnn_ffn_d2_gnn_r16_6b0e25'

def setup_inputs(seed: int=0):
    np.random.seed(seed)
    _w = jnp.asarray

    def _rec_inputs():
        import jax
        import jax.numpy as jnp
        _gk = jax.random.key(seed)
        x = -0.000364 + 1 * jax.random.normal(jax.random.fold_in(_gk, 1), (1250, 768), jnp.float32)
        src = jax.random.randint(jax.random.fold_in(_gk, 2), (40000,), 0, 1250, jnp.int32)
        dst = jax.random.randint(jax.random.fold_in(_gk, 3), (40000,), 0, 1250, jnp.int32)
        _o = jnp.argsort(dst, stable=True)
        src = src[_o]
        dst = dst[_o]
        return (x, src, dst)
    x, src, dst = _rec_inputs()

    def _L0_gnn_setup():
        import jax, jax.numpy as jnp
        import numpy as np
        N, E, DIM, HEADS = (1250, 20000, 768, 8)
        HD = DIM // HEADS
        EPS = 1e-05

        def layer_norm(x, w, b):
            mu = jnp.mean(x, axis=-1, keepdims=True)
            var = jnp.var(x, axis=-1, keepdims=True)
            return (x - mu) * jax.lax.rsqrt(var + EPS) * w + b

        def gatv2(x, src, dst, Ws, bs, Wd, bd, attn):
            H, D = attn.shape
            fs = (x @ Ws + bs).reshape(-1, H, D)
            fd = (x @ Wd + bd).reshape(-1, H, D)
            e = jax.nn.leaky_relu(fs[src] + fd[dst], 0.2)
            logits = jnp.einsum('ehd,hd->eh', e, attn)
            m = jax.ops.segment_max(logits, dst, num_segments=N)
            ex = jnp.exp(logits - m[dst])
            denom = jax.ops.segment_sum(ex, dst, num_segments=N)
            alpha = ex / denom[dst]
            out = jax.ops.segment_sum(alpha[:, :, None] * fs[src], dst, num_segments=N)
            return jax.nn.elu(out)
        key = jax.random.key(seed)
        ks = jax.random.split(key, 10)
        s = 1.0 / np.sqrt(DIM)
        return {'x': jax.random.normal(ks[0], (N, DIM), jnp.float32), 'src': jax.random.randint(ks[1], (E,), 0, N, jnp.int32), 'dst': jax.random.randint(ks[2], (E,), 0, N, jnp.int32), 'W1s': jax.random.normal(ks[3], (DIM, DIM), jnp.float32) * s, 'b1s': jnp.zeros((DIM,), jnp.float32), 'W1d': jax.random.normal(ks[4], (DIM, DIM), jnp.float32) * s, 'b1d': jnp.zeros((DIM,), jnp.float32), 'attn1': jax.random.normal(ks[5], (HEADS, HD), jnp.float32) * s, 'ln1_w': jnp.ones((DIM,), jnp.float32), 'ln1_b': jnp.zeros((DIM,), jnp.float32), 'Wos': jax.random.normal(ks[6], (DIM, DIM), jnp.float32) * s, 'bos': jnp.zeros((DIM,), jnp.float32), 'Wod': jax.random.normal(ks[7], (DIM, DIM), jnp.float32) * s, 'bod': jnp.zeros((DIM,), jnp.float32), 'attno': jax.random.normal(ks[8], (1, DIM), jnp.float32) * s, 'lno_w': jnp.ones((DIM,), jnp.float32), 'lno_b': jnp.zeros((DIM,), jnp.float32)}
    _L0_gnn_all = _L0_gnn_setup()
    _L0_gnn_in = {k: v for k, v in _L0_gnn_all.items() if k in ('W1s', 'b1s', 'W1d', 'b1d', 'attn1', 'ln1_w', 'ln1_b', 'Wos', 'bos', 'Wod', 'bod', 'attno', 'lno_w', 'lno_b')}
    del _L0_gnn_all

    def _L0_ffn_setup():
        import jax, jax.numpy as jnp
        import numpy as np
        B, L, D = (4, 1024, 768)
        E, S, H = (32, 32, 192)
        EPS = 1e-12

        def _l2norm(v, axis):
            n = jnp.sqrt(jnp.sum(v * v, axis=axis, keepdims=True))
            return v / jnp.maximum(n, EPS)
        key = jax.random.key(seed)
        ks = jax.random.split(key, 6)
        x = jax.random.normal(ks[0], (B, L, D), dtype=jnp.float32)
        phi = jax.random.normal(ks[1], (D, E, S), dtype=jnp.float32) / np.sqrt(D)
        scale = jnp.ones((1,), dtype=jnp.float32)
        w1 = jax.random.normal(ks[2], (E, D, H), dtype=jnp.float32) / np.sqrt(D)
        b1 = jax.random.normal(ks[3], (E, H), dtype=jnp.float32) * 0.01
        w2 = jax.random.normal(ks[4], (E, H, D), dtype=jnp.float32) / np.sqrt(H)
        b2 = jax.random.normal(ks[5], (E, D), dtype=jnp.float32) * 0.01
        return {'x': x, 'phi': phi, 'scale': scale, 'w1': w1, 'b1': b1, 'w2': w2, 'b2': b2}
    _L0_ffn_all = _L0_ffn_setup()
    _L0_ffn_in = {k: v for k, v in _L0_ffn_all.items() if k in ('phi', 'scale', 'w1', 'b1', 'w2', 'b2')}
    del _L0_ffn_all

    def _L1_gnn_setup():
        import jax, jax.numpy as jnp
        import numpy as np
        N_NODES = 625
        D = 768
        N_EDGES = 10000

        def gcn_conv(x, W, b, src, dst, n_nodes):
            h = x @ W
            deg = jax.ops.segment_sum(jnp.ones_like(dst, dtype=h.dtype), dst, num_segments=n_nodes)
            dinv = jnp.where(deg > 0, jax.lax.rsqrt(deg), 0.0)
            norm = dinv[src] * dinv[dst]
            msgs = h[src] * norm[:, None]
            out = jax.ops.segment_sum(msgs, dst, num_segments=n_nodes)
            return out + b

        def add_self_loops(edge_index, n_nodes):
            loop = jnp.arange(n_nodes, dtype=edge_index.dtype)
            src = jnp.concatenate([edge_index[0], loop])
            dst = jnp.concatenate([edge_index[1], loop])
            return (src, dst)
        key = jax.random.key(seed)
        k1, k2, k3, k4 = jax.random.split(key, 4)
        x = jax.random.normal(k1, (N_NODES, D), dtype=jnp.float32)
        edge_index = jax.random.randint(k2, (2, N_EDGES), 0, N_NODES, dtype=jnp.int32)
        glorot = float(np.sqrt(6.0 / (D + D)))
        W1 = jax.random.uniform(k3, (D, D), jnp.float32, -glorot, glorot)
        W2 = jax.random.uniform(k4, (D, D), jnp.float32, -glorot, glorot)
        b1 = jnp.zeros((D,), jnp.float32)
        b2 = jnp.zeros((D,), jnp.float32)
        return {'x': x, 'W1': W1, 'b1': b1, 'W2': W2, 'b2': b2, 'edge_index': edge_index}
    _L1_gnn_all = _L1_gnn_setup()
    _L1_gnn_in = {k: v for k, v in _L1_gnn_all.items() if k in ('W1', 'b1', 'W2', 'b2')}
    del _L1_gnn_all

    def _L1_ffn_setup():
        import jax, jax.numpy as jnp
        import numpy as np
        EMB = 768
        HID = 1152
        NUM_EXPERTS = 8
        TOP_K = 2
        key = jax.random.key(seed)
        ks = jax.random.split(key, 8)
        s = 0.02
        x = jax.random.normal(ks[0], (4, 1024, EMB), dtype=jnp.float32)
        router_w = jax.random.normal(ks[1], (EMB, NUM_EXPERTS), dtype=jnp.float32) * s
        router_b = jnp.zeros((NUM_EXPERTS,), dtype=jnp.float32)
        w1 = jax.random.normal(ks[2], (NUM_EXPERTS, EMB, HID), dtype=jnp.float32) * s
        b1 = jnp.zeros((NUM_EXPERTS, HID), dtype=jnp.float32)
        w2 = jax.random.normal(ks[3], (NUM_EXPERTS, HID, EMB), dtype=jnp.float32) * s
        b2 = jnp.zeros((NUM_EXPERTS, EMB), dtype=jnp.float32)
        return {'x': x, 'router_w': router_w, 'router_b': router_b, 'w1': w1, 'b1': b1, 'w2': w2, 'b2': b2}
    _L1_ffn_all = _L1_ffn_setup()
    _L1_ffn_in = {k: v for k, v in _L1_ffn_all.items() if k in ('router_w', 'router_b', 'w1', 'b1', 'w2', 'b2')}
    del _L1_ffn_all
    return {'x': x, 'src': src, 'dst': dst, 'L0_gnn_W1s': _L0_gnn_in['W1s'], 'L0_gnn_b1s': _L0_gnn_in['b1s'], 'L0_gnn_W1d': _L0_gnn_in['W1d'], 'L0_gnn_b1d': _L0_gnn_in['b1d'], 'L0_gnn_attn1': _L0_gnn_in['attn1'], 'L0_gnn_ln1_w': _L0_gnn_in['ln1_w'], 'L0_gnn_ln1_b': _L0_gnn_in['ln1_b'], 'L0_gnn_Wos': _L0_gnn_in['Wos'], 'L0_gnn_bos': _L0_gnn_in['bos'], 'L0_gnn_Wod': _L0_gnn_in['Wod'], 'L0_gnn_bod': _L0_gnn_in['bod'], 'L0_gnn_attno': _L0_gnn_in['attno'], 'L0_gnn_lno_w': _L0_gnn_in['lno_w'], 'L0_gnn_lno_b': _L0_gnn_in['lno_b'], 'L0_ffn_phi': _L0_ffn_in['phi'], 'L0_ffn_scale': _L0_ffn_in['scale'], 'L0_ffn_w1': _L0_ffn_in['w1'], 'L0_ffn_b1': _L0_ffn_in['b1'], 'L0_ffn_w2': _L0_ffn_in['w2'], 'L0_ffn_b2': _L0_ffn_in['b2'], 'L1_gnn_W1': _L1_gnn_in['W1'], 'L1_gnn_b1': _L1_gnn_in['b1'], 'L1_gnn_W2': _L1_gnn_in['W2'], 'L1_gnn_b2': _L1_gnn_in['b2'], 'L1_ffn_router_w': _L1_ffn_in['router_w'], 'L1_ffn_router_b': _L1_ffn_in['router_b'], 'L1_ffn_w1': _L1_ffn_in['w1'], 'L1_ffn_b1': _L1_ffn_in['b1'], 'L1_ffn_w2': _L1_ffn_in['w2'], 'L1_ffn_b2': _L1_ffn_in['b2']}

def reference(x, src, dst, L0_gnn_W1s, L0_gnn_b1s, L0_gnn_W1d, L0_gnn_b1d, L0_gnn_attn1, L0_gnn_ln1_w, L0_gnn_ln1_b, L0_gnn_Wos, L0_gnn_bos, L0_gnn_Wod, L0_gnn_bod, L0_gnn_attno, L0_gnn_lno_w, L0_gnn_lno_b, L0_ffn_phi, L0_ffn_scale, L0_ffn_w1, L0_ffn_b1, L0_ffn_w2, L0_ffn_b2, L1_gnn_W1, L1_gnn_b1, L1_gnn_W2, L1_gnn_b2, L1_ffn_router_w, L1_ffn_router_b, L1_ffn_w1, L1_ffn_b1, L1_ffn_w2, L1_ffn_b2):
    import jax
    import jax.numpy as jnp

    def _L0_gnn_ref(x, src, dst, W1s, b1s, W1d, b1d, attn1, ln1_w, ln1_b, Wos, bos, Wod, bod, attno, lno_w, lno_b):
        import jax, jax.numpy as jnp
        import numpy as np
        N, E, DIM, HEADS = (1250, 20000, 768, 8)
        HD = DIM // HEADS
        EPS = 1e-05

        def layer_norm(x, w, b):
            mu = jnp.mean(x, axis=-1, keepdims=True)
            var = jnp.var(x, axis=-1, keepdims=True)
            return (x - mu) * jax.lax.rsqrt(var + EPS) * w + b

        def gatv2(x, src, dst, Ws, bs, Wd, bd, attn):
            H, D = attn.shape
            fs = (x @ Ws + bs).reshape(-1, H, D)
            fd = (x @ Wd + bd).reshape(-1, H, D)
            e = jax.nn.leaky_relu(fs[src] + fd[dst], 0.2)
            logits = jnp.einsum('ehd,hd->eh', e, attn)
            m = jax.ops.segment_max(logits, dst, num_segments=N)
            ex = jnp.exp(logits - m[dst])
            denom = jax.ops.segment_sum(ex, dst, num_segments=N)
            alpha = ex / denom[dst]
            out = jax.ops.segment_sum(alpha[:, :, None] * fs[src], dst, num_segments=N)
            return jax.nn.elu(out)
        h = gatv2(x, src, dst, W1s, b1s, W1d, b1d, attn1).reshape(N, DIM)
        h = layer_norm(h + x, ln1_w, ln1_b)
        out = gatv2(h, src, dst, Wos, bos, Wod, bod, attno).reshape(N, DIM)
        return layer_norm(out, lno_w, lno_b)

    def _L0_ffn_ref(x, phi, scale, w1, b1, w2, b2):
        import jax, jax.numpy as jnp
        import numpy as np
        B, L, D = (4, 1024, 768)
        E, S, H = (32, 32, 192)
        EPS = 1e-12

        def _l2norm(v, axis):
            n = jnp.sqrt(jnp.sum(v * v, axis=axis, keepdims=True))
            return v / jnp.maximum(n, EPS)
        b, l, d = x.shape
        xn = _l2norm(x, axis=2)
        phin = scale * _l2norm(phi, axis=0)
        logits = jnp.einsum('bld,des->bles', xn, phin)
        d_w = jax.nn.softmax(logits, axis=-1)
        c_w = jax.nn.softmax(logits.reshape(b, l, E * S), axis=-1)
        slots = jnp.einsum('bld,bles->besd', xn, d_w)
        h = jax.nn.gelu(jnp.einsum('besd,edh->besh', slots, w1) + b1[:, None, :], approximate=False)
        eo = jnp.einsum('besh,ehd->besd', h, w2) + b2[:, None, :]
        eo = eo.reshape(b, E * S, d)
        return jnp.einsum('bkd,blk->bld', eo, c_w)

    def _L1_gnn_ref(x, W1, b1, W2, b2, edge_index):
        import jax, jax.numpy as jnp
        import numpy as np
        N_NODES = 625
        D = 768
        N_EDGES = 10000

        def gcn_conv(x, W, b, src, dst, n_nodes):
            h = x @ W
            deg = jax.ops.segment_sum(jnp.ones_like(dst, dtype=h.dtype), dst, num_segments=n_nodes)
            dinv = jnp.where(deg > 0, jax.lax.rsqrt(deg), 0.0)
            norm = dinv[src] * dinv[dst]
            msgs = h[src] * norm[:, None]
            out = jax.ops.segment_sum(msgs, dst, num_segments=n_nodes)
            return out + b

        def add_self_loops(edge_index, n_nodes):
            loop = jnp.arange(n_nodes, dtype=edge_index.dtype)
            src = jnp.concatenate([edge_index[0], loop])
            dst = jnp.concatenate([edge_index[1], loop])
            return (src, dst)
        n = x.shape[0]
        src, dst = add_self_loops(edge_index, n)
        h = gcn_conv(x, W1, b1, src, dst, n)
        h = jax.nn.relu(h)
        out = gcn_conv(h, W2, b2, src, dst, n)
        return out

    def _L1_ffn_ref(x, router_w, router_b, w1, b1, w2, b2):
        import jax, jax.numpy as jnp
        import numpy as np
        EMB = 768
        HID = 1152
        NUM_EXPERTS = 8
        TOP_K = 2
        B, N, E = x.shape
        T = B * N
        logits = jnp.einsum('bne,ef->bnf', x, router_w) + router_b
        probs = jax.nn.softmax(logits, axis=-1)
        topk_probs, topk_idx = jax.lax.top_k(probs, TOP_K)
        flat_x = x.reshape(T, E)
        flat_idx = topk_idx.reshape(T, TOP_K)
        flat_w = topk_probs.reshape(T, TOP_K)
        gates = jnp.zeros((T, NUM_EXPERTS), dtype=x.dtype)
        gates = gates.at[jnp.arange(T)[:, None], flat_idx].add(flat_w)
        out = jnp.zeros((T, E), dtype=x.dtype)
        for e in range(NUM_EXPERTS):
            h = jax.nn.gelu(flat_x @ w1[e] + b1[e], approximate=False)
            y = h @ w2[e] + b2[e]
            out = out + y * gates[:, e:e + 1]
        return out.reshape(B, N, E)
    edge_index = jnp.stack([src, dst])
    x = x + _L0_gnn_ref(_layernorm(x, axis=-1), src, dst, L0_gnn_W1s, L0_gnn_b1s, L0_gnn_W1d, L0_gnn_b1d, L0_gnn_attn1, L0_gnn_ln1_w, L0_gnn_ln1_b, L0_gnn_Wos, L0_gnn_bos, L0_gnn_Wod, L0_gnn_bod, L0_gnn_attno, L0_gnn_lno_w, L0_gnn_lno_b)
    x = x + _L0_ffn_ref(_layernorm(x, axis=-1)[None], L0_ffn_phi, L0_ffn_scale, L0_ffn_w1, L0_ffn_b1, L0_ffn_w2, L0_ffn_b2)[0]
    x = x + _L1_gnn_ref(_layernorm(x, axis=-1), L1_gnn_W1, L1_gnn_b1, L1_gnn_W2, L1_gnn_b2, edge_index)
    x = x + _L1_ffn_ref(_layernorm(x, axis=-1)[None], L1_ffn_router_w, L1_ffn_router_b, L1_ffn_w1, L1_ffn_b1, L1_ffn_w2, L1_ffn_b2)[0]
    return x

_drawn_inputs = setup_inputs


def setup_inputs(seed=0):
    import zlib

    import numpy as np

    out = dict(_drawn_inputs(seed))
    spreads = {'L0_gnn_b1s': (0.0, 0.1),
     'L0_gnn_b1d': (0.0, 2.0),
     'L0_gnn_ln1_w': (1.0, 0.2),
     'L0_gnn_ln1_b': (0.0, 0.1),
     'L0_gnn_bos': (0.0, 0.1),
     'L0_gnn_bod': (0.0, 0.479),
     'L0_gnn_lno_w': (1.0, 0.2),
     'L0_gnn_lno_b': (0.0, 0.1),
     'L1_gnn_b1': (0.0, 0.1),
     'L1_gnn_b2': (0.0, 0.1),
     'L1_ffn_router_b': (0.0, 0.425),
     'L1_ffn_b1': (0.0, 0.8),
     'L1_ffn_b2': (0.0, 0.375)}
    factors = {'L0_gnn_W1d': 12.902, 'L0_ffn_phi': 64.0, 'L0_ffn_b1': 55.573, 'L0_ffn_b2': 37.298}
    for name, (base, spread) in spreads.items():
        noise = np.random.default_rng([zlib.crc32(name.encode()), seed]).standard_normal(out[name].shape)
        drawn = base * np.exp(spread * noise) if base else spread * noise
        out[name] = jnp.asarray(drawn.astype(out[name].dtype))
    for name, factor in factors.items():
        out[name] = (out[name] * factor).astype(out[name].dtype)
    return out
```

```python
from contextlib import ExitStack

import concourse.bass as bass
from concourse import mybir

ALU = mybir.AluOpType
ACT = mybir.ActivationFunctionType
AX = mybir.AxisListType
F32 = mybir.dt.float32
I32 = mybir.dt.int32
U32 = mybir.dt.uint32

P = 128
NODES, D = 1250, 768
NB = -(-NODES // P)
ROWS = NB * P
LAST = NODES - (NB - 1) * P
KD = D // P
EDGES = 40000
UN = 4
GROUPS = -(-EDGES // (P * UN))
TILES = GROUPS * UN
VISITS = GROUPS + NB - 1
QT = TILES // 4
HALF = D // 2
NEG = -1.0e30
NO_NODE = 4096
HEADS = 8
BANK = 512
ds = bass.ds


def bcast(ap, axis, n):
    new = ap.unsqueeze(axis)
    shape = list(new.shape)
    shape[axis] = n
    return new.broadcast_to(shape)


class Chain:

    def __init__(self, eng, sem):
        self.eng, self.sem, self.base, self.i, self.per, self.n = eng, sem, 0, None, 0, 0

    def loop(self, i, per):
        self.base += self.n
        self.i, self.per, self.n = i, per, 0

    def end(self, times):
        assert self.n == self.per, (self.n, self.per)
        self.base += self.per * times
        self.i, self.n = None, 0

    def __call__(self, ins):
        ins.then_inc(self.sem, 1)
        self.n += 1
        at = self.base + self.n
        self.eng.wait_ge(self.sem, at if self.i is None else self.i * self.per + at)
        return ins


class Scope(ExitStack):

    def __init__(self, nc, name):
        super().__init__()
        self.nc, self.name, self.sems = nc, name, []
        self.callback(self.clear)

    def clear(self):
        if self.sems:
            self.nc.clear_and_free_semaphores(self.sems)
            self.nc.all_engine_barrier(sem_only=True)

    def sb(self, name, shape, dt=F32):
        return self.enter_context(self.nc.sbuf_tensor(f"{self.name}_{name}", shape, dt))

    def ps(self, name, shape):
        return self.enter_context(self.nc.psum_tensor(f"{self.name}_{name}", shape, F32))

    def sem(self, name):
        self.sems.append(self.nc.alloc_semaphore(f"{self.name}_{name}"))
        return self.sems[-1]


def blk(t, b):
    return t[:, ds(b, 1), :].squeeze(1)


def row_stats(chain, nc, src, st, mv):
    nc.vector.bn_stats(st[:, 0, :], src[:, 0:HALF])
    chain(nc.vector.bn_stats(st[:, 1, :], src[:, HALF:D]))
    chain.eng.nop(nofuse=True)
    chain(nc.vector.bn_aggr(mv, st[:]))


def layer_norms(nc, dve, chain, H, X, W, weight=None, bias=None):
    with dve.Fori(0, NB) as b:
        chain.loop(b, 3)
        row_stats(chain, nc, blk(X, b)[:, 0:D], W.st, W.mvb[:])
        chain(nc.vector.tensor_copy(blk(W.mv, b), W.mvb[:]))
    chain.end(NB)
    chain(nc.vector.tensor_scalar(W.val[:], W.mv[:, :, 1:2].squeeze(2), 1e-5, None, ALU.add))
    inverse_roots(nc, dve, chain, W, W.val, W.root, W.rstd)
    with dve.Fori(0, NB) as b:
        chain.loop(b, 3 if weight is not None else 1)
        h = blk(H, b)
        chain(nc.vector.tensor_scalar(h, blk(X, b)[:, 0:D], W.mv[:, ds(b, 1), 0:1].squeeze(1), W.rstd[:, ds(b, 1)], ALU.subtract, ALU.mult))
        if weight is not None:
            chain(nc.vector.tensor_tensor(h, h, weight, ALU.mult))
            chain(nc.vector.tensor_tensor(h, h, bias, ALU.add))
    chain.end(NB)


class Roots:

    def __init__(self, c):
        self.st, self.mvb, self.mv = c.sb("st", [P, 2, 6]), c.sb("mvb", [P, 2]), c.sb("mv", [P, NB, 2])
        self.val, self.root, self.rstd, self.sq = (c.sb(x, [P, NB]) for x in ("val", "root", "rstd", "sq"))
        self.s_val, self.s_root, self.n, self.m = c.sem("val"), c.sem("root"), 0, 0


def inverse_roots(nc, dve, chain, W, val, root, out):
    W.n += 1
    dve.sem_inc(W.s_val, 1)
    dve.wait_ge(W.s_root, W.n)
    chain(nc.vector.reciprocal(out[:], root[:]))
    chain(nc.vector.tensor_tensor(W.sq[:], out[:], out[:], ALU.mult))
    chain(nc.vector.tensor_tensor(W.sq[:], W.sq[:], val[:], ALU.mult))
    chain(nc.vector.tensor_scalar(W.sq[:], W.sq[:], -0.5, 1.5, ALU.mult, ALU.add))
    chain(nc.vector.tensor_tensor(out[:], out[:], W.sq[:], ALU.mult))


def square_roots(nc, act, W, val, root):
    W.m += 1
    act.wait_ge(W.s_val, W.m)
    nc.scalar.activation(root[:], val[:], ACT.Sqrt).then_inc(W.s_root, 1)


def setup(nc, R, x, src, dst):
    with Scope(nc, "set") as c:
        rows = c.sb("rows", [QT, 2, 4, P], I32)
        rowsf = c.sb("rowsf", [QT, 2, 4, P])
        first = c.sb("first", [1, GROUPS], I32)
        firstf = c.sb("firstf", [1, GROUPS])
        steps = c.sb("steps", [1, VISITS])
        before = c.sb("before", [1, VISITS, GROUPS - 1])
        svf = c.sb("svf", [1, VISITS])
        cvf = c.sb("cvf", [1, VISITS])
        ones = c.sb("ones", [P, P])
        turned = c.ps("turned", [P, 2, 4, P])
        s_zero, s_x, s_e, s_f = c.sem("zero"), c.sem("x"), c.sem("edges"), c.sem("first")
        s_gi, s_id, s_iota, s_cast, s_t, s_v = (c.sem(n) for n in ("gi", "ident", "iota", "cast", "turned", "v"))
        full = EDGES - 3 * QT * P
        block = c.enter_context(nc.Block())

        @block.sync
        def _(sp):
            sp.wait_ge(s_zero, 3)
            sp.dma_start(R.X[:, 0:NB - 1, :], x[0:(NB - 1) * P, :].rearrange("(b p) d -> p b d", p=P)).then_inc(s_x, 16)
            sp.dma_start(R.X[0:LAST, NB - 1, :], x[(NB - 1) * P:NODES, :]).then_inc(s_x, 16)
            for j, e in enumerate((src, dst)):
                whole = full // P
                sp.dma_start(rows[:, j, 0:3, :], e[0:3 * QT * P].rearrange("(q t p) -> t q p", q=3, p=P)).then_inc(s_e, 16)
                sp.dma_start(rows[0:whole, j, 3, :], e[3 * QT * P:3 * QT * P + whole * P].rearrange("(t p) -> t p", p=P)).then_inc(s_e, 16)
                sp.dma_start(rows[whole:whole + 1, j, 3, 0:full - whole * P], e[3 * QT * P + whole * P:EDGES].rearrange("(t p) -> t p", t=1)).then_inc(s_e, 16)
            with nc.allow_non_contiguous_dma("one destination of each group"):
                sp.dma_start(first[:, 0:GROUPS - 1], dst[0:(GROUPS - 1) * P * UN].rearrange("(g e) -> g e", e=P * UN)[:, 0:1].rearrange("g o -> o g")).then_inc(s_f, 16)
                sp.dma_start(first[:, GROUPS - 1:GROUPS], dst[(GROUPS - 1) * P * UN:(GROUPS - 1) * P * UN + 1].rearrange("(a b) -> a b", a=1)).then_inc(s_f, 16)
            sp.wait_ge(s_x, 32)

        @block.gpsimd
        def _(pool):
            nc.gpsimd.memset(ones[:], 1.0).then_inc(s_gi, 1)
            nc.gpsimd.iota(R.nodes[:], [[1, ROWS]], 0, 0, allow_small_or_imprecise_dtypes=True).then_inc(s_iota, 1)
            nc.gpsimd.iota(steps[:], [[1, VISITS]], 0, 0, allow_small_or_imprecise_dtypes=True).then_inc(s_iota, 1)
            pool.wait_ge(s_gi, 1)
            nc.gpsimd.affine_select(out=R.ident[:], in_=ones[:], compare_op=ALU.is_equal, fill=0.0, base=0,
                                    pattern=[[-1, P]], channel_multiplier=1).then_inc(s_id, 1)

        @block.vector
        def _(dve):
            chain = Chain(dve, s_v)
            nc.vector.memset(R.X[:, NB - 1, :], 0.0).then_inc(s_zero, 1)
            nc.vector.memset(rows[:, 0], 0).then_inc(s_zero, 1)
            nc.vector.memset(rows[:, 1], NO_NODE).then_inc(s_zero, 1)
            dve.wait_ge(s_f, 32)
            dve.wait_ge(s_iota, 2)
            chain(nc.vector.tensor_single_scalar(first[:], first[:], 7, ALU.arith_shift_right))
            chain(nc.vector.tensor_copy(firstf[:], first[:]))
            chain(nc.vector.tensor_tensor(firstf[:], firstf[:], steps[:, 0:GROUPS], ALU.add))
            chain(nc.vector.tensor_tensor(before[:], bcast(firstf[:, 1:GROUPS], 1, VISITS), bcast(steps[:], 2, GROUPS - 1), ALU.is_le))
            chain(nc.vector.reduce_sum(svf[:], before[:], AX.X))
            chain(nc.vector.tensor_tensor(cvf[:], steps[:], svf[:], ALU.subtract))
            nc.vector.tensor_copy(R.visit_group[:], svf[:])
            nc.vector.tensor_copy(R.visit_block[:], cvf[:])
            dve.wait_ge(s_e, 96)
            nc.vector.tensor_copy(rowsf[:], rows[:]).then_inc(s_cast, 1)
            dve.wait_ge(s_t, 1)
            for q in range(4):
                nc.vector.tensor_copy(R.src[:, q * QT:(q + 1) * QT], turned[:, 0, q, 0:QT])
                nc.vector.tensor_copy(R.dst[:, q * QT:(q + 1) * QT], turned[:, 1, q, 0:QT])
                nc.vector.tensor_single_scalar(R.dsti[:, q * QT:(q + 1) * QT], turned[:, 1, q, 0:QT], float(ROWS - 1), ALU.min)
            nc.vector.tensor_copy(R.ends[:, :, :, 1:P + 1], rowsf[:, 1:2])
            chain(nc.vector.memset(R.ends[:, :, :, 0:1], -1.0))
            chain(nc.vector.memset(R.ends[:, :, :, P + 1:P + 2], -1.0))

        @block.tensor
        def _(pe):
            pe.wait_ge(s_id, 1)
            pe.wait_ge(s_cast, 1)
            for j in range(2):
                for q in range(4):
                    last = nc.tensor.transpose(turned[:, j, q, 0:QT], rowsf[:, j, q, :], R.ident[0:QT, 0:QT])
            last.then_inc(s_t, 1)


def norm_rows(nc, R, name, l2=False):
    with Scope(nc, name) as c:
        W = Roots(c)
        sq = c.sb("squares", [P, D])
        s_v = c.sem("v")
        block = c.enter_context(nc.Block())

        @block.scalar
        def _(act):
            for _ in range(2 if l2 else 1):
                square_roots(nc, act, W, W.val, W.root)

        @block.vector
        def _(dve):
            chain = Chain(dve, s_v)
            layer_norms(nc, dve, chain, R.H, R.X, W)
            if l2:
                with dve.Fori(0, NB) as b:
                    chain.loop(b, 1)
                    h = blk(R.H, b)
                    chain(nc.vector.scalar_tensor_tensor(out=sq[:], in0=h, scalar=1.0, in1=h, op0=ALU.mult, op1=ALU.mult, accum_out=W.val[:, ds(b, 1)]))
                chain.end(NB)
                chain(nc.vector.tensor_scalar(W.val[:], W.val[:], 1e-24, None, ALU.max))
                inverse_roots(nc, dve, chain, W, W.val, W.root, W.rstd)
                with dve.Fori(0, NB) as b:
                    nc.vector.tensor_scalar(blk(R.H, b), blk(R.H, b), W.rstd[:, ds(b, 1)], None, ALU.mult)


def project(nc, R, name, weights, tables, biases=None, attn=None, heads=1):
    n, gat = len(weights), attn is not None
    hd = D // heads
    he = hd + 2 if gat else hd
    width = heads * he
    half = width // 2
    loads = n * (KD + 1) + 1 if gat else n * KD
    with Scope(nc, name) as c:
        w = [c.sb(f"w{j}", [P, KD, heads, he]) for j in range(n)]
        bias = [c.sb(f"bias{j}", [1, heads, he]) for j in range(n)] if gat else []
        at = c.sb("attn", [P, D]) if gat else None
        prod = c.sb("prod", [P, D]) if gat else None
        ones = c.sb("ones", [1, P])
        rows = [c.sb(f"rows{s}", [P, D]) for s in range(2)]
        rowsT = [c.sb(f"rowsT{s}", [P, KD, P]) for s in range(2)]
        out = [[c.sb(f"out{j}{s}", [P, width]) for s in range(2)] for j in range(n)] if gat else []
        psT = [c.ps(f"psT{s}", [P, 2, BANK]) for s in range(2)]
        psO = [c.ps(f"psO{j}", [P, 2, BANK]) for j in range(n)]
        s_w, s_v, s_wide, s_rows = c.sem("weights"), c.sem("v"), c.sem("wide"), c.sem("rows")
        s_turn, s_turned, s_mm, s_taken = c.sem("turn"), c.sem("turned"), c.sem("mm"), c.sem("taken")
        s_store = [c.sem(f"store{s}") for s in range(2)]
        block = c.enter_context(nc.Block())

        @block.sync
        def _(sp):
            for j in range(n):
                for k in range(KD):
                    sp.dma_start(w[j][:, k, :, 0:hd], weights[j][k * P:(k + 1) * P, :].rearrange("p (h e) -> p h e", h=heads)).then_inc(s_w, 16)
                if gat:
                    sp.dma_start(bias[j][:, :, 0:hd], biases[j].rearrange("(o h e) -> o h e", o=1, h=heads)).then_inc(s_w, 16)
            if gat:
                sp.dma_start(at[:], attn.partition_broadcast(P)).then_inc(s_w, 16)
            with sp.Fori(0, NB // 2) as i:
                for s in range(2):
                    for j in range(n):
                        b = i * 2 + s
                        sp.wait_ge(s_taken, b * n + n + j + 1)
                        rowsof = out[j][s][:] if gat else R.own[:, ds(b, 1), :].squeeze(1)
                        sp.dma_start(tables[j][ds(b * P, P), :], rowsof).then_inc(s_store[s], 16)
            for s in range(2):
                sp.wait_ge(s_store[s], 16 * (1 + n * NB // 2))

        @block.vector
        def _(dve):
            chain = Chain(dve, s_v)
            dve.sem_inc(s_turn, 2)
            dve.sem_inc(s_mm, 2)
            nc.vector.memset(ones[:], 1.0).then_inc(s_wide, 1)
            if gat:
                dve.wait_ge(s_w, 16 * loads)
                for j in range(n):
                    for k in range(KD + 1):
                        a = w[j][:, k] if k < KD else bias[j][:]
                        m = P if k < KD else 1
                        pr = prod[0:m, :].rearrange("p (h e) -> p h e", h=heads)
                        nc.vector.memset(a[:, :, hd:hd + 1], 0.0 if k < KD or j else 1.0)
                        chain(nc.vector.tensor_tensor(pr, a[:, :, 0:hd], at[0:m, :].rearrange("p (h e) -> p h e", h=heads), ALU.mult))
                        chain(nc.vector.tensor_reduce(a[:, :, hd + 1:hd + 2], pr, AX.X, ALU.add))
                dve.sem_inc(s_wide, 1)
            with dve.Fori(0, NB // 2) as i:
                for s in range(2):
                    b = i * 2 + s
                    dve.wait_ge(s_turn, b + 1)
                    nc.vector.tensor_copy(rows[s][:], R.H[:, ds(b, 1), :].squeeze(1)).then_inc(s_rows, 1)
                    dve.wait_ge(s_turn, b + 3)
                    dve.wait_ge(s_mm, b + 1)
                    nc.vector.tensor_copy(rowsT[s][:].rearrange("p (a k) q -> p a (k q)", a=2), psT[s][:, :, 0:HALF]).then_inc(s_turned, 1)

        @block.scalar
        def _(act):
            act.sem_inc(s_taken, n)
            for s in range(2):
                act.sem_inc(s_store[s], 16)
            with act.Fori(0, NB // 2) as i:
                for s in range(2):
                    b = i * 2 + s
                    act.wait_ge(s_store[s], i * 16 * n + 16)
                    act.wait_ge(s_mm, b + 3)
                    for j in range(n):
                        src = psO[j][:, :, 0:half]
                        if gat:
                            nc.scalar.copy(out[j][s][:].rearrange("p (a e) -> p a e", a=2), src).then_inc(s_taken, 1)
                        else:
                            nc.scalar.activation(R.own[:, ds(b, 1), :].squeeze(1).rearrange("p (a e) -> p a e", a=2), src, ACT.Copy,
                                                 scale=R.dinv[:, ds(b, 1)]).then_inc(s_taken, 1)

        @block.tensor
        def _(pe):
            pe.wait_ge(s_wide, 2 if gat else 1)
            pe.wait_ge(s_w, 16 * loads)
            with pe.Fori(0, NB // 2) as i:
                for s in range(2):
                    b = i * 2 + s
                    pe.wait_ge(s_rows, b + 1)
                    for k in range(KD):
                        last = nc.tensor.transpose(psT[s][:, k // 3, (k % 3) * P:(k % 3 + 1) * P], rows[s][:, k * P:(k + 1) * P], R.ident[:])
                    last.then_inc(s_turn, 1)
                    pe.wait_ge(s_taken, b * n + n)
                    pe.wait_ge(s_turned, b + 1)
                    for j in range(n):
                        for a in range(2):
                            o = psO[j][:, a, 0:half]
                            cut = slice(a * half, (a + 1) * half)
                            for k in range(KD):
                                last = nc.tensor.matmul(o, rowsT[s][:, k, :], w[j][:, k].rearrange("p h e -> p (h e)")[:, cut],
                                                        start=(k == 0), stop=(not gat and k == KD - 1))
                            if gat:
                                last = nc.tensor.matmul(o, ones[:], bias[j][:].rearrange("p h e -> p (h e)")[:, cut], start=False, stop=True)
                    last.then_inc(s_mm, 1)


def logits(nc, R, name, fs, fd, attn, heads):
    hd = D // heads
    he = hd + 2
    width = heads * he
    with Scope(nc, name) as c:
        at = c.sb("attn", [P, D])
        lists = [c.sb(f"list{j}", [P, UN], I32) for j in range(2)]
        g = [c.sb(f"g{j}", [P, UN, width]) for j in range(2)]
        z = c.sb("z", [P, UN, width])
        zr = c.sb("zr", [P, 2, D])
        part = c.sb("part", [P, 2, heads, UN])
        s_at, s_v = c.sem("attn"), c.sem("v")
        s_list, s_unlist = c.sem("list"), c.sem("unlist")
        s_g = [c.sem(f"g{k}") for k in range(UN)]
        s_free = [c.sem(f"free{k}") for k in range(UN)]
        s_sum, s_part, s_done = c.sem("sum"), c.sem("part"), c.sem("done")
        block = c.enter_context(nc.Block())

        @block.sync
        def _(sp):
            sp.dma_start(at[:], attn.partition_broadcast(P)).then_inc(s_at, 16)

        @block.gpsimd
        def _(pool):
            with pool.Fori(0, GROUPS) as i:
                for k in range(UN):
                    pool.wait_ge(s_free[k], i + 1)
                    for j, e in enumerate((R.src, R.dsti)):
                        nc.gpsimd.tensor_copy(lists[j][:, k:k + 1], e[:, ds(i * UN + k, 1)]).then_inc(s_list, 1)
                    pool.wait_ge(s_list, (i * UN + k) * 2 + 2)
                    pool.nop(nofuse=True)
                    for j, table in enumerate((fs, fd)):
                        nc.gpsimd.indirect_dma_start(
                            out=g[j][:, k, :], out_offset=None, in_=table,
                            in_offset=bass.IndirectOffsetOnAxis(ap=lists[j][:, k:k + 1], axis=0)).then_inc(s_g[k], 16)

        @block.vector
        def _(dve):
            chain = Chain(dve, s_v)
            for k in range(UN):
                dve.sem_inc(s_free[k], 1)
            dve.wait_ge(s_at, 16)
            chain(nc.vector.tensor_scalar(at[:], at[:], 0.8, None, ALU.mult))
            with dve.Fori(0, GROUPS) as i:
                chain.loop(i, 1)
                for k in range(UN):
                    dve.wait_ge(s_g[k], i * 32 + 32)
                    nc.vector.tensor_tensor(z[:, k, :], g[0][:, k, :], g[1][:, k, :], ALU.add).then_inc(s_free[k], 1)
                    dve.wait_ge(s_free[k], i + 2)
                    for h in range(heads):
                        last = nc.vector.scalar_tensor_tensor(
                            out=zr[:, k % 2, h * hd:(h + 1) * hd], in0=z[:, k, h * he:h * he + hd], scalar=0.0,
                            in1=at[:, h * hd:(h + 1) * hd], op0=ALU.max, op1=ALU.mult,
                            accum_out=part[:, 0, h, k:k + 1])
                    last.then_inc(s_part, 1)
                    dve.wait_ge(s_part, i * UN + k + 1)
                zlin = z[:].rearrange("p k (h e) -> p h k e", h=heads)[:, :, :, hd + 1:hd + 2].squeeze(3)
                chain(nc.vector.tensor_scalar(part[:, 1], zlin, 0.2, None, ALU.mult))
                nc.vector.tensor_tensor(R.L[:, 0:heads, ds(i * UN, UN)], part[:, 0], part[:, 1], ALU.add).then_inc(s_done, 1)
                dve.wait_ge(s_done, i + 1)


def edge_softmax(nc, R, name, heads):
    W = P + 2
    with Scope(nc, name) as c:
        S = c.sb("S", [QT, 4, heads, W])
        pen = c.sb("pen", [QT, 2, 4, heads, W])
        run = c.sb("run", [QT, 2, heads, W])
        sides = c.sb("sides", [QT, 4, 4, heads])
        rowsd = c.sb("rowsd", [heads, 4, TILES])
        a = c.sb("a", [heads, 6, TILES])
        seen = c.sb("seen", [heads, 2, TILES])
        carry = c.sb("carry", [heads, 2, TILES])
        psS = c.ps("psS", [P, 2, 4, P])
        psR = c.ps("psR", [heads, 4, BANK])
        psC = c.ps("psC", [P, BANK])
        s_v, s_turn, s_copied, s_side, s_rows, s_carry, s_back = (c.sem(x) for x in ("v", "turn", "copied", "side", "rows", "carry", "back"))
        s_exp, s_exped, s_ret, s_retd = c.sem("exp"), c.sem("exped"), c.sem("ret"), c.sem("retd")
        block = c.enter_context(nc.Block())

        @block.tensor
        def _(pe):
            for q in range(4):
                for h in range(heads):
                    n = q * heads + h
                    if n >= 8 and n % 4 == 0:
                        pe.wait_ge(s_copied, n // 4 - 1)
                    t = nc.tensor.transpose(psS[0:QT, n // 4 % 2, n % 4, :], R.L[:, h, q * QT:(q + 1) * QT], R.ident[:])
                    if n % 4 == 3:
                        t.then_inc(s_turn, 1)
            pe.wait_ge(s_side, 1)
            for j in range(4):
                for q in range(4):
                    last = nc.tensor.transpose(psR[:, j, q * QT:(q + 1) * QT], sides[:, q, j, :], R.ident[0:QT, 0:QT])
            last.then_inc(s_rows, 1)
            pe.wait_ge(s_carry, 1)
            for j in range(2):
                for q in range(4):
                    last = nc.tensor.transpose(psC[0:QT, (j * 4 + q) * heads:(j * 4 + q + 1) * heads], carry[:, j, q * QT:(q + 1) * QT], R.ident[0:heads, 0:heads])
            last.then_inc(s_back, 1)
            for h in range(heads):
                if h == 0:
                    pe.wait_ge(s_exped, 4)
                if h >= 2:
                    pe.wait_ge(s_retd, h - 1)
                for q in range(4):
                    last = nc.tensor.transpose(psS[:, h % 2, :, :].rearrange("p a b -> p (a b)")[:, q * QT:(q + 1) * QT], S[:, q, h, 1:P + 1], R.ident[0:QT, 0:QT])
                last.then_inc(s_ret, 1)

        @block.scalar
        def _(act):
            for n in range(heads):
                act.wait_ge(s_turn, n + 1)
                for k in range(4):
                    m = n * 4 + k
                    last = nc.scalar.copy(S[:, m // heads, m % heads, 1:P + 1], psS[0:QT, n % 2, k, :])
                last.then_inc(s_copied, 1)
            for q in range(4):
                act.wait_ge(s_exp, q + 1)
                nc.scalar.activation(S[:, q, :, 1:P + 1], S[:, q, :, 1:P + 1], ACT.Exp).then_inc(s_exped, 1)
            for h in range(heads):
                act.wait_ge(s_ret, h + 1)
                nc.scalar.copy(R.L[:, h, :], psS[:, h % 2, :, :].rearrange("p a b -> p (a b)")[:, 0:TILES]).then_inc(s_retd, 1)

        @block.vector
        def _(dve):
            chain = Chain(dve, s_v)
            flat = "p h w -> p (h w)"

            def scans():
                for q in range(4):
                    yield q
                    chain(nc.vector.tensor_tensor_scan(run[:, 0].rearrange(flat), pen[:, 0, q].rearrange(flat), S[:, q].rearrange(flat), NEG, ALU.add, ALU.max))
                    chain(nc.vector.tensor_tensor_scan(run[:, 1].rearrange(flat)[:, ::-1], pen[:, 1, q].rearrange(flat)[:, ::-1], S[:, q].rearrange(flat)[:, ::-1], NEG, ALU.add, ALU.max))
                    yield q

            chain(nc.vector.memset(pen[:], 0.0))
            for q in range(4):
                same = run[:, 0, 0, 0:P - 1]
                e = R.ends[:, 0, q]
                chain(nc.vector.tensor_tensor(same, e[:, 2:P + 1], e[:, 1:P], ALU.not_equal))
                chain(nc.vector.tensor_scalar(same, same, NEG, None, ALU.mult))
                nc.vector.tensor_copy(pen[:, 0, q, :, 2:P + 1], bcast(same, 1, heads))
                chain(nc.vector.tensor_copy(pen[:, 1, q, :, 1:P], bcast(same, 1, heads)))
            nc.vector.memset(pen[:, 0, :, :, 0:1], NEG)
            chain(nc.vector.memset(pen[:, 1, :, :, P + 1:W], NEG))
            nc.vector.memset(S[:, :, :, 0:1], NEG)
            chain(nc.vector.memset(S[:, :, :, P + 1:W], NEG))
            for q in range(4):
                nc.vector.tensor_copy(sides[:, q, 2, :], R.ends[:, 0, q, 1:2].broadcast_to([QT, heads]))
                chain(nc.vector.tensor_copy(sides[:, q, 3, :], R.ends[:, 0, q, P:P + 1].broadcast_to([QT, heads])))
            dve.wait_ge(s_copied, heads)
            it = scans()
            for q in it:
                next(it)
                nc.vector.tensor_copy(sides[:, q, 0, :], run[:, 0, :, P:P + 1].squeeze(2))
                chain(nc.vector.tensor_copy(sides[:, q, 1, :], run[:, 1, :, 1:2].squeeze(2)))
            dve.sem_inc(s_side, 1)
            dve.wait_ge(s_rows, 1)
            chain(nc.vector.tensor_copy(rowsd[:], psR[:, :, 0:TILES]))
            last, first, dfirst, dlast = (rowsd[:, j, :] for j in range(4))
            whole, cont, nocont = a[:, 0, :], a[:, 1, :], a[:, 2, :]
            T1 = TILES - 1
            nc.vector.tensor_tensor(whole, dfirst, dlast, ALU.is_equal)
            nc.vector.tensor_tensor(cont[:, 0:T1], dfirst[:, 1:TILES], dlast[:, 0:T1], ALU.is_equal)
            chain(nc.vector.memset(cont[:, T1:TILES], 0.0))
            chain(nc.vector.tensor_scalar(nocont[:, 0:T1], cont[:, 0:T1], -NEG, NEG, ALU.mult, ALU.add))
            nc.vector.tensor_tensor(a[:, 3, 1:TILES], whole[:, 1:TILES], cont[:, 0:T1], ALU.mult)
            nc.vector.tensor_tensor(a[:, 4, 0:TILES], whole, cont, ALU.mult)
            chain(nc.vector.memset(a[:, 3, 0:1], 0.0))
            chain(nc.vector.tensor_scalar(a[:, 3:5, :], a[:, 3:5, :], -NEG, NEG, ALU.mult, ALU.add))
            nc.vector.tensor_tensor_scan(seen[:, 0, :], a[:, 3, :], last, NEG, ALU.add, ALU.max)
            chain(nc.vector.tensor_tensor_scan(seen[:, 1, ::-1], a[:, 4, ::-1], first[:, ::-1], NEG, ALU.add, ALU.max))
            nc.vector.memset(carry[:, 0, 0:1], NEG)
            chain(nc.vector.memset(carry[:, 1, T1:TILES], NEG))
            nc.vector.tensor_tensor(carry[:, 0, 1:TILES], seen[:, 0, 0:T1], a[:, 2, 0:T1], ALU.add)
            chain(nc.vector.tensor_tensor(carry[:, 1, 0:T1], seen[:, 1, 1:TILES], a[:, 2, 0:T1], ALU.add))
            dve.sem_inc(s_carry, 1)
            dve.wait_ge(s_back, 1)
            back = psC[0:QT, 0:8 * heads].rearrange("p (j q h) -> p j q h", j=2, q=4)
            nc.vector.tensor_copy(S[:, :, :, 0:1], back[:, 0].unsqueeze(3))
            chain(nc.vector.tensor_copy(S[:, :, :, P + 1:W], back[:, 1].unsqueeze(3)))
            it = scans()
            for q in it:
                next(it)
                chain(nc.vector.tensor_tensor(run[:, 0], run[:, 0], run[:, 1], ALU.max))
                chain(nc.vector.tensor_tensor(S[:, q, :, 1:P + 1], S[:, q, :, 1:P + 1], run[:, 0, :, 1:P + 1], ALU.subtract))
                dve.sem_inc(s_exp, 1)


def aggregate(nc, R, name, table, width, heads=0, count=False):
    cols = width + bool(count)
    cuts = [(0, 392), (392, cols)] if cols > 768 else [(0, HALF), (HALF, cols)]
    he = width // heads if heads else width
    with Scope(nc, name) as c:
        lists = c.sb("list", [P, 2, UN], I32)
        g = c.sb("g", [P, 2, UN, cols])
        sel = c.sb("sel", [P, 2, UN, P])
        psO = [c.ps(f"psO{s}", [P, 2, BANK]) for s in range(2)]
        s_v, s_list, s_zero = c.sem("v"), c.sem("list"), c.sem("zero")
        s_g = [[c.sem(f"g{s}{k}") for k in range(UN)] for s in range(2)]
        s_w = [[c.sem(f"w{s}{k}") for k in range(UN)] for s in range(2)]
        s_mm = [[c.sem(f"mm{s}{k}") for k in range(UN)] for s in range(2)]
        s_sel, s_add = c.sem("sel"), c.sem("add")
        block = c.enter_context(nc.Block())

        @block.gpsimd
        def _(pool):
            pool.wait_ge(s_zero, 1)
            with pool.Fori(0, VISITS // 2) as i:
                for s in range(2):
                    v = i * 2 + s
                    grp = pool.value_load(R.visit_group[0:1, ds(v, 1)], min_val=0, max_val=GROUPS - 1)
                    pool.wait_ge(s_mm[s][UN - 1], i + 1)
                    nc.gpsimd.tensor_copy(lists[:, s, :], R.src[:, ds(grp * UN, UN)]).then_inc(s_list, 1)
                    for k in range(UN):
                        pool.wait_ge(s_mm[s][k], i + 1)
                        pool.wait_ge(s_list, v + 1)
                        pool.nop(nofuse=True)
                        nc.gpsimd.indirect_dma_start(
                            out=g[:, s, k, 0:width], out_offset=None, in_=table,
                            in_offset=bass.IndirectOffsetOnAxis(ap=lists[:, s, k:k + 1], axis=0)).then_inc(s_g[s][k], 16)

        @block.vector
        def _(dve):
            chain = Chain(dve, s_v)
            chain(nc.vector.memset(R.acc[:], 0.0))
            if count:
                chain(nc.vector.memset(g[:, :, :, width:cols], 1.0))
            for s in range(2):
                for k in range(UN):
                    dve.sem_inc(s_mm[s][k], 1)
            dve.sem_inc(s_zero, 1)
            dve.sem_inc(s_add, 4)

            def make(i, s):
                v = i * 2 + s
                grp = dve.value_load(R.visit_group[0:1, ds(v, 1)], min_val=0, max_val=GROUPS - 1)
                blk = dve.value_load(R.visit_block[0:1, ds(v, 1)], min_val=0, max_val=NB - 1)
                dve.wait_ge(s_mm[s][UN - 1], i + 1)
                nc.vector.tensor_tensor(sel[:, s], bcast(R.nodes[:, ds(blk * P, P)], 1, UN), bcast(R.dst[:, ds(grp * UN, UN)], 2, P), ALU.is_equal).then_inc(s_sel, 1)
                if heads == 1:
                    dve.wait_ge(s_sel, v * 2 + 1)
                    nc.vector.tensor_tensor(sel[:, s], sel[:, s], bcast(R.L[:, 0, ds(grp * UN, UN)], 2, P), ALU.mult).then_inc(s_sel, 1)
                if heads > 1:
                    for k in range(UN):
                        dve.wait_ge(s_g[s][k], i * 16 + 16)
                        rows = g[:, s, k, 0:width].rearrange("p (h e) -> p h e", h=heads)
                        nc.vector.tensor_tensor(rows, rows, R.L[:, :, ds(grp * UN + k, 1)].broadcast_to([P, heads, he]), ALU.mult).then_inc(s_w[s][k], 1)

            def add(i, s):
                v = i * 2 + s
                blk = dve.value_load(R.visit_block[0:1, ds(v, 1)], min_val=0, max_val=NB - 1)
                dve.wait_ge(s_add, v * 2 + 4)
                dve.wait_ge(s_mm[s][UN - 1], i + 2)
                for a, (lo, hi) in enumerate(cuts):
                    acc = R.acc[:, ds(blk, 1), lo:hi].squeeze(1)
                    nc.vector.tensor_tensor(acc, acc, psO[s][:, a, 0:hi - lo], ALU.add).then_inc(s_add, 1)

            make(0, 0)
            with dve.Fori(0, VISITS // 2 - 1) as i:
                make(i, 1)
                add(i, 0)
                make(i + 1, 0)
                add(i, 1)
            last = VISITS // 2 - 1
            make(last, 1)
            add(last, 0)
            add(last, 1)

        @block.tensor
        def _(pe):
            with pe.Fori(0, VISITS // 2) as i:
                for s in range(2):
                    v = i * 2 + s
                    pe.wait_ge(s_add, v * 2 + 2)
                    pe.wait_ge(s_sel, (v + 1) * (2 if heads == 1 else 1))
                    for k in range(UN):
                        if heads > 1:
                            pe.wait_ge(s_w[s][k], i + 1)
                        else:
                            pe.wait_ge(s_g[s][k], i * 16 + 16)
                        for a, (lo, hi) in enumerate(cuts):
                            last = nc.tensor.matmul(psO[s][:, a, 0:hi - lo], sel[:, s, k, :], g[:, s, k, lo:hi], start=(k == 0), stop=(k == UN - 1))
                        last.then_inc(s_mm[s][k], 1)


def finish_gat(nc, R, name, heads, weight, bias, first):
    hd = D // heads
    he = hd + 2
    with Scope(nc, name) as c:
        W = Roots(c)
        wt, bs = c.sb("weight", [P, D]), c.sb("bias", [P, D])
        den = c.sb("den", [P, 2, heads, 1])
        v, e = c.sb("values", [P, 2, D]), c.sb("e", [P, 2, D])
        s_w, s_v, s_low, s_exp = c.sem("weights"), c.sem("v"), c.sem("low"), c.sem("exp")
        block = c.enter_context(nc.Block())

        @block.sync
        def _(sp):
            sp.dma_start(wt[:], weight.partition_broadcast(P)).then_inc(s_w, 16)
            sp.dma_start(bs[:], bias.partition_broadcast(P)).then_inc(s_w, 16)

        @block.scalar
        def _(act):
            with act.Fori(0, NB // 2) as i:
                for s in range(2):
                    act.wait_ge(s_low, i * 2 + s + 1)
                    nc.scalar.activation(e[:, s, :], e[:, s, :], ACT.Exp).then_inc(s_exp, 1)
            if first:
                square_roots(nc, act, W, W.val, W.root)
            square_roots(nc, act, W, W.val, W.root)

        @block.vector
        def _(dve):
            chain = Chain(dve, s_v)

            def low(i, s):
                acc = blk(R.acc, i * 2 + s)[:, 0:heads * he].rearrange("p (h e) -> p h e", h=heads)
                chain(nc.vector.tensor_scalar(den[:, s], acc[:, :, hd:hd + 1], 1e-30, None, ALU.max))
                chain(nc.vector.reciprocal(den[:, s], den[:, s]))
                chain(nc.vector.tensor_tensor(v[:, s, :].rearrange("p (h e) -> p h e", h=heads), acc[:, :, 0:hd], den[:, s].broadcast_to([P, heads, hd]), ALU.mult))
                nc.vector.tensor_scalar(e[:, s, :], v[:, s, :], 0.0, None, ALU.min).then_inc(s_low, 1)

            def high(i, s):
                b = i * 2 + s
                dve.wait_ge(s_exp, b + 1)
                chain(nc.vector.scalar_tensor_tensor(out=v[:, s, :], in0=v[:, s, :], scalar=0.0, in1=e[:, s, :], op0=ALU.max, op1=ALU.add))
                y = blk(R.acc, b)[:, 0:D]
                if first:
                    chain(nc.vector.scalar_tensor_tensor(out=y, in0=v[:, s, :], scalar=-1.0, in1=blk(R.H, b), op0=ALU.add, op1=ALU.add))
                else:
                    chain(nc.vector.tensor_scalar(y, v[:, s, :], -1.0, None, ALU.add))

            if first:
                chain(nc.vector.tensor_scalar(W.val[:], R.acc[:, :, heads * he:heads * he + 1].squeeze(2), 1.0, None, ALU.add))
            low(0, 0)
            with dve.Fori(0, NB // 2 - 1) as i:
                chain.loop(i, 10)
                low(i, 1)
                high(i, 0)
                low(i + 1, 0)
                high(i, 1)
            chain.end(NB // 2 - 1)
            low(NB // 2 - 1, 1)
            high(NB // 2 - 1, 0)
            high(NB // 2 - 1, 1)
            if first:
                inverse_roots(nc, dve, chain, W, W.val, W.root, R.dinv)
            dve.wait_ge(s_w, 32)
            layer_norms(nc, dve, chain, R.H, R.acc, W, wt[:], bs[:])
            if not first:
                with dve.Fori(0, NB) as b:
                    nc.vector.tensor_tensor(blk(R.X, b), blk(R.X, b), blk(R.H, b), ALU.add)


EXPERTS, SLOTS, HID = 32, 32, 192
SE = EXPERTS * SLOTS
KS = SE // P
HC = HID // 2


def soft_logits(nc, R, name, phi, scale, disp, comb, ph):
    with Scope(nc, name) as c:
        sq = c.sb("sq", [P, 2, SE])
        f = c.sb("f", [P, 2, SE])
        ones, sc = c.sb("ones", [P, P]), c.sb("scale", [P, 1])
        rows = [c.sb(f"rows{s}", [P, D]) for s in range(2)]
        rowsT = [c.sb(f"rowsT{s}", [P, KD, P]) for s in range(2)]
        gm, rm, gs, rs = c.sb("gm", [P, 2, EXPERTS, 1]), c.sb("rm", [P, 2]), c.sb("gs", [P, 2, EXPERTS, 1]), c.sb("rs", [P, 2])
        psT = [c.ps(f"psT{s}", [P, 2, BANK]) for s in range(2)]
        psO = [c.ps(f"psO{s}", [P, 2, BANK]) for s in range(2)]
        s_w, s_v, s_sq, s_n, s_clip, s_root, s_phi = (c.sem(x) for x in ("weights", "v", "sq", "n", "clip", "root", "phi"))
        s_rows, s_turn, s_turned, s_mm, s_exp, s_sub = (c.sem(x) for x in ("rows", "turn", "turned", "mm", "exp", "sub"))
        block = c.enter_context(nc.Block())

        @block.sync
        def _(sp):
            sp.dma_start(ph[:], phi.rearrange("(k p) e s -> p k (e s)", p=P)).then_inc(s_w, 16)
            sp.dma_start(sc[:], scale.partition_broadcast(P)).then_inc(s_w, 16)

        @block.vector
        def _(dve):
            chain = Chain(dve, s_v)
            chain(nc.vector.memset(ones[:], 1.0))
            dve.wait_ge(s_w, 32)
            for k in range(KD):
                if k >= 2:
                    dve.wait_ge(s_n, k - 1)
                nc.vector.tensor_tensor(sq[:, k % 2, :], ph[:, k, :], ph[:, k, :], ALU.mult).then_inc(s_sq, 1)
            dve.wait_ge(s_n, KD)
            n2, r = f[:, 0, :], f[:, 1, :]
            chain(nc.vector.tensor_scalar(n2.rearrange("p (a b) -> p a b", a=2), psO[0][:], 1e-24, None, ALU.max))
            dve.sem_inc(s_clip, 1)
            dve.wait_ge(s_root, 1)
            chain(nc.vector.reciprocal(r, sq[:, 0, :]))
            chain(nc.vector.tensor_tensor(sq[:, 1, :], r, r, ALU.mult))
            chain(nc.vector.tensor_tensor(sq[:, 1, :], sq[:, 1, :], n2, ALU.mult))
            chain(nc.vector.tensor_scalar(sq[:, 1, :], sq[:, 1, :], -0.5, 1.5, ALU.mult, ALU.add))
            chain(nc.vector.tensor_tensor(r, r, sq[:, 1, :], ALU.mult))
            chain(nc.vector.tensor_scalar(r, r, sc[:], None, ALU.mult))
            for k in range(KD):
                nc.vector.tensor_tensor(ph[:, k, :], ph[:, k, :], r, ALU.mult).then_inc(s_phi, 1)
            dve.sem_inc(s_turn, 2)
            dve.sem_inc(s_mm, 2)
            ge = "p (e s) -> p e s"

            def turn(i, s):
                b = i * 2 + s
                dve.wait_ge(s_turn, b + 1)
                nc.vector.tensor_copy(rows[s][:], blk(R.H, b)).then_inc(s_rows, 1)
                dve.wait_ge(s_turn, b + 3)
                dve.wait_ge(s_mm, b + 1)
                nc.vector.tensor_copy(rowsT[s][:].rearrange("p (a k) q -> p a (k q)", a=2), psT[s][:, :, 0:HALF]).then_inc(s_turned, 1)

            def weigh(i, s):
                b = i * 2 + s
                dve.wait_ge(s_mm, b + 3)
                lg = psO[s][:].rearrange("p a (e s) -> p (a e) s", s=SLOTS)
                dsp = blk(disp, b).rearrange(ge, e=EXPERTS)
                chain(nc.vector.tensor_reduce(gm[:, s], lg, AX.X, ALU.max))
                chain(nc.vector.tensor_reduce(rm[:, s:s + 1], gm[:, s].squeeze(2), AX.X, ALU.max))
                chain(nc.vector.tensor_scalar(rm[:, s:s + 1], rm[:, s:s + 1], -1.0, None, ALU.mult))
                nc.vector.tensor_tensor(dsp, lg, gm[:, s].broadcast_to([P, EXPERTS, SLOTS]), ALU.subtract).then_inc(s_sub, 1)
                dve.wait_ge(s_exp, b * 2 + 2)
                dve.nop(nofuse=True)
                chain(nc.vector.tensor_reduce(gs[:, s], dsp, AX.X, ALU.add))
                chain(nc.vector.reciprocal(gs[:, s], gs[:, s]))
                nc.vector.tensor_tensor(dsp, dsp, gs[:, s].broadcast_to([P, EXPERTS, SLOTS]), ALU.mult)
                chain(nc.vector.reciprocal(rs[:, s:s + 1], rs[:, s:s + 1]))
                chain(nc.vector.tensor_scalar(blk(comb, b), blk(comb, b), rs[:, s:s + 1], None, ALU.mult))

            turn(0, 0)
            with dve.Fori(0, NB // 2 - 1) as i:
                chain.loop(i, 14)
                turn(i, 1)
                weigh(i, 0)
                turn(i + 1, 0)
                weigh(i, 1)
            chain.end(NB // 2 - 1)
            turn(NB // 2 - 1, 1)
            weigh(NB // 2 - 1, 0)
            weigh(NB // 2 - 1, 1)

        @block.scalar
        def _(act):
            act.wait_ge(s_clip, 1)
            nc.scalar.activation(sq[:, 0, :], f[:, 0, :], ACT.Sqrt).then_inc(s_root, 1)
            with act.Fori(0, NB // 2) as i:
                for s in range(2):
                    b = i * 2 + s
                    act.wait_ge(s_sub, b + 1)
                    nc.scalar.activation(blk(comb, b).rearrange("p (a e) -> p a e", a=2), psO[s][:], ACT.Exp,
                                         bias=rm[:, s:s + 1], accum_out=rs[:, s:s + 1]).then_inc(s_exp, 1)
                    nc.scalar.activation(blk(disp, b), blk(disp, b), ACT.Exp).then_inc(s_exp, 1)

        @block.tensor
        def _(pe):
            for k in range(KD):
                pe.wait_ge(s_sq, k + 1)
                for a in range(2):
                    last = nc.tensor.matmul(psO[0][:, a, :], ones[:], sq[:, k % 2, a * BANK:(a + 1) * BANK], start=(k == 0), stop=(k == KD - 1))
                last.then_inc(s_n, 1)
            pe.wait_ge(s_phi, KD)
            with pe.Fori(0, NB // 2) as i:
                for s in range(2):
                    b = i * 2 + s
                    pe.wait_ge(s_rows, b + 1)
                    for k in range(KD):
                        last = nc.tensor.transpose(psT[s][:, k // 3, (k % 3) * P:(k % 3 + 1) * P], rows[s][:, k * P:(k + 1) * P], R.ident[:])
                    last.then_inc(s_turn, 1)
                    pe.wait_ge(s_turned, b + 1)
                    for a in range(2):
                        for k in range(KD):
                            last = nc.tensor.matmul(psO[s][:, a, :], rowsT[s][:, k, :], ph[:, k, a * BANK:(a + 1) * BANK], start=(k == 0), stop=(k == KD - 1))
                    last.then_inc(s_mm, 1)


def soft_slots(nc, R, name, disp, slotsT):
    with Scope(nc, name) as c:
        ps = [c.ps(f"ps{j}", [P, BANK]) for j in range(4)]
        s_mm, s_copy = c.sem("mm"), c.sem("copy")
        block = c.enter_context(nc.Block())

        @block.tensor
        def _(pe):
            for n in range(2 * KD):
                k, a = n // 2, n % 2
                if n >= 4:
                    pe.wait_ge(s_copy, n - 3)
                for b in range(NB):
                    m = P if b < NB - 1 else LAST
                    last = nc.tensor.matmul(ps[n % 4][:], R.H[0:m, b, k * P:(k + 1) * P], disp[0:m, b, a * BANK:(a + 1) * BANK], start=(b == 0), stop=(b == NB - 1))
                last.then_inc(s_mm, 1)

        @block.scalar
        def _(act):
            for n in range(2 * KD):
                act.wait_ge(s_mm, n + 1)
                nc.scalar.copy(slotsT[:, n // 2, n % 2 * BANK:(n % 2 + 1) * BANK], ps[n % 4][:]).then_inc(s_copy, 1)


def soft_experts(nc, R, name, w1, b1, w2, b2, slotsT, eo):
    with Scope(nc, name) as c:
        w1t = [c.sb(f"w1{s}", [P, 2, KD, HID]) for s in range(2)]
        w2t = [c.sb(f"w2{s}", [HC, 2, 2, D]) for s in range(2)]
        b1r, b1t = c.sb("b1r", [EXPERTS, HID]), c.sb("b1t", [HC, 2, EXPERTS])
        b2t = c.sb("b2t", [P, EXPERTS // 4, D])
        hT = c.sb("hT", [HC, 4, 2, SLOTS])
        psB = c.ps("psB", [HC, 2, EXPERTS])
        psH = [c.ps(f"psH{j}", [HC, 2, SLOTS]) for j in range(2)]
        psE = [c.ps(f"psE{j}", [P, 2, BANK]) for j in range(2)]
        s_b, s_bt, s_bc, s_h, s_gelu, s_e, s_out = (c.sem(x) for x in ("b", "bt", "bc", "h", "gelu", "e", "out"))
        s_w1, s_w2, s_free = ([c.sem(f"{x}{s}") for s in range(2)] for x in ("w1", "w2", "free"))
        G = EXPERTS // 4
        block = c.enter_context(nc.Block())

        @block.sync
        def _(sp):
            sp.dma_start(b1r[:], b1).then_inc(s_b, 16)
            with sp.Fori(0, G) as g:
                for s in range(2):
                    sp.wait_ge(s_free[s], g + 1)
                    for j in range(2):
                        e = g * 4 + 2 * s + j
                        sp.dma_start(w1t[s][:, j], w1[ds(e, 1)].squeeze(0).rearrange("(k p) h -> p k h", p=P)).then_inc(s_w1[s], 16)
                        sp.dma_start(w2t[s][:, j], w2[ds(e, 1)].squeeze(0).rearrange("(m p) d -> p m d", p=HC)).then_inc(s_w2[s], 16)

        @block.scalar
        def _(act):
            for j in range(4):
                act.dma_start(b2t[32 * j:32 * j + 32], b2.rearrange("(g j) d -> j g d", j=4)[j].partition_broadcast(32)).then_inc(s_b, 16)
            act.wait_ge(s_bt, 1)
            nc.scalar.copy(b1t[:], psB[:]).then_inc(s_bc, 1)
            act.wait_ge(s_bc, 1)
            with act.Fori(0, G) as g:
                for j in range(4):
                    act.wait_ge(s_h, g * 4 + j + 1)
                    if j == 0:
                        act.wait_ge(s_e, g + 1)
                    for m in range(2):
                        last = nc.scalar.activation(hT[:, j, m, :], psH[j % 2][:, m, :], ACT.Gelu, bias=b1t[:, m, ds(g * 4 + j, 1)])
                    last.then_inc(s_gelu, 1)

        @block.vector
        def _(dve):
            for s in range(2):
                dve.sem_inc(s_free[s], 1)
            dve.sem_inc(s_e, 1)
            dve.sem_inc(s_out, 2)
            dve.wait_ge(s_b, 80)
            with dve.Fori(0, G // 2) as i:
                for s in range(2):
                    g = i * 2 + s
                    dve.wait_ge(s_e, g + 2)
                    nc.vector.tensor_tensor(blk(eo, g).rearrange("p (a d) -> p a d", a=2), psE[s][:, :, 0:HALF],
                                            blk(b2t, g).rearrange("p (a d) -> p a d", a=2), ALU.add).then_inc(s_out, 1)

        @block.tensor
        def _(pe):
            pe.wait_ge(s_b, 80)
            for m in range(2):
                last = nc.tensor.transpose(psB[:, m, :], b1r[:, m * HC:(m + 1) * HC], R.ident[0:EXPERTS, 0:EXPERTS])
            last.then_inc(s_bt, 1)
            with pe.Fori(0, G // 2) as i:
                for t in range(2):
                    g = i * 2 + t

                    def hidden(j):
                        if j % 2 == 0:
                            pe.wait_ge(s_w1[j // 2], g * 32 + 32)
                        for m in range(2):
                            for k in range(KD):
                                last = nc.tensor.matmul(psH[j % 2][:, m, :], w1t[j // 2][:, j % 2, k, m * HC:(m + 1) * HC],
                                                        slotsT[:, k, ds(g * P + j * SLOTS, SLOTS)], start=(k == 0), stop=(k == KD - 1))
                        last.then_inc(s_h, 1)

                    def outer(j):
                        if j == 0:
                            pe.wait_ge(s_out, g + 1)
                        if j % 2 == 0:
                            pe.wait_ge(s_w2[j // 2], g * 32 + 32)
                        pe.wait_ge(s_gelu, g * 4 + j + 1)
                        for a in range(2):
                            for m in range(2):
                                last = nc.tensor.matmul(psE[t][32 * j:32 * j + 32, a, 0:HALF], hT[:, j, m, :], w2t[j // 2][:, j % 2, m, a * HALF:(a + 1) * HALF],
                                                        start=(m == 0), stop=(m == 1))
                        if j % 2:
                            last.then_inc(s_free[j // 2], 1)

                    hidden(0)
                    hidden(1)
                    outer(0)
                    hidden(2)
                    outer(1)
                    hidden(3)
                    outer(2)
                    outer(3)
                    pe.wait_ge(s_free[1], g + 2)
                    pe.sem_inc(s_e, 1)


def soft_combine(nc, R, name, comb, eo):
    with Scope(nc, name) as c:
        rows = [c.sb(f"rows{s}", [P, SE]) for s in range(2)]
        rowsT = [c.sb(f"rowsT{s}", [P, KS, P]) for s in range(2)]
        psT = [c.ps(f"psT{s}", [P, 2, BANK]) for s in range(2)]
        psO = [c.ps(f"psO{s}", [P, 2, BANK]) for s in range(2)]
        s_rows, s_turn, s_turned, s_mm, s_add = (c.sem(x) for x in ("rows", "turn", "turned", "mm", "add"))
        block = c.enter_context(nc.Block())

        @block.scalar
        def _(act):
            act.sem_inc(s_turn, 2)
            act.sem_inc(s_mm, 2)
            with act.Fori(0, NB // 2) as i:
                for s in range(2):
                    b = i * 2 + s
                    act.wait_ge(s_turn, b + 1)
                    nc.scalar.copy(rows[s][:], blk(comb, b)).then_inc(s_rows, 1)
                    act.wait_ge(s_turn, b + 3)
                    act.wait_ge(s_mm, b + 1)
                    nc.scalar.copy(rowsT[s][:].rearrange("p (a k) q -> p a (k q)", a=2), psT[s][:]).then_inc(s_turned, 1)

        @block.vector
        def _(dve):
            dve.sem_inc(s_add, 2)
            with dve.Fori(0, NB // 2) as i:
                for s in range(2):
                    b = i * 2 + s
                    dve.wait_ge(s_mm, b + 3)
                    x = blk(R.X, b).rearrange("p (a d) -> p a d", a=2)
                    nc.vector.tensor_tensor(x, x, psO[s][:, :, 0:HALF], ALU.add).then_inc(s_add, 1)

        @block.tensor
        def _(pe):
            with pe.Fori(0, NB // 2) as i:
                for s in range(2):
                    b = i * 2 + s
                    pe.wait_ge(s_rows, b + 1)
                    for k in range(KS):
                        last = nc.tensor.transpose(psT[s][:, k // 4, (k % 4) * P:(k % 4 + 1) * P], rows[s][:, k * P:(k + 1) * P], R.ident[:])
                    last.then_inc(s_turn, 1)
                    pe.wait_ge(s_add, b + 1)
                    pe.wait_ge(s_turned, b + 1)
                    for a in range(2):
                        for k in range(KS):
                            last = nc.tensor.matmul(psO[s][:, a, 0:HALF], rowsT[s][:, k, :], eo[:, k, a * HALF:(a + 1) * HALF], start=(k == 0), stop=(k == KS - 1))
                    last.then_inc(s_mm, 1)


def finish_gcn(nc, R, name, bias, first):
    with Scope(nc, name) as c:
        bs = c.sb("bias", [P, D])
        s_w, s_v = c.sem("weights"), c.sem("v")
        block = c.enter_context(nc.Block())

        @block.sync
        def _(sp):
            sp.dma_start(bs[:], bias.partition_broadcast(P)).then_inc(s_w, 16)

        @block.vector
        def _(dve):
            chain = Chain(dve, s_v)
            dve.wait_ge(s_w, 16)
            with dve.Fori(0, NB) as b:
                chain.loop(b, 3)
                y = blk(R.acc, b)[:, 0:D]
                chain(nc.vector.tensor_tensor(y, y, blk(R.own, b), ALU.add))
                chain(nc.vector.scalar_tensor_tensor(out=y, in0=y, scalar=R.dinv[:, ds(b, 1)], in1=bs[:], op0=ALU.mult, op1=ALU.add))
                if first:
                    chain(nc.vector.tensor_scalar(blk(R.H, b), y, 0.0, None, ALU.max))
                else:
                    chain(nc.vector.tensor_tensor(blk(R.X, b), blk(R.X, b), y, ALU.add))


ME, MHID, TOP = 8, 1152, 2
MB = (TOP * NODES - ME) // P + ME
MSLOTS = MB * P
KH = MHID // P
SPARE = MSLOTS + TOP * P


def route(nc, R, name, wr, br, rows_table, slot_table):
    with Scope(nc, name) as c:
        w, bias, one = c.sb("w", [P, KD, ME]), c.sb("bias", [1, ME]), c.sb("one", [1, P])
        rows = [c.sb(f"rows{s}", [P, D]) for s in range(2)]
        rowsT = [c.sb(f"rowsT{s}", [P, KD, P]) for s in range(2)]
        pr, best = c.sb("probs", [P, NB, ME]), c.sb("best", [P, NB, ME])
        which, whichf = c.sb("which", [P, NB, ME], U32), c.sb("whichf", [P, NB, TOP])
        red = c.sb("red", [P, NB, 1])
        eight, rown, valid = c.sb("eight", [P, ME]), c.sb("rown", [P, NB]), c.sb("valid", [P, NB])
        spare, tri, ones = c.sb("spare", [P, NB, TOP]), c.sb("tri", [P, P]), c.sb("ones", [P, P])
        hot, member = c.sb("hot", [P, NB, TOP, ME]), c.sb("member", [P, NB, ME])
        off = c.sb("off", [P, NB + 1, ME])
        blocks, blocksi = c.sb("blocks", [P, ME]), c.sb("blocksi", [P, ME], I32)
        start = c.sb("start", [P, ME + 1])
        place, placed = c.sb("place", [P, NB, ME]), c.sb("placed", [P, NB, TOP, ME])
        slotf = c.sb("slotf", [P, NB, TOP, 1])
        nodei, none = c.sb("nodei", [P, NB], I32), c.sb("none", [P, SPARE // P], I32)
        mb, ends, exf = c.sb("mb", [1, MB]), c.sb("ends", [1, MB, ME]), c.sb("exf", [1, MB])
        psT = [c.ps(f"psT{s}", [P, 2, BANK]) for s in range(2)]
        psL = [c.ps(f"psL{s}", [P, BANK]) for s in range(2)]
        psC = c.ps("psC", [P, 2, NB, ME])
        s_w, s_v, s_c, s_rows, s_turn, s_turned, s_mm = (c.sem(x) for x in ("weights", "v", "consts", "rows", "turn", "turned", "mm"))
        s_logit, s_sub, s_exp, s_member, s_rank, s_slot, s_st, s_init, s_sc, s_ld = (
            c.sem(x) for x in ("logit", "sub", "exp", "member", "rank", "slot", "st", "init", "sc", "ld"))
        block = c.enter_context(nc.Block())

        @block.sync
        def _(sp):
            sp.dma_start(w[:], wr.rearrange("(k p) e -> p k e", p=P)).then_inc(s_w, 16)
            sp.dma_start(bias[:], br.rearrange("(o e) -> o e", o=1)).then_inc(s_w, 16)
            sp.dma_start(rows_table.rearrange("(b p) d -> p b d", p=P), R.H[:]).then_inc(s_st, 16)
            sp.wait_ge(s_c, 7)
            sp.dma_start(slot_table.rearrange("(p j) o -> p (j o)", p=P), none[:]).then_inc(s_init, 16)
            sp.wait_ge(s_sc, 16 * TOP * NB)
            sp.dma_start(R.slot_node[:], slot_table[0:MSLOTS, :].rearrange("(j p) o -> p (j o)", p=P), allow_slow_non_contiguous=True).then_inc(s_ld, 16)
            sp.wait_ge(s_ld, 16)
            sp.wait_ge(s_st, 16)

        @block.gpsimd
        def _(pool):
            lax = dict(allow_small_or_imprecise_dtypes=True)
            nc.gpsimd.iota(eight[:], [[1, ME]], 0, 0, **lax).then_inc(s_c, 1)
            nc.gpsimd.iota(rown[:], [[P, NB]], 0, 1, **lax).then_inc(s_c, 1)
            nc.gpsimd.iota(nodei[:], [[P, NB]], 0, 1).then_inc(s_c, 1)
            nc.gpsimd.iota(spare[:], [[0, NB], [1, TOP]], MSLOTS, TOP, **lax).then_inc(s_c, 1)
            nc.gpsimd.iota(mb[:], [[1, MB]], 0, 0, **lax).then_inc(s_c, 1)
            nc.gpsimd.memset(ones[:], 1.0).then_inc(s_c, 1)
            nc.gpsimd.memset(none[:], ROWS - 1).then_inc(s_c, 1)
            pool.wait_ge(s_c, 7)
            nc.gpsimd.affine_select(out=tri[:], in_=ones[:], compare_op=ALU.is_gt, fill=0.0, base=0, pattern=[[1, P]], channel_multiplier=-1).then_inc(s_c, 1)
            pool.wait_ge(s_init, 16)
            pool.wait_ge(s_slot, 1)
            for b in range(NB):
                for k in range(TOP):
                    nc.gpsimd.indirect_dma_start(out=slot_table, out_offset=bass.IndirectOffsetOnAxis(ap=R.slot[:, b, k:k + 1], axis=0),
                                                 in_=nodei[:, b:b + 1], in_offset=None).then_inc(s_sc, 16)

        @block.scalar
        def _(act):
            act.wait_ge(s_sub, 1)
            nc.scalar.activation(pr[:], pr[:], ACT.Exp).then_inc(s_exp, 1)

        @block.vector
        def _(dve):
            chain = Chain(dve, s_v)
            dve.sem_inc(s_turn, 2)
            dve.sem_inc(s_mm, 2)
            chain(nc.vector.memset(one[:], 1.0))
            dve.sem_inc(s_logit, 2)
            with dve.Fori(0, NB // 2) as i:
                for s in range(2):
                    b = i * 2 + s
                    dve.wait_ge(s_turn, b + 1)
                    nc.vector.tensor_copy(rows[s][:], blk(R.H, b)).then_inc(s_rows, 1)
                    dve.wait_ge(s_turn, b + 3)
                    dve.wait_ge(s_mm, b + 1)
                    nc.vector.tensor_copy(rowsT[s][:].rearrange("p (a k) q -> p a (k q)", a=2), psT[s][:, :, 0:HALF]).then_inc(s_turned, 1)
                    dve.wait_ge(s_mm, b + 3)
                    nc.vector.tensor_copy(blk(pr, b), psL[s][:, 0:ME]).then_inc(s_logit, 1)
            dve.wait_ge(s_logit, NB + 2)
            chain(nc.vector.tensor_reduce(red[:], pr[:], AX.X, ALU.max))
            chain(nc.vector.tensor_tensor(pr[:], pr[:], red[:].broadcast_to([P, NB, ME]), ALU.subtract))
            dve.sem_inc(s_sub, 1)
            dve.wait_ge(s_exp, 1)
            chain(nc.vector.tensor_reduce(red[:], pr[:], AX.X, ALU.add))
            chain(nc.vector.reciprocal(red[:], red[:]))
            chain(nc.vector.tensor_tensor(pr[:], pr[:], red[:].broadcast_to([P, NB, ME]), ALU.mult))
            for b in range(NB):
                last = nc.vector.max(best[:, b, :], pr[:, b, :])
            chain(last)
            for b in range(NB):
                last = nc.vector.max_index(which[:, b, :], best[:, b, :], pr[:, b, :])
            chain(last)
            nc.vector.tensor_copy(R.gate[:], best[:, :, 0:TOP])
            chain(nc.vector.tensor_copy(whichf[:], which[:, :, 0:TOP]))
            dve.wait_ge(s_c, 8)
            chain(nc.vector.tensor_scalar(valid[:], rown[:], float(NODES), None, ALU.is_lt))
            for k in range(TOP):
                last = nc.vector.tensor_tensor(hot[:, :, k, :], bcast(whichf[:, :, k], 2, ME), bcast(eight[:], 1, NB), ALU.is_equal)
            chain(last)
            chain(nc.vector.tensor_tensor(member[:], hot[:, :, 0, :], hot[:, :, 1, :], ALU.add))
            chain(nc.vector.tensor_tensor(member[:], member[:], bcast(valid[:], 2, ME), ALU.mult))
            dve.sem_inc(s_member, 1)
            dve.wait_ge(s_rank, 1)
            chain(nc.vector.memset(off[:, 0, :], 0.0))
            for b in range(NB):
                chain(nc.vector.tensor_tensor(off[:, b + 1, :], off[:, b, :], psC[:, 1, b, :], ALU.add))
            chain(nc.vector.tensor_scalar(blocks[:], off[:, NB, :], float(P - 1), None, ALU.add))
            chain(nc.vector.tensor_copy(blocksi[:], blocks[:]))
            chain(nc.vector.tensor_single_scalar(blocksi[:], blocksi[:], 7, ALU.arith_shift_right))
            chain(nc.vector.tensor_copy(blocks[:], blocksi[:]))
            chain(nc.vector.memset(start[:, 0:1], 0.0))
            for e in range(ME):
                chain(nc.vector.tensor_tensor(start[:, e + 1:e + 2], start[:, e:e + 1], blocks[:, e:e + 1], ALU.add))
            chain(nc.vector.tensor_tensor(place[:], off[:, 0:NB, :], psC[:, 0], ALU.add))
            chain(nc.vector.tensor_scalar(blocks[:], start[:, 0:ME], float(P), None, ALU.mult))
            chain(nc.vector.tensor_tensor(place[:], place[:], bcast(blocks[:], 1, NB), ALU.add))
            for k in range(TOP):
                last = nc.vector.tensor_tensor(placed[:, :, k, :], hot[:, :, k, :], place[:], ALU.mult)
            chain(last)
            chain(nc.vector.tensor_reduce(slotf[:], placed[:], AX.X, ALU.add))
            sf = slotf[:].squeeze(3)
            chain(nc.vector.tensor_tensor(sf, sf, spare[:], ALU.subtract))
            chain(nc.vector.tensor_tensor(sf, sf, bcast(valid[:], 2, TOP), ALU.mult))
            chain(nc.vector.tensor_tensor(sf, sf, spare[:], ALU.add))
            chain(nc.vector.tensor_copy(R.slot[:], sf))
            dve.sem_inc(s_slot, 1)
            chain(nc.vector.tensor_tensor(ends[:], bcast(start[0:1, 1:ME + 1], 1, MB), bcast(mb[:], 2, ME), ALU.is_le))
            chain(nc.vector.reduce_sum(exf[:], ends[:], AX.X))
            chain(nc.vector.tensor_scalar(exf[:], exf[:], float(ME - 1), None, ALU.min))
            chain(nc.vector.tensor_copy(R.block_expert[:], exf[:]))

        @block.tensor
        def _(pe):
            pe.wait_ge(s_w, 32)
            pe.wait_ge(s_v, 1)
            with pe.Fori(0, NB // 2) as i:
                for s in range(2):
                    b = i * 2 + s
                    pe.wait_ge(s_rows, b + 1)
                    for k in range(KD):
                        last = nc.tensor.transpose(psT[s][:, k // 3, (k % 3) * P:(k % 3 + 1) * P], rows[s][:, k * P:(k + 1) * P], R.ident[:])
                    last.then_inc(s_turn, 1)
                    pe.wait_ge(s_turned, b + 1)
                    pe.wait_ge(s_logit, b + 1)
                    for k in range(KD):
                        nc.tensor.matmul(psL[s][:, 0:ME], rowsT[s][:, k, :], w[:, k, :], start=(k == 0), stop=False)
                    nc.tensor.matmul(psL[s][:, 0:ME], one[:], bias[:], start=False, stop=True).then_inc(s_mm, 1)
            pe.wait_ge(s_member, 1)
            m = member[:].rearrange("p b e -> p (b e)")
            nc.tensor.matmul(psC[:, 0].rearrange("p b e -> p (b e)"), tri[:], m, start=True, stop=True)
            nc.tensor.matmul(psC[:, 1].rearrange("p b e -> p (b e)"), ones[:], m, start=True, stop=True).then_inc(s_rank, 1)


def experts(nc, R, name, rows_table, w1, b1, w2, b2, out_table):
    with Scope(nc, name) as c:
        w1t = [c.sb(f"w1{s}", [P, KD, MHID]) for s in range(2)]
        w2t = [c.sb(f"w2{s}", [P, KH, D]) for s in range(2)]
        b1r, b1t = c.sb("b1r", [ME, MHID]), c.sb("b1t", [P, KH, ME])
        rows = [R.H[:, s, :] for s in range(2)]
        y = [R.H[:, 2 + s, :] for s in range(2)]
        b2t = [R.H[:, 4 + s, :] for s in range(2)]
        rowsT = c.sb("rowsT", [P, KD, P])
        hT = [c.sb(f"hT{s}", [P, KH, P]) for s in range(2)]
        psT = c.ps("psT", [P, 2, BANK])
        psH = [c.ps(f"psH{j}", [P, BANK]) for j in range(4)]
        psY = c.ps("psY", [P, 2, BANK])
        s_b, s_bt, s_bc, s_turn, s_turned, s_h, s_gelu, s_y, s_add = (c.sem(x) for x in ("b", "bt", "bc", "turn", "turned", "h", "gelu", "y", "add"))
        s_w1, s_w2, s_b2, s_rows, s_st = ([c.sem(f"{x}{s}") for s in range(2)] for x in ("w1", "w2", "b2", "rows", "st"))
        block = c.enter_context(nc.Block())
        PAIRS = MB // 2

        def blocks(eng, one):
            with eng.Fori(0, PAIRS) as i:
                for s in range(2):
                    one(i, s)
            if MB % 2:
                one(PAIRS, 0)

        @block.sync
        def _(sp):
            sp.dma_start(b1r[:], b1).then_inc(s_b, 16)

            def load(i, s):
                j = i * 2 + s
                e = sp.value_load(R.block_expert[0:1, ds(j, 1)], min_val=0, max_val=ME - 1)
                sp.wait_ge(s_h, j * KH + KH)
                sp.dma_start(w1t[s][:], w1[ds(e, 1)].squeeze(0).rearrange("(k p) h -> p k h", p=P)).then_inc(s_w1[s], 16)
                sp.wait_ge(s_add, j + 1)
                sp.dma_start(w2t[s][:], w2[ds(e, 1)].squeeze(0).rearrange("(k p) d -> p k d", p=P)).then_inc(s_w2[s], 16)
                sp.dma_start(b2t[s], b2[ds(e, 1)].squeeze(0).partition_broadcast(P)).then_inc(s_b2[s], 16)

            def store(i, s):
                sp.wait_ge(s_add, i * 2 + s + 3)
                sp.dma_start(out_table[ds((i * 2 + s) * P, P), :], y[s]).then_inc(s_st[s], 16)

            load(0, 0)
            load(0, 1)
            with sp.Fori(0, PAIRS - 1) as i:
                for s in range(2):
                    store(i, s)
                    load(i + 1, s)
            store(PAIRS - 1, 0)
            if MB % 2:
                load(PAIRS, 0)
            store(PAIRS - 1, 1)
            if MB % 2:
                store(PAIRS, 0)
            for s in range(2):
                sp.wait_ge(s_st[s], 16 * (1 + PAIRS + (MB % 2 and not s)))

        @block.gpsimd
        def _(pool):
            def gather(i, s):
                pool.wait_ge(s_turn, i * 2 + s + 1)
                nc.gpsimd.tensor_copy(R.list[:, s:s + 1], R.slot_node[:, ds(i * 2 + s, 1)]).then_inc(s_bc, 1)
                pool.wait_ge(s_bc, i * 2 + s + 1)
                pool.nop(nofuse=True)
                nc.gpsimd.indirect_dma_start(out=rows[s], out_offset=None, in_=rows_table,
                                             in_offset=bass.IndirectOffsetOnAxis(ap=R.list[:, s:s + 1], axis=0)).then_inc(s_rows[s], 16)

            blocks(pool, gather)

        @block.scalar
        def _(act):
            act.wait_ge(s_bt, 1)
            nc.scalar.copy(b1t[:], psY[:, 0, 0:KH * ME].rearrange("p (k e) -> p k e", e=ME)).then_inc(s_b, 1)
            act.wait_ge(s_b, 17)

            def gelus(i, s):
                j = i * 2 + s
                e = act.value_load(R.block_expert[0:1, ds(j, 1)], min_val=0, max_val=ME - 1)
                act.wait_ge(s_y, j + 1)
                for m in range(KH):
                    act.wait_ge(s_h, (j + 2) * KH + m + 1)
                    nc.scalar.activation(hT[s][:, m, :], psH[m % 4][:, 0:P], ACT.Gelu, bias=b1t[:, m, ds(e, 1)]).then_inc(s_gelu, 1)

            blocks(act, gelus)

        @block.vector
        def _(dve):
            dve.sem_inc(s_turn, 2)
            dve.sem_inc(s_h, 2 * KH)
            dve.sem_inc(s_y, 2)
            dve.sem_inc(s_add, 2)
            for s in range(2):
                dve.sem_inc(s_st[s], 16)

            def turned(i, s):
                j = i * 2 + s
                dve.wait_ge(s_turn, j + 3)
                nc.vector.tensor_copy(rowsT[:].rearrange("p (a k) q -> p a (k q)", a=2), psT[:, :, 0:HALF]).then_inc(s_turned, 1)

            def finish(i, s):
                j = i * 2 + s
                dve.wait_ge(s_y, j + 3)
                dve.wait_ge(s_b2[s], i * 16 + 16)
                dve.wait_ge(s_st[s], i * 16 + 16)
                nc.vector.tensor_tensor(y[s].rearrange("p (a d) -> p a d", a=2), psY[:, :, 0:HALF], b2t[s].rearrange("p (a d) -> p a d", a=2), ALU.add).then_inc(s_add, 1)

            def both(i, s):
                turned(i, s)
                finish(i, s)

            blocks(dve, both)

        @block.tensor
        def _(pe):
            pe.wait_ge(s_b, 16)
            for k in range(KH):
                last = nc.tensor.transpose(psY[:, 0, k * ME:(k + 1) * ME], b1r[:, k * P:(k + 1) * P], R.ident[0:ME, 0:ME])
            last.then_inc(s_bt, 1)
            pe.wait_ge(s_b, 17)

            def one(i, s):
                j = i * 2 + s
                pe.wait_ge(s_rows[s], i * 16 + 16)
                for k in range(KD):
                    last = nc.tensor.transpose(psT[:, k // 3, (k % 3) * P:(k % 3 + 1) * P], rows[s][:, k * P:(k + 1) * P], R.ident[:])
                last.then_inc(s_turn, 1)
                pe.wait_ge(s_turned, j + 1)
                pe.wait_ge(s_w1[s], i * 16 + 16)
                for m in range(KH):
                    if m >= 4:
                        pe.wait_ge(s_gelu, j * KH + m - 3)
                    for k in range(KD):
                        last = nc.tensor.matmul(psH[m % 4][:, 0:P], w1t[s][:, k, m * P:(m + 1) * P], rowsT[:, k, :],
                                                start=(k == 0), stop=(k == KD - 1))
                    last.then_inc(s_h, 1)
                pe.wait_ge(s_w2[s], i * 16 + 16)
                pe.wait_ge(s_add, j + 2)
                for m in range(KH):
                    pe.wait_ge(s_gelu, j * KH + m + 1)
                    for a in range(2):
                        last = nc.tensor.matmul(psY[:, a, 0:HALF], hT[s][:, m, :], w2t[s][:, m, a * HALF:(a + 1) * HALF], start=(m == 0), stop=(m == KH - 1))
                last.then_inc(s_y, 1)

            blocks(pe, one)


def combine(nc, R, name, out_table, out):
    with Scope(nc, name) as c:
        g = [[R.H[:, 2 * s + k, :] for k in range(TOP)] for s in range(4)]
        s_v, s_done, s_st = c.sem("v"), c.sem("done"), c.sem("st")
        s_g = [c.sem(f"g{s}") for s in range(4)]
        block = c.enter_context(nc.Block())

        @block.gpsimd
        def _(pool):
            for b in range(NB):
                if b >= 4:
                    pool.wait_ge(s_done, b - 3)
                m = P if b < NB - 1 else LAST
                for k in range(TOP):
                    nc.gpsimd.indirect_dma_start(out=g[b % 4][k][0:m], out_offset=None, in_=out_table,
                                                 in_offset=bass.IndirectOffsetOnAxis(ap=R.slot[0:m, b, k:k + 1], axis=0)).then_inc(s_g[b % 4], 16)

        @block.vector
        def _(dve):
            chain = Chain(dve, s_v)
            for b in range(NB):
                dve.wait_ge(s_g[b % 4], 32 * (b // 4 + 1))
                m = P if b < NB - 1 else LAST
                x = R.X[0:m, b, :]
                chain(nc.vector.scalar_tensor_tensor(out=x, in0=g[b % 4][0][0:m], scalar=R.gate[0:m, b, 0:1], in1=x, op0=ALU.mult, op1=ALU.add))
                nc.vector.scalar_tensor_tensor(out=x, in0=g[b % 4][1][0:m], scalar=R.gate[0:m, b, 1:2], in1=x, op0=ALU.mult, op1=ALU.add).then_inc(s_done, 1)

        @block.sync
        def _(sp):
            for b in range(NB):
                m = P if b < NB - 1 else LAST
                sp.wait_ge(s_done, b + 1)
                sp.dma_start(out[b * P:b * P + m, :], R.X[0:m, b, :]).then_inc(s_st, 16)
            sp.wait_ge(s_st, 16 * NB)


def program(nc, A, out):
    with ExitStack() as ctx:
        def sb(name, shape, dt=F32):
            return ctx.enter_context(nc.sbuf_tensor(name, shape, dt))

        class R:
            pass

        R.ident = sb("ident", [P, P])
        R.nodes = sb("nodes", [P, ROWS])
        R.X = sb("X", [P, NB, D])
        R.H = sb("H", [P, NB, D])
        R.src = sb("src", [P, TILES], I32)
        R.dsti = sb("dsti", [P, TILES], I32)
        R.dst = sb("dst", [P, TILES])
        R.ends = sb("ends", [QT, 1, 4, P + 2])
        R.visit_group = sb("visit_group", [1, VISITS], I32)
        R.visit_block = sb("visit_block", [1, VISITS], I32)
        R.dinv = sb("dinv", [P, NB])

        def table(name, width, rows=ROWS):
            return nc.dram_tensor(name, (rows, width), F32, kind="Internal").ap()

        setup(nc, R, A["x"], A["src"], A["dst"])
        norm_rows(nc, R, "ln0")
        fs, fd = table("fs1", D + 16), table("fd1", D + 16)
        with ExitStack() as gat:
            R.L = gat.enter_context(nc.sbuf_tensor("L", [P, HEADS, TILES], F32))
            attn1 = A["L0_gnn_attn1"].rearrange("h d -> (h d)")
            project(nc, R, "p1", [A["L0_gnn_W1s"], A["L0_gnn_W1d"]], [fs, fd], [A["L0_gnn_b1s"], A["L0_gnn_b1d"]], attn1, HEADS)
            logits(nc, R, "l1", fs, fd, attn1, HEADS)
            edge_softmax(nc, R, "s1", HEADS)
            R.acc = gat.enter_context(nc.sbuf_tensor("acc", [P, NB, D + 17], F32))
            aggregate(nc, R, "a1", fs, D + 16, HEADS, count=True)
            finish_gat(nc, R, "f1", HEADS, A["L0_gnn_ln1_w"], A["L0_gnn_ln1_b"], True)
            attno = A["L0_gnn_attno"].rearrange("h d -> (h d)")
            fs, fd = table("fs2", D + 2), table("fd2", D + 2)
            project(nc, R, "p2", [A["L0_gnn_Wos"], A["L0_gnn_Wod"]], [fs, fd], [A["L0_gnn_bos"], A["L0_gnn_bod"]], attno, 1)
            logits(nc, R, "l2", fs, fd, attno, 1)
            edge_softmax(nc, R, "s2", 1)
            aggregate(nc, R, "a2", fs, D + 2, 1)
            finish_gat(nc, R, "f2", 1, A["L0_gnn_lno_w"], A["L0_gnn_lno_b"], False)
        norm_rows(nc, R, "ln1", l2=True)
        with ExitStack() as soft:
            comb = soft.enter_context(nc.sbuf_tensor("comb", [P, NB, SE], F32))
            slotsT = soft.enter_context(nc.sbuf_tensor("slotsT", [P, KD, SE], F32))
            with nc.sbuf_tensor("disp", [P, NB, SE], F32) as disp:
                soft_logits(nc, R, "m1", A["L0_ffn_phi"], A["L0_ffn_scale"], disp, comb, slotsT)
                soft_slots(nc, R, "m2", disp, slotsT)
            eo = R.H
            soft_experts(nc, R, "m3", A["L0_ffn_w1"], A["L0_ffn_b1"], A["L0_ffn_w2"], A["L0_ffn_b2"], slotsT, eo)
            soft_combine(nc, R, "m4", comb, eo)
        norm_rows(nc, R, "ln2")
        with ExitStack() as gcn:
            R.own = gcn.enter_context(nc.sbuf_tensor("own", [P, NB, D], F32))
            R.acc = gcn.enter_context(nc.sbuf_tensor("acc2", [P, NB, D], F32))
            for n, w, bias in ((1, "L1_gnn_W1", "L1_gnn_b1"), (2, "L1_gnn_W2", "L1_gnn_b2")):
                hs = table(f"hs{n}", D)
                project(nc, R, f"pc{n}", [A[w]], [hs])
                aggregate(nc, R, f"ac{n}", hs, D)
                finish_gcn(nc, R, f"fc{n}", A[bias], n == 1)
        norm_rows(nc, R, "ln3")
        R.gate, R.slot = sb("gate", [P, NB, TOP]), sb("slot", [P, NB, TOP], I32)
        R.slot_node, R.block_expert = sb("slot_node", [P, MB], I32), sb("block_expert", [1, MB], I32)
        R.list = sb("list", [P, 2], I32)
        rows_table, out_table = table("moe_rows", D), table("moe_out", D, MSLOTS)
        slot_table = nc.dram_tensor("moe_slots", (SPARE, 1), I32, kind="Internal").ap()
        route(nc, R, "r1", A["L1_ffn_router_w"], A["L1_ffn_router_b"], rows_table, slot_table)
        experts(nc, R, "r2", rows_table, A["L1_ffn_w1"], A["L1_ffn_b1"], A["L1_ffn_w2"], A["L1_ffn_b2"], out_table)
        combine(nc, R, "r3", out_table, out)


_INS = ["x", "src", "dst", "L0_gnn_W1s", "L0_gnn_b1s", "L0_gnn_W1d", "L0_gnn_b1d", "L0_gnn_attn1", "L0_gnn_ln1_w", "L0_gnn_ln1_b",
        "L0_gnn_Wos", "L0_gnn_bos", "L0_gnn_Wod", "L0_gnn_bod", "L0_gnn_attno", "L0_gnn_lno_w", "L0_gnn_lno_b",
        "L0_ffn_phi", "L0_ffn_scale", "L0_ffn_w1", "L0_ffn_b1", "L0_ffn_w2", "L0_ffn_b2",
        "L1_gnn_W1", "L1_gnn_b1", "L1_gnn_W2", "L1_gnn_b2",
        "L1_ffn_router_w", "L1_ffn_router_b", "L1_ffn_w1", "L1_ffn_b1", "L1_ffn_w2", "L1_ffn_b2"]


def kernel(**inputs):
    import numpy as np
    import concourse.bacc as bacc
    from concourse.bass_utils import run_bass_kernel_spmd as run

    nc = bacc.Bacc("TRN2", target_bir_lowering=False, num_devices=1)
    arrays, args = {}, {}
    for name in _INS:
        a = np.ascontiguousarray(inputs[name])
        arrays[f"in_{name}"] = a
        args[name] = nc.dram_tensor(f"in_{name}", a.shape, mybir.dt.from_np(a.dtype), kind="ExternalInput").ap()
    out = nc.dram_tensor("out", (NODES, D), F32, kind="ExternalOutput").ap()
    program(nc, args, out)
    r = run(nc, [arrays], core_ids=[0])
    return r.results[0]["out"]
```

```python
from contextlib import ExitStack

import concourse.bass as bass
from concourse import mybir

ALU = mybir.AluOpType
ACT = mybir.ActivationFunctionType
AX = mybir.AxisListType
F32 = mybir.dt.float32
I32 = mybir.dt.int32
U32 = mybir.dt.uint32
FR = mybir.dt.float32r
F16, BF16 = mybir.dt.float16, mybir.dt.bfloat16

P = 128
NODES, D = 1250, 768
NB = -(-NODES // P)
ROWS = NB * P
LAST = NODES - (NB - 1) * P
KD = D // P
EDGES = 40000
UN = 4
GROUPS = -(-EDGES // (P * UN))
TILES = GROUPS * UN
VISITS = GROUPS + NB - 1
QT = TILES // 4
HALF = D // 2
NEG = -1.0e30
NO_NODE = 4096
HEADS = 8
BANK = 512
ds = bass.ds


def bcast(ap, axis, n):
    new = ap.unsqueeze(axis)
    shape = list(new.shape)
    shape[axis] = n
    return new.broadcast_to(shape)


class Chain:

    def __init__(self, eng, sem):
        self.eng, self.sem, self.base, self.i, self.per, self.n = eng, sem, 0, None, 0, 0

    def loop(self, i, per):
        self.base += self.n
        self.i, self.per, self.n = i, per, 0

    def end(self, times):
        assert self.n == self.per, (self.n, self.per)
        self.base += self.per * times
        self.i, self.n = None, 0

    def __call__(self, ins):
        ins.then_inc(self.sem, 1)
        self.n += 1
        at = self.base + self.n
        self.eng.wait_ge(self.sem, at if self.i is None else self.i * self.per + at)
        return ins


class Scope(ExitStack):

    def __init__(self, nc, name):
        super().__init__()
        self.nc, self.name, self.sems = nc, name, []
        self.callback(self.clear)

    def clear(self):
        if self.sems:
            self.nc.clear_and_free_semaphores(self.sems)
            self.nc.all_engine_barrier(sem_only=True)

    def sb(self, name, shape, dt=F32):
        return self.enter_context(self.nc.sbuf_tensor(f"{self.name}_{name}", shape, dt))

    def ps(self, name, shape):
        return self.enter_context(self.nc.psum_tensor(f"{self.name}_{name}", shape, F32))

    def sem(self, name):
        self.sems.append(self.nc.alloc_semaphore(f"{self.name}_{name}"))
        return self.sems[-1]


def head_width(heads):
    he = D // heads + 3
    while heads * he % 4:
        he += 1
    return he


def blk(t, b):
    return t[:, ds(b, 1), :].squeeze(1)


def row_stats(chain, nc, src, st, mv):
    nc.vector.bn_stats(st[:, 0, :], src[:, 0:HALF])
    chain(nc.vector.bn_stats(st[:, 1, :], src[:, HALF:D]))
    chain.eng.nop(nofuse=True)
    chain(nc.vector.bn_aggr(mv, st[:]))


def layer_norms(nc, dve, chain, H, X, W, weight=None, bias=None):
    with dve.Fori(0, NB) as b:
        chain.loop(b, 3)
        row_stats(chain, nc, blk(X, b)[:, 0:D], W.st, W.mvb[:])
        chain(nc.vector.tensor_copy(blk(W.mv, b), W.mvb[:]))
    chain.end(NB)
    chain(nc.vector.tensor_scalar(W.val[:], W.mv[:, :, 1:2].squeeze(2), 1e-5, None, ALU.add))
    inverse_roots(nc, dve, chain, W, W.val, W.root, W.rstd)
    with dve.Fori(0, NB) as b:
        chain.loop(b, 3 if weight is not None else 1)
        h = blk(H, b)
        chain(nc.vector.tensor_scalar(h, blk(X, b)[:, 0:D], W.mv[:, ds(b, 1), 0:1].squeeze(1), W.rstd[:, ds(b, 1)], ALU.subtract, ALU.mult))
        if weight is not None:
            chain(nc.vector.tensor_tensor(h, h, weight, ALU.mult))
            chain(nc.vector.tensor_tensor(h, h, bias, ALU.add))
    chain.end(NB)


class Roots:

    def __init__(self, c):
        self.st, self.mvb, self.mv = c.sb("st", [P, 2, 6]), c.sb("mvb", [P, 2]), c.sb("mv", [P, NB, 2])
        self.val, self.root, self.rstd, self.sq = (c.sb(x, [P, NB]) for x in ("val", "root", "rstd", "sq"))
        self.s_val, self.s_root, self.n, self.m = c.sem("val"), c.sem("root"), 0, 0


def inverse_roots(nc, dve, chain, W, val, root, out):
    W.n += 1
    dve.sem_inc(W.s_val, 1)
    dve.wait_ge(W.s_root, W.n)
    chain(nc.vector.reciprocal(out[:], root[:]))
    chain(nc.vector.tensor_tensor(W.sq[:], out[:], out[:], ALU.mult))
    chain(nc.vector.tensor_tensor(W.sq[:], W.sq[:], val[:], ALU.mult))
    chain(nc.vector.tensor_scalar(W.sq[:], W.sq[:], -0.5, 1.5, ALU.mult, ALU.add))
    chain(nc.vector.tensor_tensor(out[:], out[:], W.sq[:], ALU.mult))


def square_roots(nc, act, W, val, root):
    W.m += 1
    act.wait_ge(W.s_val, W.m)
    nc.scalar.activation(root[:], val[:], ACT.Sqrt).then_inc(W.s_root, 1)


def setup(nc, R, x, src, dst):
    with Scope(nc, "set") as c:
        rows = c.sb("rows", [QT, 2, 4, P], I32)
        rowsf = c.sb("rowsf", [QT, 2, 4, P])
        first = c.sb("first", [1, GROUPS], I32)
        firstf = c.sb("firstf", [1, GROUPS])
        steps = c.sb("steps", [1, VISITS])
        before = c.sb("before", [1, VISITS, GROUPS - 1])
        svf = c.sb("svf", [1, VISITS])
        cvf = c.sb("cvf", [1, VISITS])
        ones = c.sb("ones", [P, P])
        blocks = c.sb("blocks", [P, TILES], I32)
        minus_p = c.sb("minus_p", [P, 1])
        turned = c.ps("turned", [P, 2, 4, P])
        spread = c.ps("spread", [P, VISITS])
        s_blocks = c.sem("blocks")
        s_zero, s_x, s_e, s_f, s_p = (c.sem(n) for n in ("zero", "x", "edges", "first", "lists"))
        s_gi, s_id, s_iota, s_cast, s_t, s_v = (c.sem(n) for n in ("gi", "ident", "iota", "cast", "turned", "v"))
        full = EDGES - 3 * QT * P
        block = c.enter_context(nc.Block())

        @block.sync
        def _(sp):
            sp.wait_ge(s_zero, 3)
            sp.dma_start(R.X[:, 0:NB - 1, :], x[0:(NB - 1) * P, :].rearrange("(b p) d -> p b d", p=P)).then_inc(s_x, 16)
            sp.dma_start(R.X[0:LAST, NB - 1, :], x[(NB - 1) * P:NODES, :]).then_inc(s_x, 16)
            for j, e in enumerate((src, dst)):
                whole = full // P
                sp.dma_start(rows[:, j, 0:3, :], e[0:3 * QT * P].rearrange("(q t p) -> t q p", q=3, p=P)).then_inc(s_e, 16)
                sp.dma_start(rows[0:whole, j, 3, :], e[3 * QT * P:3 * QT * P + whole * P].rearrange("(t p) -> t p", p=P)).then_inc(s_e, 16)
                sp.dma_start(rows[whole:whole + 1, j, 3, 0:full - whole * P], e[3 * QT * P + whole * P:EDGES].rearrange("(t p) -> t p", t=1)).then_inc(s_e, 16)
            with nc.allow_non_contiguous_dma("one destination of each group"):
                sp.dma_start(first[:, 0:GROUPS - 1], dst[0:(GROUPS - 1) * P * UN].rearrange("(g e) -> g e", e=P * UN)[:, 0:1].rearrange("g o -> o g")).then_inc(s_f, 16)
                sp.dma_start(first[:, GROUPS - 1:GROUPS], dst[(GROUPS - 1) * P * UN:(GROUPS - 1) * P * UN + 1].rearrange("(a b) -> a b", a=1)).then_inc(s_f, 16)
            sp.wait_ge(s_x, 32)
            sp.wait_ge(s_cast, 1)
            for q in range(4):
                sp.dma_start(R.dst_rows.rearrange("g (u p) -> (g u) p", p=P)[q * QT:(q + 1) * QT, :], rowsf[:, 1, q, :]).then_inc(s_p, 16)
            sp.wait_ge(s_p, 64)

        @block.gpsimd
        def _(pool):
            nc.gpsimd.memset(ones[:], 1.0).then_inc(s_gi, 1)
            nc.gpsimd.iota(R.nodes[:], [[1, ROWS]], 0, 0, allow_small_or_imprecise_dtypes=True).then_inc(s_iota, 1)
            nc.gpsimd.iota(steps[:], [[1, VISITS]], 0, 0, allow_small_or_imprecise_dtypes=True).then_inc(s_iota, 1)
            nc.gpsimd.iota(minus_p[:], [[1, 1]], 0, -1, allow_small_or_imprecise_dtypes=True).then_inc(s_iota, 1)
            pool.wait_ge(s_gi, 1)
            nc.gpsimd.affine_select(out=R.ident[:], in_=ones[:], compare_op=ALU.is_equal, fill=0.0, base=0,
                                    pattern=[[-1, P]], channel_multiplier=1).then_inc(s_id, 1)

        @block.vector
        def _(dve):
            chain = Chain(dve, s_v)
            nc.vector.memset(R.X[:, NB - 1, :], 0.0).then_inc(s_zero, 1)
            nc.vector.memset(rows[:, 0], 0).then_inc(s_zero, 1)
            nc.vector.memset(rows[:, 1], NO_NODE).then_inc(s_zero, 1)
            dve.wait_ge(s_f, 32)
            dve.wait_ge(s_iota, 3)
            chain(nc.vector.tensor_single_scalar(first[:], first[:], 7, ALU.arith_shift_right))
            chain(nc.vector.tensor_copy(firstf[:], first[:]))
            chain(nc.vector.tensor_tensor(firstf[:], firstf[:], steps[:, 0:GROUPS], ALU.add))
            chain(nc.vector.tensor_tensor(before[:], bcast(firstf[:, 1:GROUPS], 1, VISITS), bcast(steps[:], 2, GROUPS - 1), ALU.is_le))
            chain(nc.vector.reduce_sum(svf[:], before[:], AX.X))
            chain(nc.vector.tensor_tensor(cvf[:], steps[:], svf[:], ALU.subtract))
            nc.vector.tensor_copy(R.visit_group[:], svf[:])
            nc.vector.tensor_copy(R.visit_block[:], cvf[:])
            dve.sem_inc(s_blocks, 1)
            dve.wait_ge(s_e, 96)
            nc.vector.tensor_copy(rowsf[:], rows[:]).then_inc(s_cast, 1)
            dve.wait_ge(s_t, 1)
            for q in range(4):
                nc.vector.tensor_copy(R.src[:, q * QT:(q + 1) * QT], turned[:, 0, q, 0:QT])
                nc.vector.tensor_copy(R.dst[:, q * QT:(q + 1) * QT], turned[:, 1, q, 0:QT])
                chain(nc.vector.tensor_copy(blocks[:, q * QT:(q + 1) * QT], turned[:, 1, q, 0:QT]))
            nc.vector.tensor_copy(R.ends[:, :, :, 1:P + 1], rowsf[:, 1:2])
            nc.vector.tensor_scalar(R.visit_minus[:], spread[:], -1.0, None, ALU.mult)
            nc.vector.tensor_scalar(R.visit_row[:], spread[:], -float(P), minus_p[:], ALU.mult, ALU.add)
            chain(nc.vector.tensor_single_scalar(blocks[:], blocks[:], 7, ALU.arith_shift_right))
            chain(nc.vector.tensor_copy(R.dst_block[:], blocks[:]))
            chain(nc.vector.memset(R.ends[:, :, :, 0:1], -1.0))
            chain(nc.vector.memset(R.ends[:, :, :, P + 1:P + 2], -1.0))

        @block.tensor
        def _(pe):
            pe.wait_ge(s_id, 1)
            pe.wait_ge(s_cast, 1)
            for j in range(2):
                for q in range(4):
                    nc.tensor.transpose(turned[:, j, q, 0:QT], rowsf[:, j, q, :], R.ident[0:QT, 0:QT])
            pe.wait_ge(s_blocks, 1)
            pe.wait_ge(s_gi, 1)
            last = nc.tensor.matmul(spread[:], ones[0:1, :], cvf[:], start=True, stop=True)
            last.then_inc(s_t, 1)


def norm_rows(nc, R, name, l2=False):
    with Scope(nc, name) as c:
        W = Roots(c)
        sq = c.sb("squares", [P, D])
        s_v = c.sem("v")
        block = c.enter_context(nc.Block())

        @block.scalar
        def _(act):
            for _ in range(2 if l2 else 1):
                square_roots(nc, act, W, W.val, W.root)

        @block.vector
        def _(dve):
            chain = Chain(dve, s_v)
            layer_norms(nc, dve, chain, R.H, R.X, W)
            if l2:
                with dve.Fori(0, NB) as b:
                    chain.loop(b, 1)
                    h = blk(R.H, b)
                    chain(nc.vector.scalar_tensor_tensor(out=sq[:], in0=h, scalar=1.0, in1=h, op0=ALU.mult, op1=ALU.mult, accum_out=W.val[:, ds(b, 1)]))
                chain.end(NB)
                chain(nc.vector.tensor_scalar(W.val[:], W.val[:], 1e-24, None, ALU.max))
                inverse_roots(nc, dve, chain, W, W.val, W.root, W.rstd)
                with dve.Fori(0, NB) as b:
                    nc.vector.tensor_scalar(blk(R.H, b), blk(R.H, b), W.rstd[:, ds(b, 1)], None, ALU.mult)


def project(nc, R, name, weights, table, biases, attn, heads):
    n = len(weights)
    hd, he = D // heads, head_width(heads)
    width = heads * he
    half = width // 2
    loads = n * (KD + 1) + 1
    with Scope(nc, name) as c:
        w = [c.sb(f"w{j}", [P, KD, heads, he]) for j in range(n)]
        bias = [c.sb(f"bias{j}", [1, heads, he]) for j in range(n)]
        ones = c.sb("ones", [1, P])
        rows = [c.sb(f"rows{s}", [P, D]) for s in range(2)]
        prod, at = rows
        rowsT = [c.sb(f"rowsT{s}", [P, KD, P]) for s in range(2)]
        out = [c.sb(f"out{s}", [P, width]) for s in range(2)]
        psT = [c.ps(f"psT{s}", [P, 2, BANK]) for s in range(2)]
        psO = [c.ps(f"psO{j}", [P, 2, BANK]) for j in range(n)]
        s_w, s_v, s_wide, s_rows = c.sem("weights"), c.sem("v"), c.sem("wide"), c.sem("rows")
        s_turn, s_turned, s_mm, s_taken, s_low = (c.sem(x) for x in ("turn", "turned", "mm", "taken", "low"))
        s_store = [c.sem(f"store{s}") for s in range(2)]
        block = c.enter_context(nc.Block())

        @block.sync
        def _(sp):
            for j in range(n):
                for k in range(KD):
                    sp.dma_start(w[j][:, k, :, 0:hd], weights[j][k * P:(k + 1) * P, :].rearrange("p (h e) -> p h e", h=heads)).then_inc(s_w, 16)
                sp.dma_start(bias[j][:, :, 0:hd], biases[j].rearrange("(o h e) -> o h e", o=1, h=heads)).then_inc(s_w, 16)
            sp.dma_start(at[:], attn.partition_broadcast(P)).then_inc(s_w, 16)
            with sp.Fori(0, NB // 2) as i:
                for s in range(2):
                    b = i * 2 + s
                    sp.wait_ge(s_taken, b * n + n + 1)
                    sp.dma_start(table[ds(b * P, P), :], out[s][:]).then_inc(s_store[s], 16)
            for s in range(2):
                sp.wait_ge(s_store[s], 16 * (1 + NB // 2))

        @block.vector
        def _(dve):
            chain = Chain(dve, s_v)
            dve.sem_inc(s_turn, 2)
            dve.sem_inc(s_mm, 2 * n)
            nc.vector.memset(ones[:], 1.0).then_inc(s_wide, 1)
            dve.wait_ge(s_w, 16 * loads)
            for j in range(n):
                for k in range(KD + 1):
                    a = w[j][:, k] if k < KD else bias[j][:]
                    m = P if k < KD else 1
                    pr = prod[0:m, :].rearrange("p (h e) -> p h e", h=heads)
                    nc.vector.memset(a[:, :, hd:hd + 1], 0.0 if k < KD or j else 1.0)
                    if he > hd + 3:
                        nc.vector.memset(a[:, :, hd + 3:he], 0.0)
                    chain(nc.vector.scalar_tensor_tensor(out=pr, in0=a[:, :, 0:hd], scalar=0.2, in1=at[0:m, :].rearrange("p (h e) -> p h e", h=heads),
                                                         op0=ALU.mult, op1=ALU.mult))
                    chain(nc.vector.tensor_reduce(a[:, :, hd + 1:hd + 2], pr, AX.X, ALU.add))
                    chain(nc.vector.tensor_scalar(a[:, :, hd + 2:hd + 3], a[:, :, hd + 1:hd + 2], -1.0, None, ALU.mult))
            dve.sem_inc(s_wide, 1)

            def turn(i, s):
                b = i * 2 + s
                dve.wait_ge(s_turn, b + 1)
                nc.vector.tensor_copy(rows[s][:], blk(R.H, b)).then_inc(s_rows, 1)
                dve.wait_ge(s_turn, b + 3)
                dve.wait_ge(s_mm, b * n + n)
                nc.vector.tensor_copy(rowsT[s][:].rearrange("p (a k) q -> p a (k q)", a=2), psT[s][:, :, 0:HALF]).then_inc(s_turned, 1)

            def low(b):
                dve.wait_ge(s_taken, b * n + n + 2)
                hi = blk(R.fd, b).bitcast(F32).rearrange("p (a e) -> p a e", a=2)
                nc.vector.tensor_tensor(blk(R.fdl, b).rearrange("p (a e) -> p a e", a=2), psO[1][:, :, 0:half], hi, ALU.subtract).then_inc(s_low, 1)

            dve.sem_inc(s_low, 1)
            turn(0, 0)
            with dve.Fori(0, NB // 2 - 1) as i:
                turn(i, 1)
                low(i * 2)
                turn(i + 1, 0)
                low(i * 2 + 1)
            turn(NB // 2 - 1, 1)
            low(NB - 2)
            low(NB - 1)

        @block.scalar
        def _(act):
            act.sem_inc(s_taken, n)
            for s in range(2):
                act.sem_inc(s_store[s], 16)
            with act.Fori(0, NB // 2) as i:
                for s in range(2):
                    b = i * 2 + s
                    act.wait_ge(s_store[s], i * 16 + 16)
                    act.wait_ge(s_mm, b * n + 2 * n + 1)
                    nc.scalar.copy(out[s][:].rearrange("p (a e) -> p a e", a=2), psO[0][:, :, 0:half]).then_inc(s_taken, 1)
                    act.wait_ge(s_mm, b * n + 2 * n + 2)
                    nc.scalar.copy(blk(R.fd, b).rearrange("p (a e) -> p a e", a=2), psO[1][:, :, 0:half]).then_inc(s_taken, 1)

        @block.tensor
        def _(pe):
            pe.wait_ge(s_wide, 2)
            pe.wait_ge(s_w, 16 * loads)

            def turn(b, s):
                pe.wait_ge(s_rows, b + 1)
                for k in range(KD):
                    last = nc.tensor.transpose(psT[s][:, k // 3, (k % 3) * P:(k % 3 + 1) * P], rows[s][:, k * P:(k + 1) * P], R.ident[:])
                last.then_inc(s_turn, 1)

            def multiply(b, s):
                pe.wait_ge(s_turned, b + 1)
                for j in range(n):
                    pe.wait_ge(s_taken, b * n + j + 1)
                    if j:
                        pe.wait_ge(s_low, b + 1)
                    for a in range(2):
                        o = psO[j][:, a, 0:half]
                        cut = slice(a * half, (a + 1) * half)
                        for k in range(KD):
                            last = nc.tensor.matmul(o, rowsT[s][:, k, :], w[j][:, k].rearrange("p h e -> p (h e)")[:, cut],
                                                    start=(k == 0), stop=False)
                        last = nc.tensor.matmul(o, ones[:], bias[j][:].rearrange("p h e -> p (h e)")[:, cut], start=False, stop=True)
                    last.then_inc(s_mm, 1)

            turn(0, 0)
            with pe.Fori(0, NB // 2 - 1) as i:
                turn(i * 2 + 1, 1)
                multiply(i * 2, 0)
                turn(i * 2 + 2, 0)
                multiply(i * 2 + 1, 1)
            turn(NB - 1, 1)
            multiply(NB - 2, 0)
            multiply(NB - 1, 1)


def logits(nc, R, name, fs, attn, heads):
    hd, he = D // heads, head_width(heads)
    width = heads * he
    half = width // 2
    cuts = [(0, half), (half, width)]
    if heads == 1:
        added = [(0, half)]
        parts = cuts
    else:
        added = [(0, half), (half, half + 2 * he)]
        parts = [(h * he, (h + 1) * he) for h in range(heads)]
    by_pe = added[-1][1]
    with Scope(nc, name) as c:
        at = c.sb("attn", [P, width])
        lists = c.sb("list", [P, 2, UN], I32)
        g = c.sb("g", [P, 2, UN, width])
        dsts, away = c.sb("dsts", [P, 2, UN * P]), c.sb("away", [P, UN * P])
        one = c.sb("one", [P, 1])
        spread = c.sb("spread", [P, 2, UN, P], FR)
        z = c.sb("z", [P, 2, width - by_pe])
        zr = c.sb("zr", [P, 2, width])
        part = c.sb("part", [P, 2, UN, len(parts)])
        inside = c.sb("inside", [P, 2, UN])
        fdc = [[c.sb(f"fdc{s}{t}", [P, width], FR) for t in range(2)] for s in range(2)]
        psZ = [c.ps(f"psZ{k}", [P, 2, BANK]) for k in range(UN)]
        s_at, s_v, s_one, s_list, s_z = c.sem("attn"), c.sem("v"), c.sem("one"), c.sem("list"), c.sem("z")
        s_g = [[c.sem(f"g{s}{k}") for k in range(UN)] for s in range(2)]
        s_d = [c.sem(f"d{s}") for s in range(2)]
        s_away, s_spread, s_rows, s_inside = (c.sem(x) for x in ("away", "spread", "rows", "inside"))
        s_mm, s_part, s_tail, s_sum = c.sem("mm"), c.sem("part"), c.sem("tail"), c.sem("sum")
        block = c.enter_context(nc.Block())

        @block.sync
        def _(sp):
            sp.wait_ge(s_one, 1)
            sp.dma_start(at[:].rearrange("p (h e) -> p h e", h=heads)[:, :, 0:hd], attn.rearrange("(h e) -> h e", h=heads).partition_broadcast(P)).then_inc(s_at, 16)
            with sp.Fori(0, VISITS // 2) as i:
                for s in range(2):
                    v = i * 2 + s
                    grp = sp.value_load(R.visit_group[0:1, ds(v, 1)], min_val=0, max_val=GROUPS - 1)
                    sp.wait_ge(s_spread, v + 1)
                    sp.dma_start(dsts[:, s, :], R.dst_rows[ds(grp, 1), :].squeeze(0).partition_broadcast(P)).then_inc(s_d[s], 16)

        @block.scalar
        def _(act):
            act.sem_inc(s_spread, 2)
            act.wait_ge(s_one, 1)
            with act.Fori(0, VISITS // 2) as i:
                for s in range(2):
                    v = i * 2 + s
                    b = act.value_load(R.visit_block[0:1, ds(v, 1)], min_val=0, max_val=NB - 1)
                    grp = act.value_load(R.visit_group[0:1, ds(v, 1)], min_val=0, max_val=GROUPS - 1)
                    act.wait_ge(s_d[s], i * 16 + 16)
                    nc.scalar.activation(away[:], dsts[:, s, :], ACT.Abs, bias=R.visit_row[:, ds(v, 1)]).then_inc(s_away, 1)
                    act.wait_ge(s_part, v * UN + UN)
                    act.wait_ge(s_away, v + 1)
                    nc.scalar.activation(spread[:, s].rearrange("p k e -> p (k e)"), away[:], ACT.Relu, scale=-1.0, bias=one[:]).then_inc(s_spread, 1)
                    nc.scalar.copy(fdc[s][0][:], blk(R.fd, b).bitcast(F32))
                    nc.scalar.copy(fdc[s][1][:], blk(R.fdl, b).bitcast(F32)).then_inc(s_rows, 1)
                    act.wait_ge(s_sum, v + 1)
                    nc.scalar.activation(inside[:, s, :], R.dst_block[:, ds(grp * UN, UN)], ACT.Abs, bias=R.visit_minus[:, ds(v, 1)]).then_inc(s_inside, 1)
                    act.wait_ge(s_inside, v * 2 + 1)
                    nc.scalar.activation(inside[:, s, :], inside[:, s, :], ACT.Relu, scale=-1.0, bias=one[:]).then_inc(s_inside, 1)

        @block.gpsimd
        def _(pool):
            nc.gpsimd.memset(R.L[:, 0:heads, :], 0.0).then_inc(s_sum, 2)

            def gather(v, s):
                grp = pool.value_load(R.visit_group[0:1, ds(v, 1)], min_val=0, max_val=GROUPS - 1)
                pool.wait_ge(s_part, v * UN + UN)
                nc.gpsimd.tensor_copy(lists[:, s, :], R.src[:, ds(grp * UN, UN)]).then_inc(s_list, 1)
                for k in range(UN):
                    pool.wait_ge(s_part, v * UN + k + 1)
                    pool.wait_ge(s_list, v + 1)
                    pool.nop(nofuse=True)
                    nc.gpsimd.indirect_dma_start(
                        out=g[:, s, k, :], out_offset=None, in_=fs,
                        in_offset=bass.IndirectOffsetOnAxis(ap=lists[:, s, k:k + 1], axis=0)).then_inc(s_g[s][k], 16)

            def add(v, s):
                grp = pool.value_load(R.visit_group[0:1, ds(v, 1)], min_val=0, max_val=GROUPS - 1)
                pool.wait_ge(s_part, v * UN + 3 * UN)
                n = 2 if heads == 1 else 1
                if heads == 1:
                    nc.gpsimd.tensor_tensor(part[:, s, :, 0:1], part[:, s, :, 0:1], part[:, s, :, 1:2], ALU.add).then_inc(s_tail, 1)
                    pool.wait_ge(s_tail, v * n + 1)
                pool.wait_ge(s_inside, v * 2 + 2)
                pt = part[:, s, :, 0:heads]
                nc.gpsimd.tensor_tensor(pt, pt, bcast(inside[:, s, :], 2, heads), ALU.mult).then_inc(s_tail, 1)
                pool.wait_ge(s_tail, v * n + n)
                pool.wait_ge(s_sum, v + 2)
                sums = R.L[:, 0:heads, ds(grp * UN, UN)]
                nc.gpsimd.tensor_tensor(sums, sums, pt.rearrange("p k h -> p h k"), ALU.add).then_inc(s_sum, 1)

            gather(0, 0)
            with pool.Fori(0, VISITS // 2 - 1) as i:
                gather(i * 2 + 1, 1)
                add(i * 2, 0)
                gather(i * 2 + 2, 0)
                add(i * 2 + 1, 1)
            gather(VISITS - 1, 1)
            add(VISITS - 2, 0)
            add(VISITS - 1, 1)
            pool.wait_ge(s_sum, VISITS + 2)

        @block.vector
        def _(dve):
            chain = Chain(dve, s_v)
            dve.sem_inc(s_part, 2 * UN)
            chain(nc.vector.memset(one[:], 1.0))
            chain(nc.vector.memset(at[:], 0.0))
            dve.sem_inc(s_one, 1)
            dve.wait_ge(s_at, 16)
            ah = at[:].rearrange("p (h e) -> p h e", h=heads)
            nc.vector.memset(ah[:, :, hd + 1:hd + 2], 1.0)
            nc.vector.memset(ah[:, :, hd + 2:hd + 3], -1.0)
            chain(nc.vector.tensor_scalar(ah[:, :, 0:hd], ah[:, :, 0:hd], 0.8, None, ALU.mult))
            with dve.Fori(0, VISITS // 2) as i:
                for s in range(2):
                    v = i * 2 + s
                    dve.wait_ge(s_sum, v + 1)
                    for k in range(UN):
                        n, j = v * UN + k, k % 2
                        dve.wait_ge(s_mm, n + 1)
                        nc.vector.tensor_tensor(z[:, j, :], psZ[k][:, 1, by_pe - half:half], g[:, s, k, by_pe:width], ALU.add).then_inc(s_z, 1)
                        waited = False
                        for m, (lo, hi) in enumerate(parts):
                            own = lo >= by_pe
                            if own and not waited:
                                dve.wait_ge(s_z, n + 1)
                                waited = True
                            src = z[:, j, lo - by_pe:hi - by_pe] if own else psZ[k][:, lo // half, lo % half:lo % half + hi - lo]
                            last = nc.vector.scalar_tensor_tensor(out=zr[:, j, lo:hi], in0=src, scalar=0.0, in1=at[:, lo:hi], op0=ALU.max, op1=ALU.mult,
                                                                  accum_out=part[:, s, k, m:m + 1])
                        last.then_inc(s_part, 1)

        @block.tensor
        def _(pe):
            with pe.Fori(0, VISITS // 2) as i:
                for s in range(2):
                    v = i * 2 + s
                    pe.wait_ge(s_spread, v + 3)
                    pe.wait_ge(s_rows, v + 1)
                    for k in range(UN):
                        pe.wait_ge(s_part, v * UN + k + UN + 1)
                        for a, (lo, hi) in enumerate(cuts):
                            for t in range(2):
                                nc.tensor.matmul(psZ[k][:, a, 0:half], spread[:, s, k, :], fdc[s][t][:, lo:hi], start=(t == 0), stop=(t == 1))
                        pe.wait_ge(s_g[s][k], i * 16 + 16)
                        for a, (lo, hi) in enumerate(added):
                            last = nc.tensor.matmul(psZ[k][:, a, 0:hi - lo], R.ident[:], g[:, s, k, lo:hi], start=False, stop=True, skip_group_check=True)
                        last.then_inc(s_mm, 1)


def edge_softmax(nc, R, name, heads):
    W = P + 2
    with Scope(nc, name) as c:
        S = c.sb("S", [QT, 4, heads, W])
        pen = c.sb("pen", [QT, 2, 4, heads, W])
        run = c.sb("run", [QT, 2, heads, W])
        sides = c.sb("sides", [QT, 4, 4, heads])
        rowsd = c.sb("rowsd", [heads, 4, TILES])
        a = c.sb("a", [heads, 6, TILES])
        seen = c.sb("seen", [heads, 2, TILES])
        carry = c.sb("carry", [heads, 2, TILES])
        psS = c.ps("psS", [P, 2, 4, P])
        psR = c.ps("psR", [heads, 4, BANK])
        psC = c.ps("psC", [P, BANK])
        s_v, s_turn, s_copied, s_side, s_rows, s_carry, s_back = (c.sem(x) for x in ("v", "turn", "copied", "side", "rows", "carry", "back"))
        s_exp, s_exped, s_ret, s_retd = c.sem("exp"), c.sem("exped"), c.sem("ret"), c.sem("retd")
        block = c.enter_context(nc.Block())

        @block.tensor
        def _(pe):
            for q in range(4):
                for h in range(heads):
                    n = q * heads + h
                    if n >= 8 and n % 4 == 0:
                        pe.wait_ge(s_copied, n // 4 - 1)
                    t = nc.tensor.transpose(psS[0:QT, n // 4 % 2, n % 4, :], R.L[:, h, q * QT:(q + 1) * QT], R.ident[:])
                    if n % 4 == 3:
                        t.then_inc(s_turn, 1)
            pe.wait_ge(s_side, 1)
            for j in range(4):
                for q in range(4):
                    last = nc.tensor.transpose(psR[:, j, q * QT:(q + 1) * QT], sides[:, q, j, :], R.ident[0:QT, 0:QT])
            last.then_inc(s_rows, 1)
            pe.wait_ge(s_carry, 1)
            for j in range(2):
                for q in range(4):
                    last = nc.tensor.transpose(psC[0:QT, (j * 4 + q) * heads:(j * 4 + q + 1) * heads], carry[:, j, q * QT:(q + 1) * QT], R.ident[0:heads, 0:heads])
            last.then_inc(s_back, 1)
            for h in range(heads):
                if h == 0:
                    pe.wait_ge(s_exped, 4)
                if h >= 2:
                    pe.wait_ge(s_retd, h - 1)
                for q in range(4):
                    last = nc.tensor.transpose(psS[:, h % 2, :, :].rearrange("p a b -> p (a b)")[:, q * QT:(q + 1) * QT], S[:, q, h, 1:P + 1], R.ident[0:QT, 0:QT])
                last.then_inc(s_ret, 1)

        @block.scalar
        def _(act):
            for n in range(heads):
                act.wait_ge(s_turn, n + 1)
                for k in range(4):
                    m = n * 4 + k
                    last = nc.scalar.copy(S[:, m // heads, m % heads, 1:P + 1], psS[0:QT, n % 2, k, :])
                last.then_inc(s_copied, 1)
            for q in range(4):
                act.wait_ge(s_exp, q + 1)
                nc.scalar.activation(S[:, q, :, 1:P + 1], S[:, q, :, 1:P + 1], ACT.Exp).then_inc(s_exped, 1)
            for h in range(heads):
                act.wait_ge(s_ret, h + 1)
                nc.scalar.copy(R.L[:, h, :], psS[:, h % 2, :, :].rearrange("p a b -> p (a b)")[:, 0:TILES]).then_inc(s_retd, 1)

        @block.vector
        def _(dve):
            chain = Chain(dve, s_v)
            flat = "p h w -> p (h w)"

            def scans():
                for q in range(4):
                    yield q
                    chain(nc.vector.tensor_tensor_scan(run[:, 0].rearrange(flat), pen[:, 0, q].rearrange(flat), S[:, q].rearrange(flat), NEG, ALU.add, ALU.max))
                    chain(nc.vector.tensor_tensor_scan(run[:, 1].rearrange(flat)[:, ::-1], pen[:, 1, q].rearrange(flat)[:, ::-1], S[:, q].rearrange(flat)[:, ::-1], NEG, ALU.add, ALU.max))
                    yield q

            chain(nc.vector.memset(pen[:], 0.0))
            for q in range(4):
                same = run[:, 0, 0, 0:P - 1]
                e = R.ends[:, 0, q]
                chain(nc.vector.tensor_tensor(same, e[:, 2:P + 1], e[:, 1:P], ALU.not_equal))
                chain(nc.vector.tensor_scalar(same, same, NEG, None, ALU.mult))
                nc.vector.tensor_copy(pen[:, 0, q, :, 2:P + 1], bcast(same, 1, heads))
                chain(nc.vector.tensor_copy(pen[:, 1, q, :, 1:P], bcast(same, 1, heads)))
            nc.vector.memset(pen[:, 0, :, :, 0:1], NEG)
            chain(nc.vector.memset(pen[:, 1, :, :, P + 1:W], NEG))
            nc.vector.memset(S[:, :, :, 0:1], NEG)
            chain(nc.vector.memset(S[:, :, :, P + 1:W], NEG))
            for q in range(4):
                nc.vector.tensor_copy(sides[:, q, 2, :], R.ends[:, 0, q, 1:2].broadcast_to([QT, heads]))
                chain(nc.vector.tensor_copy(sides[:, q, 3, :], R.ends[:, 0, q, P:P + 1].broadcast_to([QT, heads])))
            dve.wait_ge(s_copied, heads)
            it = scans()
            for q in it:
                next(it)
                nc.vector.tensor_copy(sides[:, q, 0, :], run[:, 0, :, P:P + 1].squeeze(2))
                chain(nc.vector.tensor_copy(sides[:, q, 1, :], run[:, 1, :, 1:2].squeeze(2)))
            dve.sem_inc(s_side, 1)
            dve.wait_ge(s_rows, 1)
            chain(nc.vector.tensor_copy(rowsd[:], psR[:, :, 0:TILES]))
            last, first, dfirst, dlast = (rowsd[:, j, :] for j in range(4))
            whole, cont, nocont = a[:, 0, :], a[:, 1, :], a[:, 2, :]
            T1 = TILES - 1
            nc.vector.tensor_tensor(whole, dfirst, dlast, ALU.is_equal)
            nc.vector.tensor_tensor(cont[:, 0:T1], dfirst[:, 1:TILES], dlast[:, 0:T1], ALU.is_equal)
            chain(nc.vector.memset(cont[:, T1:TILES], 0.0))
            chain(nc.vector.tensor_scalar(nocont[:, 0:T1], cont[:, 0:T1], -NEG, NEG, ALU.mult, ALU.add))
            nc.vector.tensor_tensor(a[:, 3, 1:TILES], whole[:, 1:TILES], cont[:, 0:T1], ALU.mult)
            nc.vector.tensor_tensor(a[:, 4, 0:TILES], whole, cont, ALU.mult)
            chain(nc.vector.memset(a[:, 3, 0:1], 0.0))
            chain(nc.vector.tensor_scalar(a[:, 3:5, :], a[:, 3:5, :], -NEG, NEG, ALU.mult, ALU.add))
            nc.vector.tensor_tensor_scan(seen[:, 0, :], a[:, 3, :], last, NEG, ALU.add, ALU.max)
            chain(nc.vector.tensor_tensor_scan(seen[:, 1, ::-1], a[:, 4, ::-1], first[:, ::-1], NEG, ALU.add, ALU.max))
            nc.vector.memset(carry[:, 0, 0:1], NEG)
            chain(nc.vector.memset(carry[:, 1, T1:TILES], NEG))
            nc.vector.tensor_tensor(carry[:, 0, 1:TILES], seen[:, 0, 0:T1], a[:, 2, 0:T1], ALU.add)
            chain(nc.vector.tensor_tensor(carry[:, 1, 0:T1], seen[:, 1, 1:TILES], a[:, 2, 0:T1], ALU.add))
            dve.sem_inc(s_carry, 1)
            dve.wait_ge(s_back, 1)
            back = psC[0:QT, 0:8 * heads].rearrange("p (j q h) -> p j q h", j=2, q=4)
            nc.vector.tensor_copy(S[:, :, :, 0:1], back[:, 0].unsqueeze(3))
            chain(nc.vector.tensor_copy(S[:, :, :, P + 1:W], back[:, 1].unsqueeze(3)))
            it = scans()
            for q in it:
                next(it)
                chain(nc.vector.tensor_tensor(run[:, 0], run[:, 0], run[:, 1], ALU.max))
                chain(nc.vector.tensor_tensor(S[:, q, :, 1:P + 1], S[:, q, :, 1:P + 1], run[:, 0, :, 1:P + 1], ALU.subtract))
                dve.sem_inc(s_exp, 1)


def aggregate(nc, R, name, table, width, heads=0, count=False):
    cols = width + bool(count)
    cuts = [(0, width // 2), (width // 2, cols)]
    he = width // heads
    with Scope(nc, name) as c:
        lists = c.sb("list", [P, 2, UN], I32)
        g = c.sb("g", [P, 2, UN, cols])
        sel = c.sb("sel", [P, 2, UN, P])
        psO = [c.ps(f"psO{s}", [P, 2, BANK]) for s in range(2)]
        s_v, s_list, s_zero = c.sem("v"), c.sem("list"), c.sem("zero")
        s_g = [[c.sem(f"g{s}{k}") for k in range(UN)] for s in range(2)]
        s_w = [[c.sem(f"w{s}{k}") for k in range(UN)] for s in range(2)]
        s_mm = [[c.sem(f"mm{s}{k}") for k in range(UN)] for s in range(2)]
        s_sel, s_add = c.sem("sel"), c.sem("add")
        block = c.enter_context(nc.Block())

        @block.gpsimd
        def _(pool):
            pool.wait_ge(s_zero, 1)
            with pool.Fori(0, VISITS // 2) as i:
                for s in range(2):
                    v = i * 2 + s
                    grp = pool.value_load(R.visit_group[0:1, ds(v, 1)], min_val=0, max_val=GROUPS - 1)
                    pool.wait_ge(s_mm[s][UN - 1], i + 1)
                    nc.gpsimd.tensor_copy(lists[:, s, :], R.src[:, ds(grp * UN, UN)]).then_inc(s_list, 1)
                    for k in range(UN):
                        pool.wait_ge(s_mm[s][k], i + 1)
                        pool.wait_ge(s_list, v + 1)
                        pool.nop(nofuse=True)
                        nc.gpsimd.indirect_dma_start(
                            out=g[:, s, k, 0:width], out_offset=None, in_=table,
                            in_offset=bass.IndirectOffsetOnAxis(ap=lists[:, s, k:k + 1], axis=0)).then_inc(s_g[s][k], 16)

        @block.vector
        def _(dve):
            chain = Chain(dve, s_v)
            chain(nc.vector.memset(R.acc[:], 0.0))
            if count:
                chain(nc.vector.memset(g[:, :, :, width:cols], 1.0))
            for s in range(2):
                for k in range(UN):
                    dve.sem_inc(s_mm[s][k], 1)
            dve.sem_inc(s_zero, 1)
            dve.sem_inc(s_add, 4)

            def make(i, s):
                v = i * 2 + s
                grp = dve.value_load(R.visit_group[0:1, ds(v, 1)], min_val=0, max_val=GROUPS - 1)
                blk = dve.value_load(R.visit_block[0:1, ds(v, 1)], min_val=0, max_val=NB - 1)
                dve.wait_ge(s_mm[s][UN - 1], i + 1)
                nc.vector.tensor_tensor(sel[:, s], bcast(R.nodes[:, ds(blk * P, P)], 1, UN), bcast(R.dst[:, ds(grp * UN, UN)], 2, P), ALU.is_equal).then_inc(s_sel, 1)
                if heads == 1:
                    dve.wait_ge(s_sel, v * 2 + 1)
                    nc.vector.tensor_tensor(sel[:, s], sel[:, s], bcast(R.L[:, 0, ds(grp * UN, UN)], 2, P), ALU.mult).then_inc(s_sel, 1)
                if heads > 1:
                    for k in range(UN):
                        dve.wait_ge(s_g[s][k], i * 16 + 16)
                        rows = g[:, s, k, 0:width].rearrange("p (h e) -> p h e", h=heads)
                        nc.vector.tensor_tensor(rows, rows, R.L[:, :, ds(grp * UN + k, 1)].broadcast_to([P, heads, he]), ALU.mult).then_inc(s_w[s][k], 1)

            def add(i, s):
                v = i * 2 + s
                blk = dve.value_load(R.visit_block[0:1, ds(v, 1)], min_val=0, max_val=NB - 1)
                dve.wait_ge(s_add, v * 2 + 4)
                dve.wait_ge(s_mm[s][UN - 1], i + 2)
                for a, (lo, hi) in enumerate(cuts):
                    acc = R.acc[:, ds(blk, 1), lo:hi].squeeze(1)
                    nc.vector.tensor_tensor(acc, acc, psO[s][:, a, 0:hi - lo], ALU.add).then_inc(s_add, 1)

            make(0, 0)
            with dve.Fori(0, VISITS // 2 - 1) as i:
                make(i, 1)
                add(i, 0)
                make(i + 1, 0)
                add(i, 1)
            last = VISITS // 2 - 1
            make(last, 1)
            add(last, 0)
            add(last, 1)

        @block.tensor
        def _(pe):
            with pe.Fori(0, VISITS // 2) as i:
                for s in range(2):
                    v = i * 2 + s
                    pe.wait_ge(s_add, v * 2 + 2)
                    pe.wait_ge(s_sel, (v + 1) * (2 if heads == 1 else 1))
                    for k in range(UN):
                        if heads > 1:
                            pe.wait_ge(s_w[s][k], i + 1)
                        else:
                            pe.wait_ge(s_g[s][k], i * 16 + 16)
                        for a, (lo, hi) in enumerate(cuts):
                            last = nc.tensor.matmul(psO[s][:, a, 0:hi - lo], sel[:, s, k, :], g[:, s, k, lo:hi], start=(k == 0), stop=(k == UN - 1))
                        last.then_inc(s_mm[s][k], 1)


def finish_gat(nc, R, name, heads, weight, bias, first):
    hd, he = D // heads, head_width(heads)
    with Scope(nc, name) as c:
        W = Roots(c)
        wt, bs = c.sb("weight", [P, D]), c.sb("bias", [P, D])
        den = c.sb("den", [P, 2, heads, 1])
        v, e = c.sb("values", [P, 2, D]), c.sb("e", [P, 2, D])
        s_w, s_v, s_low, s_exp = c.sem("weights"), c.sem("v"), c.sem("low"), c.sem("exp")
        block = c.enter_context(nc.Block())

        @block.sync
        def _(sp):
            sp.dma_start(wt[:], weight.partition_broadcast(P)).then_inc(s_w, 16)
            sp.dma_start(bs[:], bias.partition_broadcast(P)).then_inc(s_w, 16)

        @block.scalar
        def _(act):
            with act.Fori(0, NB // 2) as i:
                for s in range(2):
                    act.wait_ge(s_low, i * 2 + s + 1)
                    nc.scalar.activation(e[:, s, :], e[:, s, :], ACT.Exp).then_inc(s_exp, 1)
            if first:
                square_roots(nc, act, W, W.val, W.root)
            square_roots(nc, act, W, W.val, W.root)

        @block.vector
        def _(dve):
            chain = Chain(dve, s_v)

            def low(i, s):
                acc = blk(R.acc, i * 2 + s)[:, 0:heads * he].rearrange("p (h e) -> p h e", h=heads)
                chain(nc.vector.tensor_scalar(den[:, s], acc[:, :, hd:hd + 1], 1e-30, None, ALU.max))
                chain(nc.vector.reciprocal(den[:, s], den[:, s]))
                chain(nc.vector.tensor_tensor(v[:, s, :].rearrange("p (h e) -> p h e", h=heads), acc[:, :, 0:hd], den[:, s].broadcast_to([P, heads, hd]), ALU.mult))
                nc.vector.tensor_scalar(e[:, s, :], v[:, s, :], 0.0, None, ALU.min).then_inc(s_low, 1)

            def high(i, s):
                b = i * 2 + s
                dve.wait_ge(s_exp, b + 1)
                chain(nc.vector.scalar_tensor_tensor(out=v[:, s, :], in0=v[:, s, :], scalar=0.0, in1=e[:, s, :], op0=ALU.max, op1=ALU.add))
                y = blk(R.acc, b)[:, 0:D]
                if first:
                    chain(nc.vector.scalar_tensor_tensor(out=y, in0=v[:, s, :], scalar=-1.0, in1=blk(R.H, b), op0=ALU.add, op1=ALU.add))
                else:
                    chain(nc.vector.tensor_scalar(y, v[:, s, :], -1.0, None, ALU.add))

            if first:
                chain(nc.vector.tensor_scalar(W.val[:], R.acc[:, :, heads * he:heads * he + 1].squeeze(2), 1.0, None, ALU.add))
            low(0, 0)
            with dve.Fori(0, NB // 2 - 1) as i:
                chain.loop(i, 10)
                low(i, 1)
                high(i, 0)
                low(i + 1, 0)
                high(i, 1)
            chain.end(NB // 2 - 1)
            low(NB // 2 - 1, 1)
            high(NB // 2 - 1, 0)
            high(NB // 2 - 1, 1)
            if first:
                inverse_roots(nc, dve, chain, W, W.val, W.root, R.dinv)
            dve.wait_ge(s_w, 32)
            layer_norms(nc, dve, chain, R.H, R.acc, W, wt[:], bs[:])
            if not first:
                with dve.Fori(0, NB) as b:
                    nc.vector.tensor_tensor(blk(R.X, b), blk(R.X, b), blk(R.H, b), ALU.add)


EXPERTS, SLOTS, HID = 32, 32, 192
SE = EXPERTS * SLOTS
KS = SE // P
HC = HID // 2


def soft_logits(nc, R, name, phi, scale, disp, comb, ph):
    with Scope(nc, name) as c:
        sq = c.sb("sq", [P, 2, SE])
        f = c.sb("f", [P, 2, SE])
        ones, sc = c.sb("ones", [P, P]), c.sb("scale", [P, 1])
        rows = [c.sb(f"rows{s}", [P, D]) for s in range(2)]
        rowsT = [c.sb(f"rowsT{s}", [P, KD, P]) for s in range(2)]
        gm, rm, gs, rs = c.sb("gm", [P, 2, EXPERTS, 1]), c.sb("rm", [P, 2]), c.sb("gs", [P, 2, EXPERTS, 1]), c.sb("rs", [P, 2])
        psT = [c.ps(f"psT{s}", [P, 2, BANK]) for s in range(2)]
        psO = [c.ps(f"psO{s}", [P, 2, BANK]) for s in range(2)]
        s_w, s_v, s_sq, s_n, s_clip, s_root, s_phi = (c.sem(x) for x in ("weights", "v", "sq", "n", "clip", "root", "phi"))
        s_rows, s_turn, s_turned, s_mm, s_exp, s_sub = (c.sem(x) for x in ("rows", "turn", "turned", "mm", "exp", "sub"))
        block = c.enter_context(nc.Block())

        @block.sync
        def _(sp):
            sp.dma_start(ph[:], phi.rearrange("(k p) e s -> p k (e s)", p=P)).then_inc(s_w, 16)
            sp.dma_start(sc[:], scale.partition_broadcast(P)).then_inc(s_w, 16)

        @block.vector
        def _(dve):
            chain = Chain(dve, s_v)
            chain(nc.vector.memset(ones[:], 1.0))
            dve.wait_ge(s_w, 32)
            for k in range(KD):
                if k >= 2:
                    dve.wait_ge(s_n, k - 1)
                nc.vector.tensor_tensor(sq[:, k % 2, :], ph[:, k, :], ph[:, k, :], ALU.mult).then_inc(s_sq, 1)
            dve.wait_ge(s_n, KD)
            n2, r = f[:, 0, :], f[:, 1, :]
            chain(nc.vector.tensor_scalar(n2.rearrange("p (a b) -> p a b", a=2), psO[0][:], 1e-24, None, ALU.max))
            dve.sem_inc(s_clip, 1)
            dve.wait_ge(s_root, 1)
            chain(nc.vector.reciprocal(r, sq[:, 0, :]))
            chain(nc.vector.tensor_tensor(sq[:, 1, :], r, r, ALU.mult))
            chain(nc.vector.tensor_tensor(sq[:, 1, :], sq[:, 1, :], n2, ALU.mult))
            chain(nc.vector.tensor_scalar(sq[:, 1, :], sq[:, 1, :], -0.5, 1.5, ALU.mult, ALU.add))
            chain(nc.vector.tensor_tensor(r, r, sq[:, 1, :], ALU.mult))
            chain(nc.vector.tensor_scalar(r, r, sc[:], None, ALU.mult))
            for k in range(KD):
                nc.vector.tensor_tensor(ph[:, k, :], ph[:, k, :], r, ALU.mult).then_inc(s_phi, 1)
            dve.sem_inc(s_turn, 2)
            dve.sem_inc(s_mm, 2)
            ge = "p (e s) -> p e s"

            def turn(i, s):
                b = i * 2 + s
                dve.wait_ge(s_turn, b + 1)
                nc.vector.tensor_copy(rows[s][:], blk(R.H, b)).then_inc(s_rows, 1)
                dve.wait_ge(s_turn, b + 3)
                dve.wait_ge(s_mm, b + 1)
                nc.vector.tensor_copy(rowsT[s][:].rearrange("p (a k) q -> p a (k q)", a=2), psT[s][:, :, 0:HALF]).then_inc(s_turned, 1)

            def weigh(i, s):
                b = i * 2 + s
                dve.wait_ge(s_mm, b + 3)
                lg = psO[s][:].rearrange("p a (e s) -> p (a e) s", s=SLOTS)
                dsp = blk(disp, b).rearrange(ge, e=EXPERTS)
                chain(nc.vector.tensor_reduce(gm[:, s], lg, AX.X, ALU.max))
                chain(nc.vector.tensor_reduce(rm[:, s:s + 1], gm[:, s].squeeze(2), AX.X, ALU.max))
                chain(nc.vector.tensor_scalar(rm[:, s:s + 1], rm[:, s:s + 1], -1.0, None, ALU.mult))
                nc.vector.tensor_tensor(dsp, lg, gm[:, s].broadcast_to([P, EXPERTS, SLOTS]), ALU.subtract).then_inc(s_sub, 1)
                dve.wait_ge(s_exp, b * 2 + 2)
                dve.nop(nofuse=True)
                chain(nc.vector.tensor_reduce(gs[:, s], dsp, AX.X, ALU.add))
                chain(nc.vector.reciprocal(gs[:, s], gs[:, s]))
                nc.vector.tensor_tensor(dsp, dsp, gs[:, s].broadcast_to([P, EXPERTS, SLOTS]), ALU.mult)
                chain(nc.vector.reciprocal(rs[:, s:s + 1], rs[:, s:s + 1]))
                chain(nc.vector.tensor_scalar(blk(comb, b), blk(comb, b), rs[:, s:s + 1], None, ALU.mult))

            turn(0, 0)
            with dve.Fori(0, NB // 2 - 1) as i:
                chain.loop(i, 14)
                turn(i, 1)
                weigh(i, 0)
                turn(i + 1, 0)
                weigh(i, 1)
            chain.end(NB // 2 - 1)
            turn(NB // 2 - 1, 1)
            weigh(NB // 2 - 1, 0)
            weigh(NB // 2 - 1, 1)

        @block.scalar
        def _(act):
            act.wait_ge(s_clip, 1)
            nc.scalar.activation(sq[:, 0, :], f[:, 0, :], ACT.Sqrt).then_inc(s_root, 1)
            with act.Fori(0, NB // 2) as i:
                for s in range(2):
                    b = i * 2 + s
                    act.wait_ge(s_sub, b + 1)
                    nc.scalar.activation(blk(comb, b).rearrange("p (a e) -> p a e", a=2), psO[s][:], ACT.Exp,
                                         bias=rm[:, s:s + 1], accum_out=rs[:, s:s + 1]).then_inc(s_exp, 1)
                    nc.scalar.activation(blk(disp, b), blk(disp, b), ACT.Exp).then_inc(s_exp, 1)

        @block.tensor
        def _(pe):
            for k in range(KD):
                pe.wait_ge(s_sq, k + 1)
                for a in range(2):
                    last = nc.tensor.matmul(psO[0][:, a, :], ones[:], sq[:, k % 2, a * BANK:(a + 1) * BANK], start=(k == 0), stop=(k == KD - 1))
                last.then_inc(s_n, 1)
            pe.wait_ge(s_phi, KD)
            with pe.Fori(0, NB // 2) as i:
                for s in range(2):
                    b = i * 2 + s
                    pe.wait_ge(s_rows, b + 1)
                    for k in range(KD):
                        last = nc.tensor.transpose(psT[s][:, k // 3, (k % 3) * P:(k % 3 + 1) * P], rows[s][:, k * P:(k + 1) * P], R.ident[:])
                    last.then_inc(s_turn, 1)
                    pe.wait_ge(s_turned, b + 1)
                    for a in range(2):
                        for k in range(KD):
                            last = nc.tensor.matmul(psO[s][:, a, :], rowsT[s][:, k, :], ph[:, k, a * BANK:(a + 1) * BANK], start=(k == 0), stop=(k == KD - 1))
                    last.then_inc(s_mm, 1)


def soft_slots(nc, R, name, disp, slotsT):
    with Scope(nc, name) as c:
        ps = [c.ps(f"ps{j}", [P, BANK]) for j in range(4)]
        s_mm, s_copy = c.sem("mm"), c.sem("copy")
        block = c.enter_context(nc.Block())

        @block.tensor
        def _(pe):
            for n in range(2 * KD):
                k, a = n // 2, n % 2
                if n >= 4:
                    pe.wait_ge(s_copy, n - 3)
                for b in range(NB):
                    m = P if b < NB - 1 else LAST
                    last = nc.tensor.matmul(ps[n % 4][:], R.H[0:m, b, k * P:(k + 1) * P], disp[0:m, b, a * BANK:(a + 1) * BANK], start=(b == 0), stop=(b == NB - 1))
                last.then_inc(s_mm, 1)

        @block.scalar
        def _(act):
            for n in range(2 * KD):
                act.wait_ge(s_mm, n + 1)
                nc.scalar.copy(slotsT[:, n // 2, n % 2 * BANK:(n % 2 + 1) * BANK], ps[n % 4][:]).then_inc(s_copy, 1)


def soft_experts(nc, R, name, w1, b1, w2, b2, slotsT, eo):
    with Scope(nc, name) as c:
        w1t = [c.sb(f"w1{s}", [P, 2, KD, HID]) for s in range(2)]
        w2t = [c.sb(f"w2{s}", [HC, 2, 2, D]) for s in range(2)]
        b1r, b1t = c.sb("b1r", [EXPERTS, HID]), c.sb("b1t", [HC, 2, EXPERTS])
        b2t = c.sb("b2t", [P, EXPERTS // 4, D])
        hT = c.sb("hT", [HC, 4, 2, SLOTS])
        psB = c.ps("psB", [HC, 2, EXPERTS])
        psH = [c.ps(f"psH{j}", [HC, 2, SLOTS]) for j in range(2)]
        psE = [c.ps(f"psE{j}", [P, 2, BANK]) for j in range(2)]
        s_b, s_bt, s_bc, s_h, s_gelu, s_e, s_out = (c.sem(x) for x in ("b", "bt", "bc", "h", "gelu", "e", "out"))
        s_w1, s_w2, s_free = ([c.sem(f"{x}{s}") for s in range(2)] for x in ("w1", "w2", "free"))
        G = EXPERTS // 4
        block = c.enter_context(nc.Block())

        @block.sync
        def _(sp):
            sp.dma_start(b1r[:], b1).then_inc(s_b, 16)
            with sp.Fori(0, G) as g:
                for s in range(2):
                    sp.wait_ge(s_free[s], g + 1)
                    for j in range(2):
                        e = g * 4 + 2 * s + j
                        sp.dma_start(w1t[s][:, j], w1[ds(e, 1)].squeeze(0).rearrange("(k p) h -> p k h", p=P)).then_inc(s_w1[s], 16)
                        sp.dma_start(w2t[s][:, j], w2[ds(e, 1)].squeeze(0).rearrange("(m p) d -> p m d", p=HC)).then_inc(s_w2[s], 16)

        @block.scalar
        def _(act):
            for j in range(4):
                act.dma_start(b2t[32 * j:32 * j + 32], b2.rearrange("(g j) d -> j g d", j=4)[j].partition_broadcast(32)).then_inc(s_b, 16)
            act.wait_ge(s_bt, 1)
            nc.scalar.copy(b1t[:], psB[:]).then_inc(s_bc, 1)
            act.wait_ge(s_bc, 1)
            with act.Fori(0, G) as g:
                for j in range(4):
                    act.wait_ge(s_h, g * 4 + j + 1)
                    if j == 0:
                        act.wait_ge(s_e, g + 1)
                    for m in range(2):
                        last = nc.scalar.activation(hT[:, j, m, :], psH[j % 2][:, m, :], ACT.Gelu, bias=b1t[:, m, ds(g * 4 + j, 1)])
                    last.then_inc(s_gelu, 1)

        @block.vector
        def _(dve):
            for s in range(2):
                dve.sem_inc(s_free[s], 1)
            dve.sem_inc(s_e, 1)
            dve.sem_inc(s_out, 2)
            dve.wait_ge(s_b, 80)
            with dve.Fori(0, G // 2) as i:
                for s in range(2):
                    g = i * 2 + s
                    dve.wait_ge(s_e, g + 2)
                    nc.vector.tensor_tensor(blk(eo, g).rearrange("p (a d) -> p a d", a=2), psE[s][:, :, 0:HALF],
                                            blk(b2t, g).rearrange("p (a d) -> p a d", a=2), ALU.add).then_inc(s_out, 1)

        @block.tensor
        def _(pe):
            pe.wait_ge(s_b, 80)
            for m in range(2):
                last = nc.tensor.transpose(psB[:, m, :], b1r[:, m * HC:(m + 1) * HC], R.ident[0:EXPERTS, 0:EXPERTS])
            last.then_inc(s_bt, 1)
            with pe.Fori(0, G // 2) as i:
                for t in range(2):
                    g = i * 2 + t

                    def hidden(j):
                        if j % 2 == 0:
                            pe.wait_ge(s_w1[j // 2], g * 32 + 32)
                        for m in range(2):
                            for k in range(KD):
                                last = nc.tensor.matmul(psH[j % 2][:, m, :], w1t[j // 2][:, j % 2, k, m * HC:(m + 1) * HC],
                                                        slotsT[:, k, ds(g * P + j * SLOTS, SLOTS)], start=(k == 0), stop=(k == KD - 1))
                        last.then_inc(s_h, 1)

                    def outer(j):
                        if j == 0:
                            pe.wait_ge(s_out, g + 1)
                        if j % 2 == 0:
                            pe.wait_ge(s_w2[j // 2], g * 32 + 32)
                        pe.wait_ge(s_gelu, g * 4 + j + 1)
                        for a in range(2):
                            for m in range(2):
                                last = nc.tensor.matmul(psE[t][32 * j:32 * j + 32, a, 0:HALF], hT[:, j, m, :], w2t[j // 2][:, j % 2, m, a * HALF:(a + 1) * HALF],
                                                        start=(m == 0), stop=(m == 1))
                        if j % 2:
                            last.then_inc(s_free[j // 2], 1)

                    hidden(0)
                    hidden(1)
                    outer(0)
                    hidden(2)
                    outer(1)
                    hidden(3)
                    outer(2)
                    outer(3)
                    pe.wait_ge(s_free[1], g + 2)
                    pe.sem_inc(s_e, 1)


def soft_combine(nc, R, name, comb, eo):
    with Scope(nc, name) as c:
        rows = [c.sb(f"rows{s}", [P, SE]) for s in range(2)]
        rowsT = [c.sb(f"rowsT{s}", [P, KS, P]) for s in range(2)]
        psT = [c.ps(f"psT{s}", [P, 2, BANK]) for s in range(2)]
        psO = [c.ps(f"psO{s}", [P, 2, BANK]) for s in range(2)]
        s_rows, s_turn, s_turned, s_mm, s_add = (c.sem(x) for x in ("rows", "turn", "turned", "mm", "add"))
        block = c.enter_context(nc.Block())

        @block.scalar
        def _(act):
            act.sem_inc(s_turn, 2)
            act.sem_inc(s_mm, 2)
            with act.Fori(0, NB // 2) as i:
                for s in range(2):
                    b = i * 2 + s
                    act.wait_ge(s_turn, b + 1)
                    nc.scalar.copy(rows[s][:], blk(comb, b)).then_inc(s_rows, 1)
                    act.wait_ge(s_turn, b + 3)
                    act.wait_ge(s_mm, b + 1)
                    nc.scalar.copy(rowsT[s][:].rearrange("p (a k) q -> p a (k q)", a=2), psT[s][:]).then_inc(s_turned, 1)

        @block.vector
        def _(dve):
            dve.sem_inc(s_add, 2)
            with dve.Fori(0, NB // 2) as i:
                for s in range(2):
                    b = i * 2 + s
                    dve.wait_ge(s_mm, b + 3)
                    x = blk(R.X, b).rearrange("p (a d) -> p a d", a=2)
                    nc.vector.tensor_tensor(x, x, psO[s][:, :, 0:HALF], ALU.add).then_inc(s_add, 1)

        @block.tensor
        def _(pe):
            with pe.Fori(0, NB // 2) as i:
                for s in range(2):
                    b = i * 2 + s
                    pe.wait_ge(s_rows, b + 1)
                    for k in range(KS):
                        last = nc.tensor.transpose(psT[s][:, k // 4, (k % 4) * P:(k % 4 + 1) * P], rows[s][:, k * P:(k + 1) * P], R.ident[:])
                    last.then_inc(s_turn, 1)
                    pe.wait_ge(s_add, b + 1)
                    pe.wait_ge(s_turned, b + 1)
                    for a in range(2):
                        for k in range(KS):
                            last = nc.tensor.matmul(psO[s][:, a, 0:HALF], rowsT[s][:, k, :], eo[:, k, a * HALF:(a + 1) * HALF], start=(k == 0), stop=(k == KS - 1))
                    last.then_inc(s_mm, 1)


def edge_counts(nc, R, name):
    BY_ACT = 1
    with Scope(nc, name) as c:
        nodes = c.sb("nodes", [P, ROWS], F16)
        srcf, minus = c.sb("src", [P, TILES]), c.sb("minus", [P, TILES])
        one = c.sb("one", [P, 1])
        away = c.sb("away", [P, 2, ROWS], F16)
        pick = c.sb("pick", [P, 2, UN, ROWS], BF16)
        sel = c.sb("sel", [P, 2, UN, P], BF16)
        psC = [c.ps(f"psC{s}", [P, 3 * BANK]) for s in range(2)]
        s_v, s_zero, s_cast, s_sel, s_pick, s_mm, s_add = (c.sem(x) for x in ("v", "zero", "cast", "sel", "pick", "mm", "add"))
        s_minus, s_away = c.sem("minus"), c.sem("away")
        block = c.enter_context(nc.Block())

        @block.gpsimd
        def _(pool):
            nc.gpsimd.memset(R.CT[:], 0.0).then_inc(s_zero, 1)

        @block.scalar
        def _(act):
            act.wait_ge(s_cast, 1)
            nc.scalar.mul(minus[:], srcf[:], -1.0).then_inc(s_minus, 1)
            act.wait_ge(s_minus, 1)
            with act.Fori(0, VISITS // 2) as i:
                for s in range(2):
                    v = i * 2 + s
                    grp = act.value_load(R.visit_group[0:1, ds(v, 1)], min_val=0, max_val=GROUPS - 1)
                    act.wait_ge(s_mm, v + 1)
                    for k in range(UN - BY_ACT, UN):
                        nc.scalar.activation(away[:, s, :], nodes[:], ACT.Abs, bias=minus[:, ds(grp * UN + k, 1)]).then_inc(s_away, 1)
                        act.wait_ge(s_away, v * BY_ACT + k - UN + BY_ACT + 1)
                        last = nc.scalar.activation(pick[:, s, k, :], away[:, s, :], ACT.Relu, scale=-1.0, bias=one[:])
                    last.then_inc(s_pick, 1)

        @block.vector
        def _(dve):
            chain = Chain(dve, s_v)
            chain(nc.vector.memset(one[:], 1.0))
            chain(nc.vector.tensor_copy(nodes[:], R.nodes[:]))
            chain(nc.vector.tensor_copy(srcf[:], R.src[:]))
            dve.sem_inc(s_cast, 1)
            dve.sem_inc(s_mm, 2)
            dve.sem_inc(s_add, 2)

            def make(i, s):
                v = i * 2 + s
                grp = dve.value_load(R.visit_group[0:1, ds(v, 1)], min_val=0, max_val=GROUPS - 1)
                blk_ = dve.value_load(R.visit_block[0:1, ds(v, 1)], min_val=0, max_val=NB - 1)
                dve.wait_ge(s_mm, v + 1)
                nc.vector.tensor_tensor(sel[:, s], bcast(R.nodes[:, ds(blk_ * P, P)], 1, UN), bcast(R.dst[:, ds(grp * UN, UN)], 2, P), ALU.is_equal)
                for k in range(UN - BY_ACT):
                    last = nc.vector.tensor_scalar(pick[:, s, k, :], nodes[:], srcf[:, ds(grp * UN + k, 1)], None, ALU.is_equal)
                last.then_inc(s_sel, 1)

            def add(i, s):
                v = i * 2 + s
                blk_ = dve.value_load(R.visit_block[0:1, ds(v, 1)], min_val=0, max_val=NB - 1)
                dve.wait_ge(s_mm, v + 3)
                dve.wait_ge(s_add, v + 2)
                cols = R.CT[:, :, ds(blk_ * P, P)]
                nc.vector.tensor_tensor(cols, cols, psC[s][:, 0:ROWS].rearrange("p (c i) -> p c i", c=NB), ALU.add).then_inc(s_add, 1)

            make(0, 0)
            dve.wait_ge(s_zero, 1)
            with dve.Fori(0, VISITS // 2 - 1) as i:
                make(i, 1)
                add(i, 0)
                make(i + 1, 0)
                add(i, 1)
            make(VISITS // 2 - 1, 1)
            add(VISITS // 2 - 1, 0)
            add(VISITS // 2 - 1, 1)
            dve.wait_ge(s_add, VISITS + 2)
            for b in range(NB):
                own = R.CT[:, b, b * P:(b + 1) * P]
                nc.vector.tensor_tensor(own, own, R.ident[:], ALU.add)

        @block.tensor
        def _(pe):
            with pe.Fori(0, VISITS // 2) as i:
                for s in range(2):
                    v = i * 2 + s
                    pe.wait_ge(s_add, v + 1)
                    pe.wait_ge(s_sel, v + 1)
                    pe.wait_ge(s_pick, v + 1)
                    for b in range(NB):
                        for k in range(UN):
                            last = nc.tensor.matmul(psC[s][:, b * P:(b + 1) * P], pick[:, s, k, b * P:(b + 1) * P], sel[:, s, k, :],
                                                    start=(k == 0), stop=(k == UN - 1))
                    last.then_inc(s_mm, 1)


def gcn_layer(nc, R, name, rows, weight, bias, first):
    CH = 2 * P
    with Scope(nc, name) as c:
        w, bs = c.sb("w", [P, KD, D]), c.sb("bias", [P, D])
        sumT = [c.sb(f"sumT{s}", [P, KD, CH]) for s in range(2)]
        y = c.sb("y", [P, 2, HALF])
        psY = [c.ps(f"psY{s}", [P, KD // 2, BANK]) for s in range(2)]
        psO = c.ps("psO", [P, 2, BANK])
        s_w, s_b, s_rows, s_mix, s_copied, s_mm, s_taken, s_y = (c.sem(x) for x in ("weights", "bias", "rows", "mix", "copied", "mm", "taken", "y"))
        block = c.enter_context(nc.Block())

        @block.sync
        def _(sp):
            sp.dma_start(w[:], weight.rearrange("(k p) d -> p k d", p=P)).then_inc(s_w, 16)
            sp.dma_start(bs[:], bias.partition_broadcast(P)).then_inc(s_b, 16)

        @block.scalar
        def _(act):
            def copy(c_, s):
                act.wait_ge(s_mm, c_ * 4 + 4)
                for a in range(KD // 2):
                    act.wait_ge(s_mix, c_ * 3 + a + 1)
                    nc.scalar.copy(sumT[s][:, 2 * a:2 * a + 2, :].rearrange("p k i -> p (k i)"), psY[s][:, a, :]).then_inc(s_copied, 1)

            copy(0, 0)
            with act.Fori(0, NB // 4) as i:
                copy(i * 2 + 1, 1)
                copy(i * 2 + 2, 0)

        @block.vector
        def _(dve):
            dve.sem_inc(s_mm, 8)
            dve.sem_inc(s_copied, 6)
            dve.sem_inc(s_taken, 2)
            if first:
                for b in range(NB):
                    nc.vector.tensor_scalar(rows[:, b, :], rows[:, b, :], R.dinv[:, b:b + 1], None, ALU.mult).then_inc(s_rows, 1)
            dve.wait_ge(s_b, 16)
            with dve.Fori(0, NB) as b:
                for a in range(2):
                    cut = slice(a * HALF, (a + 1) * HALF)
                    dve.wait_ge(s_mm, b * 2 + a + 9)
                    nc.vector.scalar_tensor_tensor(out=y[:, a, :], in0=psO[:, a, 0:HALF], scalar=R.dinv[:, ds(b, 1)], in1=bs[:, cut],
                                                   op0=ALU.mult, op1=ALU.add).then_inc(s_taken, 1)
                    dve.wait_ge(s_taken, b * 2 + a + 3)
                    if first:
                        nc.vector.tensor_scalar(R.out[:, ds(b, 1), cut].squeeze(1), y[:, a, :], 0.0, R.dinv[:, ds(b, 1)], ALU.max, ALU.mult).then_inc(s_y, 1)
                    else:
                        xb = R.X[:, ds(b, 1), cut].squeeze(1)
                        nc.vector.tensor_tensor(xb, xb, y[:, a, :], ALU.add).then_inc(s_y, 1)
            dve.wait_ge(s_y, 2 * NB)

        @block.tensor
        def _(pe):
            def mix(c_, s, start=False):
                pe.wait_ge(s_copied, c_ * 3 + 3)
                for k in range(KD):
                    for b in range(NB):
                        if start and k == 0:
                            pe.wait_ge(s_rows, b + 1)
                        last = nc.tensor.matmul(psY[s][:, k // 2, (k % 2) * CH:(k % 2 + 1) * CH], rows[:, b, k * P:(k + 1) * P],
                                                R.CT[:, b, ds(c_ * CH, CH)], start=(b == 0), stop=(b == NB - 1))
                    if k % 2:
                        last.then_inc(s_mix, 1)

            def multiply(c_, s):
                pe.wait_ge(s_copied, c_ * 3 + 9)
                for q in range(2):
                    for a in range(2):
                        pe.wait_ge(s_taken, c_ * 4 + q * 2 + a + 1)
                        for k in range(KD):
                            last = nc.tensor.matmul(psO[:, a, 0:HALF], sumT[s][:, k, q * P:(q + 1) * P], w[:, k, a * HALF:(a + 1) * HALF],
                                                    start=(k == 0), stop=(k == KD - 1))
                        last.then_inc(s_mm, 1)

            mix(0, 0, first)
            pe.wait_ge(s_w, 16)
            with pe.Fori(0, NB // 4) as i:
                mix(i * 2 + 1, 1)
                multiply(i * 2, 0)
                mix(i * 2 + 2, 0)
                multiply(i * 2 + 1, 1)
            multiply(NB // 2 - 1, 0)


ME, MHID, TOP = 8, 1152, 2
MB = (TOP * NODES - ME) // P + ME
MSLOTS = MB * P
KH = MHID // P
SPARE = MSLOTS + TOP * P


def route(nc, R, name, wr, br, rows_table, slot_table):
    with Scope(nc, name) as c:
        w, bias, one = c.sb("w", [P, KD, ME]), c.sb("bias", [1, ME]), c.sb("one", [1, P])
        rows = [c.sb(f"rows{s}", [P, D]) for s in range(2)]
        rowsT = [c.sb(f"rowsT{s}", [P, KD, P]) for s in range(2)]
        pr, best = c.sb("probs", [P, NB, ME]), c.sb("best", [P, NB, ME])
        which, whichf = c.sb("which", [P, NB, ME], U32), c.sb("whichf", [P, NB, TOP])
        red = c.sb("red", [P, NB, 1])
        eight, rown, valid = c.sb("eight", [P, ME]), c.sb("rown", [P, NB]), c.sb("valid", [P, NB])
        spare, tri, ones = c.sb("spare", [P, NB, TOP]), c.sb("tri", [P, P]), c.sb("ones", [P, P])
        hot, member = c.sb("hot", [P, NB, TOP, ME]), c.sb("member", [P, NB, ME])
        off = c.sb("off", [P, NB + 1, ME])
        blocks, blocksi = c.sb("blocks", [P, ME]), c.sb("blocksi", [P, ME], I32)
        start = c.sb("start", [P, ME + 1])
        place, placed = c.sb("place", [P, NB, ME]), c.sb("placed", [P, NB, TOP, ME])
        slotf = c.sb("slotf", [P, NB, TOP, 1])
        nodei, none = c.sb("nodei", [P, NB], I32), c.sb("none", [P, SPARE // P], I32)
        mb, ends, exf = c.sb("mb", [1, MB]), c.sb("ends", [1, MB, ME]), c.sb("exf", [1, MB])
        psT = [c.ps(f"psT{s}", [P, 2, BANK]) for s in range(2)]
        psL = [c.ps(f"psL{s}", [P, BANK]) for s in range(2)]
        psC = c.ps("psC", [P, 2, NB, ME])
        s_w, s_v, s_c, s_rows, s_turn, s_turned, s_mm = (c.sem(x) for x in ("weights", "v", "consts", "rows", "turn", "turned", "mm"))
        s_logit, s_sub, s_exp, s_member, s_rank, s_slot, s_st, s_init, s_sc, s_ld = (
            c.sem(x) for x in ("logit", "sub", "exp", "member", "rank", "slot", "st", "init", "sc", "ld"))
        block = c.enter_context(nc.Block())

        @block.sync
        def _(sp):
            sp.dma_start(w[:], wr.rearrange("(k p) e -> p k e", p=P)).then_inc(s_w, 16)
            sp.dma_start(bias[:], br.rearrange("(o e) -> o e", o=1)).then_inc(s_w, 16)
            sp.dma_start(rows_table.rearrange("(b p) d -> p b d", p=P), R.H[:]).then_inc(s_st, 16)
            sp.wait_ge(s_c, 7)
            sp.dma_start(slot_table.rearrange("(p j) o -> p (j o)", p=P), none[:]).then_inc(s_init, 16)
            sp.wait_ge(s_sc, 16 * TOP * NB)
            sp.dma_start(R.slot_node[:], slot_table[0:MSLOTS, :].rearrange("(j p) o -> p (j o)", p=P), allow_slow_non_contiguous=True).then_inc(s_ld, 16)
            sp.wait_ge(s_ld, 16)
            sp.wait_ge(s_st, 16)

        @block.gpsimd
        def _(pool):
            lax = dict(allow_small_or_imprecise_dtypes=True)
            nc.gpsimd.iota(eight[:], [[1, ME]], 0, 0, **lax).then_inc(s_c, 1)
            nc.gpsimd.iota(rown[:], [[P, NB]], 0, 1, **lax).then_inc(s_c, 1)
            nc.gpsimd.iota(nodei[:], [[P, NB]], 0, 1).then_inc(s_c, 1)
            nc.gpsimd.iota(spare[:], [[0, NB], [1, TOP]], MSLOTS, TOP, **lax).then_inc(s_c, 1)
            nc.gpsimd.iota(mb[:], [[1, MB]], 0, 0, **lax).then_inc(s_c, 1)
            nc.gpsimd.memset(ones[:], 1.0).then_inc(s_c, 1)
            nc.gpsimd.memset(none[:], ROWS - 1).then_inc(s_c, 1)
            pool.wait_ge(s_c, 7)
            nc.gpsimd.affine_select(out=tri[:], in_=ones[:], compare_op=ALU.is_gt, fill=0.0, base=0, pattern=[[1, P]], channel_multiplier=-1).then_inc(s_c, 1)
            pool.wait_ge(s_init, 16)
            pool.wait_ge(s_slot, 1)
            for b in range(NB):
                for k in range(TOP):
                    nc.gpsimd.indirect_dma_start(out=slot_table, out_offset=bass.IndirectOffsetOnAxis(ap=R.slot[:, b, k:k + 1], axis=0),
                                                 in_=nodei[:, b:b + 1], in_offset=None).then_inc(s_sc, 16)

        @block.scalar
        def _(act):
            act.wait_ge(s_sub, 1)
            nc.scalar.activation(pr[:], pr[:], ACT.Exp).then_inc(s_exp, 1)

        @block.vector
        def _(dve):
            chain = Chain(dve, s_v)
            dve.sem_inc(s_turn, 2)
            dve.sem_inc(s_mm, 2)
            chain(nc.vector.memset(one[:], 1.0))
            dve.sem_inc(s_logit, 2)
            with dve.Fori(0, NB // 2) as i:
                for s in range(2):
                    b = i * 2 + s
                    dve.wait_ge(s_turn, b + 1)
                    nc.vector.tensor_copy(rows[s][:], blk(R.H, b)).then_inc(s_rows, 1)
                    dve.wait_ge(s_turn, b + 3)
                    dve.wait_ge(s_mm, b + 1)
                    nc.vector.tensor_copy(rowsT[s][:].rearrange("p (a k) q -> p a (k q)", a=2), psT[s][:, :, 0:HALF]).then_inc(s_turned, 1)
                    dve.wait_ge(s_mm, b + 3)
                    nc.vector.tensor_copy(blk(pr, b), psL[s][:, 0:ME]).then_inc(s_logit, 1)
            dve.wait_ge(s_logit, NB + 2)
            chain(nc.vector.tensor_reduce(red[:], pr[:], AX.X, ALU.max))
            chain(nc.vector.tensor_tensor(pr[:], pr[:], red[:].broadcast_to([P, NB, ME]), ALU.subtract))
            dve.sem_inc(s_sub, 1)
            dve.wait_ge(s_exp, 1)
            chain(nc.vector.tensor_reduce(red[:], pr[:], AX.X, ALU.add))
            chain(nc.vector.reciprocal(red[:], red[:]))
            chain(nc.vector.tensor_tensor(pr[:], pr[:], red[:].broadcast_to([P, NB, ME]), ALU.mult))
            for b in range(NB):
                last = nc.vector.max(best[:, b, :], pr[:, b, :])
            chain(last)
            for b in range(NB):
                last = nc.vector.max_index(which[:, b, :], best[:, b, :], pr[:, b, :])
            chain(last)
            nc.vector.tensor_copy(R.gate[:], best[:, :, 0:TOP])
            chain(nc.vector.tensor_copy(whichf[:], which[:, :, 0:TOP]))
            dve.wait_ge(s_c, 8)
            chain(nc.vector.tensor_scalar(valid[:], rown[:], float(NODES), None, ALU.is_lt))
            for k in range(TOP):
                last = nc.vector.tensor_tensor(hot[:, :, k, :], bcast(whichf[:, :, k], 2, ME), bcast(eight[:], 1, NB), ALU.is_equal)
            chain(last)
            chain(nc.vector.tensor_tensor(member[:], hot[:, :, 0, :], hot[:, :, 1, :], ALU.add))
            chain(nc.vector.tensor_tensor(member[:], member[:], bcast(valid[:], 2, ME), ALU.mult))
            dve.sem_inc(s_member, 1)
            dve.wait_ge(s_rank, 1)
            chain(nc.vector.memset(off[:, 0, :], 0.0))
            for b in range(NB):
                chain(nc.vector.tensor_tensor(off[:, b + 1, :], off[:, b, :], psC[:, 1, b, :], ALU.add))
            chain(nc.vector.tensor_scalar(blocks[:], off[:, NB, :], float(P - 1), None, ALU.add))
            chain(nc.vector.tensor_copy(blocksi[:], blocks[:]))
            chain(nc.vector.tensor_single_scalar(blocksi[:], blocksi[:], 7, ALU.arith_shift_right))
            chain(nc.vector.tensor_copy(blocks[:], blocksi[:]))
            chain(nc.vector.memset(start[:, 0:1], 0.0))
            for e in range(ME):
                chain(nc.vector.tensor_tensor(start[:, e + 1:e + 2], start[:, e:e + 1], blocks[:, e:e + 1], ALU.add))
            chain(nc.vector.tensor_tensor(place[:], off[:, 0:NB, :], psC[:, 0], ALU.add))
            chain(nc.vector.tensor_scalar(blocks[:], start[:, 0:ME], float(P), None, ALU.mult))
            chain(nc.vector.tensor_tensor(place[:], place[:], bcast(blocks[:], 1, NB), ALU.add))
            for k in range(TOP):
                last = nc.vector.tensor_tensor(placed[:, :, k, :], hot[:, :, k, :], place[:], ALU.mult)
            chain(last)
            chain(nc.vector.tensor_reduce(slotf[:], placed[:], AX.X, ALU.add))
            sf = slotf[:].squeeze(3)
            chain(nc.vector.tensor_tensor(sf, sf, spare[:], ALU.subtract))
            chain(nc.vector.tensor_tensor(sf, sf, bcast(valid[:], 2, TOP), ALU.mult))
            chain(nc.vector.tensor_tensor(sf, sf, spare[:], ALU.add))
            chain(nc.vector.tensor_copy(R.slot[:], sf))
            dve.sem_inc(s_slot, 1)
            chain(nc.vector.tensor_tensor(ends[:], bcast(start[0:1, 1:ME + 1], 1, MB), bcast(mb[:], 2, ME), ALU.is_le))
            chain(nc.vector.reduce_sum(exf[:], ends[:], AX.X))
            chain(nc.vector.tensor_scalar(exf[:], exf[:], float(ME - 1), None, ALU.min))
            chain(nc.vector.tensor_copy(R.block_expert[:], exf[:]))

        @block.tensor
        def _(pe):
            pe.wait_ge(s_w, 32)
            pe.wait_ge(s_v, 1)
            with pe.Fori(0, NB // 2) as i:
                for s in range(2):
                    b = i * 2 + s
                    pe.wait_ge(s_rows, b + 1)
                    for k in range(KD):
                        last = nc.tensor.transpose(psT[s][:, k // 3, (k % 3) * P:(k % 3 + 1) * P], rows[s][:, k * P:(k + 1) * P], R.ident[:])
                    last.then_inc(s_turn, 1)
                    pe.wait_ge(s_turned, b + 1)
                    pe.wait_ge(s_logit, b + 1)
                    for k in range(KD):
                        nc.tensor.matmul(psL[s][:, 0:ME], rowsT[s][:, k, :], w[:, k, :], start=(k == 0), stop=False)
                    nc.tensor.matmul(psL[s][:, 0:ME], one[:], bias[:], start=False, stop=True).then_inc(s_mm, 1)
            pe.wait_ge(s_member, 1)
            m = member[:].rearrange("p b e -> p (b e)")
            nc.tensor.matmul(psC[:, 0].rearrange("p b e -> p (b e)"), tri[:], m, start=True, stop=True)
            nc.tensor.matmul(psC[:, 1].rearrange("p b e -> p (b e)"), ones[:], m, start=True, stop=True).then_inc(s_rank, 1)


def experts(nc, R, name, rows_table, w1, b1, w2, b2, out_table):
    with Scope(nc, name) as c:
        w1t = [c.sb(f"w1{s}", [P, KD, MHID]) for s in range(2)]
        w2t = [c.sb(f"w2{s}", [P, KH, D]) for s in range(2)]
        b1r, b1t = c.sb("b1r", [ME, MHID]), c.sb("b1t", [P, KH, ME])
        rows = [R.H[:, s, :] for s in range(2)]
        y = [R.H[:, 2 + s, :] for s in range(2)]
        b2t = [R.H[:, 4 + s, :] for s in range(2)]
        rowsT = c.sb("rowsT", [P, KD, P])
        hT = [c.sb(f"hT{s}", [P, KH, P]) for s in range(2)]
        psT = c.ps("psT", [P, 2, BANK])
        psH = [c.ps(f"psH{j}", [P, BANK]) for j in range(4)]
        psY = c.ps("psY", [P, 2, BANK])
        s_b, s_bt, s_bc, s_turn, s_turned, s_h, s_gelu, s_y, s_add = (c.sem(x) for x in ("b", "bt", "bc", "turn", "turned", "h", "gelu", "y", "add"))
        s_w1, s_w2, s_b2, s_rows, s_st = ([c.sem(f"{x}{s}") for s in range(2)] for x in ("w1", "w2", "b2", "rows", "st"))
        block = c.enter_context(nc.Block())
        PAIRS = MB // 2

        def blocks(eng, one):
            with eng.Fori(0, PAIRS) as i:
                for s in range(2):
                    one(i, s)
            if MB % 2:
                one(PAIRS, 0)

        @block.sync
        def _(sp):
            sp.dma_start(b1r[:], b1).then_inc(s_b, 16)

            def load(i, s):
                j = i * 2 + s
                e = sp.value_load(R.block_expert[0:1, ds(j, 1)], min_val=0, max_val=ME - 1)
                sp.wait_ge(s_h, j * KH + KH)
                sp.dma_start(w1t[s][:], w1[ds(e, 1)].squeeze(0).rearrange("(k p) h -> p k h", p=P)).then_inc(s_w1[s], 16)
                sp.wait_ge(s_add, j + 1)
                sp.dma_start(w2t[s][:], w2[ds(e, 1)].squeeze(0).rearrange("(k p) d -> p k d", p=P)).then_inc(s_w2[s], 16)
                sp.dma_start(b2t[s], b2[ds(e, 1)].squeeze(0).partition_broadcast(P)).then_inc(s_b2[s], 16)

            def store(i, s):
                sp.wait_ge(s_add, i * 2 + s + 3)
                sp.dma_start(out_table[ds((i * 2 + s) * P, P), :], y[s]).then_inc(s_st[s], 16)

            load(0, 0)
            load(0, 1)
            with sp.Fori(0, PAIRS - 1) as i:
                for s in range(2):
                    store(i, s)
                    load(i + 1, s)
            store(PAIRS - 1, 0)
            if MB % 2:
                load(PAIRS, 0)
            store(PAIRS - 1, 1)
            if MB % 2:
                store(PAIRS, 0)
            for s in range(2):
                sp.wait_ge(s_st[s], 16 * (1 + PAIRS + (MB % 2 and not s)))

        @block.gpsimd
        def _(pool):
            def gather(i, s):
                pool.wait_ge(s_turn, i * 2 + s + 1)
                nc.gpsimd.tensor_copy(R.list[:, s:s + 1], R.slot_node[:, ds(i * 2 + s, 1)]).then_inc(s_bc, 1)
                pool.wait_ge(s_bc, i * 2 + s + 1)
                pool.nop(nofuse=True)
                nc.gpsimd.indirect_dma_start(out=rows[s], out_offset=None, in_=rows_table,
                                             in_offset=bass.IndirectOffsetOnAxis(ap=R.list[:, s:s + 1], axis=0)).then_inc(s_rows[s], 16)

            blocks(pool, gather)

        @block.scalar
        def _(act):
            act.wait_ge(s_bt, 1)
            nc.scalar.copy(b1t[:], psY[:, 0, 0:KH * ME].rearrange("p (k e) -> p k e", e=ME)).then_inc(s_b, 1)
            act.wait_ge(s_b, 17)

            def gelus(i, s):
                j = i * 2 + s
                e = act.value_load(R.block_expert[0:1, ds(j, 1)], min_val=0, max_val=ME - 1)
                act.wait_ge(s_y, j + 1)
                for m in range(KH):
                    act.wait_ge(s_h, (j + 2) * KH + m + 1)
                    nc.scalar.activation(hT[s][:, m, :], psH[m % 4][:, 0:P], ACT.Gelu, bias=b1t[:, m, ds(e, 1)]).then_inc(s_gelu, 1)

            blocks(act, gelus)

        @block.vector
        def _(dve):
            dve.sem_inc(s_turn, 2)
            dve.sem_inc(s_h, 2 * KH)
            dve.sem_inc(s_y, 2)
            dve.sem_inc(s_add, 2)
            for s in range(2):
                dve.sem_inc(s_st[s], 16)

            def turned(i, s):
                j = i * 2 + s
                dve.wait_ge(s_turn, j + 3)
                nc.vector.tensor_copy(rowsT[:].rearrange("p (a k) q -> p a (k q)", a=2), psT[:, :, 0:HALF]).then_inc(s_turned, 1)

            def finish(i, s):
                j = i * 2 + s
                dve.wait_ge(s_y, j + 3)
                dve.wait_ge(s_b2[s], i * 16 + 16)
                dve.wait_ge(s_st[s], i * 16 + 16)
                nc.vector.tensor_tensor(y[s].rearrange("p (a d) -> p a d", a=2), psY[:, :, 0:HALF], b2t[s].rearrange("p (a d) -> p a d", a=2), ALU.add).then_inc(s_add, 1)

            def both(i, s):
                turned(i, s)
                finish(i, s)

            blocks(dve, both)

        @block.tensor
        def _(pe):
            pe.wait_ge(s_b, 16)
            for k in range(KH):
                last = nc.tensor.transpose(psY[:, 0, k * ME:(k + 1) * ME], b1r[:, k * P:(k + 1) * P], R.ident[0:ME, 0:ME])
            last.then_inc(s_bt, 1)
            pe.wait_ge(s_b, 17)

            def one(i, s):
                j = i * 2 + s
                pe.wait_ge(s_rows[s], i * 16 + 16)
                for k in range(KD):
                    last = nc.tensor.transpose(psT[:, k // 3, (k % 3) * P:(k % 3 + 1) * P], rows[s][:, k * P:(k + 1) * P], R.ident[:])
                last.then_inc(s_turn, 1)
                pe.wait_ge(s_turned, j + 1)
                pe.wait_ge(s_w1[s], i * 16 + 16)
                for m in range(KH):
                    if m >= 4:
                        pe.wait_ge(s_gelu, j * KH + m - 3)
                    for k in range(KD):
                        last = nc.tensor.matmul(psH[m % 4][:, 0:P], w1t[s][:, k, m * P:(m + 1) * P], rowsT[:, k, :],
                                                start=(k == 0), stop=(k == KD - 1))
                    last.then_inc(s_h, 1)
                pe.wait_ge(s_w2[s], i * 16 + 16)
                pe.wait_ge(s_add, j + 2)
                for m in range(KH):
                    pe.wait_ge(s_gelu, j * KH + m + 1)
                    for a in range(2):
                        last = nc.tensor.matmul(psY[:, a, 0:HALF], hT[s][:, m, :], w2t[s][:, m, a * HALF:(a + 1) * HALF], start=(m == 0), stop=(m == KH - 1))
                last.then_inc(s_y, 1)

            blocks(pe, one)


def combine(nc, R, name, out_table, out):
    with Scope(nc, name) as c:
        g = [[R.H[:, 2 * s + k, :] for k in range(TOP)] for s in range(4)]
        s_v, s_done, s_st = c.sem("v"), c.sem("done"), c.sem("st")
        s_g = [c.sem(f"g{s}") for s in range(4)]
        block = c.enter_context(nc.Block())

        @block.gpsimd
        def _(pool):
            for b in range(NB):
                if b >= 4:
                    pool.wait_ge(s_done, b - 3)
                m = P if b < NB - 1 else LAST
                for k in range(TOP):
                    nc.gpsimd.indirect_dma_start(out=g[b % 4][k][0:m], out_offset=None, in_=out_table,
                                                 in_offset=bass.IndirectOffsetOnAxis(ap=R.slot[0:m, b, k:k + 1], axis=0)).then_inc(s_g[b % 4], 16)

        @block.vector
        def _(dve):
            chain = Chain(dve, s_v)
            for b in range(NB):
                dve.wait_ge(s_g[b % 4], 32 * (b // 4 + 1))
                m = P if b < NB - 1 else LAST
                x = R.X[0:m, b, :]
                chain(nc.vector.scalar_tensor_tensor(out=x, in0=g[b % 4][0][0:m], scalar=R.gate[0:m, b, 0:1], in1=x, op0=ALU.mult, op1=ALU.add))
                nc.vector.scalar_tensor_tensor(out=x, in0=g[b % 4][1][0:m], scalar=R.gate[0:m, b, 1:2], in1=x, op0=ALU.mult, op1=ALU.add).then_inc(s_done, 1)

        @block.sync
        def _(sp):
            for b in range(NB):
                m = P if b < NB - 1 else LAST
                sp.wait_ge(s_done, b + 1)
                sp.dma_start(out[b * P:b * P + m, :], R.X[0:m, b, :]).then_inc(s_st, 16)
            sp.wait_ge(s_st, 16 * NB)


def program(nc, A, out):
    with ExitStack() as ctx:
        def sb(name, shape, dt=F32):
            return ctx.enter_context(nc.sbuf_tensor(name, shape, dt))

        class R:
            pass

        R.ident = sb("ident", [P, P])
        R.nodes = sb("nodes", [P, ROWS])
        R.X = sb("X", [P, NB, D])
        R.H = sb("H", [P, NB, D])
        R.src = sb("src", [P, TILES], I32)
        R.dst_block = sb("dst_block", [P, TILES])
        R.dst = sb("dst", [P, TILES])
        R.ends = sb("ends", [QT, 1, 4, P + 2])
        R.visit_group = sb("visit_group", [1, VISITS], I32)
        R.visit_block = sb("visit_block", [1, VISITS], I32)
        R.visit_minus, R.visit_row = sb("visit_minus", [P, VISITS]), sb("visit_row", [P, VISITS])
        R.dinv = sb("dinv", [P, NB])
        R.dst_rows = nc.dram_tensor("dst_rows", (GROUPS, UN * P), F32, kind="Internal").ap()

        def table(name, width, rows=ROWS):
            return nc.dram_tensor(name, (rows, width), F32, kind="Internal").ap()

        setup(nc, R, A["x"], A["src"], A["dst"])
        norm_rows(nc, R, "ln0")
        with ExitStack() as gat:
            R.L = gat.enter_context(nc.sbuf_tensor("L", [P, HEADS, TILES], F32))
            layers = ((1, HEADS, "W1s", "W1d", "b1s", "b1d", "attn1", "ln1_w", "ln1_b"),
                      (2, 1, "Wos", "Wod", "bos", "bod", "attno", "lno_w", "lno_b"))
            for n, heads, ws, wd, bs, bd, at, lw, lb in layers:
                ws, wd, bs, bd, at, lw, lb = (A["L0_gnn_" + x] for x in (ws, wd, bs, bd, at, lw, lb))
                at = at.rearrange("h d -> (h d)")
                width = heads * head_width(heads)
                fs = table(f"fs{n}", width)
                with nc.sbuf_tensor(f"fd{n}", [P, NB, width], FR) as R.fd, nc.sbuf_tensor(f"fdl{n}", [P, NB, width], FR) as R.fdl:
                    project(nc, R, f"p{n}", [ws, wd], fs, [bs, bd], at, heads)
                    logits(nc, R, f"l{n}", fs, at, heads)
                edge_softmax(nc, R, f"s{n}", heads)
                with nc.sbuf_tensor(f"acc{n}", [P, NB, width + (n == 1)], F32) as R.acc:
                    aggregate(nc, R, f"a{n}", fs, width, heads, count=(n == 1))
                    finish_gat(nc, R, f"f{n}", heads, lw, lb, n == 1)
        norm_rows(nc, R, "ln1", l2=True)
        with ExitStack() as soft:
            comb = soft.enter_context(nc.sbuf_tensor("comb", [P, NB, SE], F32))
            slotsT = soft.enter_context(nc.sbuf_tensor("slotsT", [P, KD, SE], F32))
            with nc.sbuf_tensor("disp", [P, NB, SE], F32) as disp:
                soft_logits(nc, R, "m1", A["L0_ffn_phi"], A["L0_ffn_scale"], disp, comb, slotsT)
                soft_slots(nc, R, "m2", disp, slotsT)
            eo = R.H
            soft_experts(nc, R, "m3", A["L0_ffn_w1"], A["L0_ffn_b1"], A["L0_ffn_w2"], A["L0_ffn_b2"], slotsT, eo)
            soft_combine(nc, R, "m4", comb, eo)
        norm_rows(nc, R, "ln2")
        with ExitStack() as gcn:
            R.CT = gcn.enter_context(nc.sbuf_tensor("CT", [P, NB, ROWS], F32))
            edge_counts(nc, R, "ec")
            R.out = gcn.enter_context(nc.sbuf_tensor("gcn_out", [P, NB, D], F32))
            gcn_layer(nc, R, "gc1", R.H, A["L1_gnn_W1"], A["L1_gnn_b1"], True)
            gcn_layer(nc, R, "gc2", R.out, A["L1_gnn_W2"], A["L1_gnn_b2"], False)
        norm_rows(nc, R, "ln3")
        R.gate, R.slot = sb("gate", [P, NB, TOP]), sb("slot", [P, NB, TOP], I32)
        R.slot_node, R.block_expert = sb("slot_node", [P, MB], I32), sb("block_expert", [1, MB], I32)
        R.list = sb("list", [P, 2], I32)
        rows_table, out_table = table("moe_rows", D), table("moe_out", D, MSLOTS)
        slot_table = nc.dram_tensor("moe_slots", (SPARE, 1), I32, kind="Internal").ap()
        route(nc, R, "r1", A["L1_ffn_router_w"], A["L1_ffn_router_b"], rows_table, slot_table)
        experts(nc, R, "r2", rows_table, A["L1_ffn_w1"], A["L1_ffn_b1"], A["L1_ffn_w2"], A["L1_ffn_b2"], out_table)
        combine(nc, R, "r3", out_table, out)


_INS = ["x", "src", "dst", "L0_gnn_W1s", "L0_gnn_b1s", "L0_gnn_W1d", "L0_gnn_b1d", "L0_gnn_attn1", "L0_gnn_ln1_w", "L0_gnn_ln1_b",
        "L0_gnn_Wos", "L0_gnn_bos", "L0_gnn_Wod", "L0_gnn_bod", "L0_gnn_attno", "L0_gnn_lno_w", "L0_gnn_lno_b",
        "L0_ffn_phi", "L0_ffn_scale", "L0_ffn_w1", "L0_ffn_b1", "L0_ffn_w2", "L0_ffn_b2",
        "L1_gnn_W1", "L1_gnn_b1", "L1_gnn_W2", "L1_gnn_b2",
        "L1_ffn_router_w", "L1_ffn_router_b", "L1_ffn_w1", "L1_ffn_b1", "L1_ffn_w2", "L1_ffn_b2"]


def kernel(**inputs):
    import numpy as np
    import concourse.bacc as bacc
    from concourse.bass_utils import run_bass_kernel_spmd as run

    nc = bacc.Bacc("TRN2", target_bir_lowering=False, num_devices=1)
    arrays, args = {}, {}
    for name in _INS:
        a = np.ascontiguousarray(inputs[name])
        arrays[f"in_{name}"] = a
        args[name] = nc.dram_tensor(f"in_{name}", a.shape, mybir.dt.from_np(a.dtype), kind="ExternalInput").ap()
    out = nc.dram_tensor("out", (NODES, D), F32, kind="ExternalOutput").ap()
    program(nc, args, out)
    r = run(nc, [arrays], core_ids=[0])
    return r.results[0]["out"]
```

```python
from contextlib import ExitStack

import concourse.bass as bass
from concourse import mybir

ALU = mybir.AluOpType
ACT = mybir.ActivationFunctionType
AX = mybir.AxisListType
F32 = mybir.dt.float32
I32 = mybir.dt.int32
U32 = mybir.dt.uint32
FR = mybir.dt.float32r
F16, BF16 = mybir.dt.float16, mybir.dt.bfloat16

P = 128
NODES, D = 1250, 768
NB = -(-NODES // P)
ROWS = NB * P
LAST = NODES - (NB - 1) * P
KD = D // P
EDGES = 40000
UN = 4
GROUPS = -(-EDGES // (P * UN))
VISITS = GROUPS + NB - 1
WIDE = 8
WIDE_GROUPS = -(-EDGES // (P * WIDE))
WIDE_VISITS = WIDE_GROUPS + NB - 1
TILES = WIDE_GROUPS * WIDE
QT = TILES // 4
HALF = D // 2
NEG = -1.0e30
NO_NODE = 4096
HEADS = 8
BANK = 512
ds = bass.ds


def bcast(ap, axis, n):
    new = ap.unsqueeze(axis)
    shape = list(new.shape)
    shape[axis] = n
    return new.broadcast_to(shape)


class Chain:

    def __init__(self, eng, sem):
        self.eng, self.sem, self.base, self.i, self.per, self.n = eng, sem, 0, None, 0, 0

    def loop(self, i, per):
        self.base += self.n
        self.i, self.per, self.n = i, per, 0

    def end(self, times):
        assert self.n == self.per, (self.n, self.per)
        self.base += self.per * times
        self.i, self.n = None, 0

    def __call__(self, ins):
        ins.then_inc(self.sem, 1)
        self.n += 1
        at = self.base + self.n
        self.eng.wait_ge(self.sem, at if self.i is None else self.i * self.per + at)
        return ins


class Scope(ExitStack):

    def __init__(self, nc, name):
        super().__init__()
        self.nc, self.name, self.sems = nc, name, []
        self.callback(self.clear)

    def clear(self):
        if self.sems:
            self.nc.clear_and_free_semaphores(self.sems)
            self.nc.all_engine_barrier(sem_only=True)

    def sb(self, name, shape, dt=F32):
        return self.enter_context(self.nc.sbuf_tensor(f"{self.name}_{name}", shape, dt))

    def ps(self, name, shape):
        return self.enter_context(self.nc.psum_tensor(f"{self.name}_{name}", shape, F32))

    def sem(self, name):
        self.sems.append(self.nc.alloc_semaphore(f"{self.name}_{name}"))
        return self.sems[-1]


def head_width(heads):
    he = D // heads + 3
    while heads * he % 4:
        he += 1
    return he


def blk(t, b):
    return t[:, ds(b, 1), :].squeeze(1)


def layer_norms(nc, dve, chain, H, X, W, weight=None, bias=None, row=None):
    for b in range(NB):
        for a in range(2):
            last = nc.vector.bn_stats(W.st[:, b, a, :], X[:, b, a * HALF:(a + 1) * HALF])
    chain(last)
    for b in range(NB):
        last = nc.vector.bn_aggr(W.mv[:, b, :], W.st[:, b])
    chain(last)
    chain(nc.vector.tensor_scalar(W.val[:], W.mv[:, :, 1:2].squeeze(2), 1e-5, None, ALU.add))
    inverse_roots(nc, dve, chain, W, W.val, W.root, W.rstd)
    if weight is not None:
        for b in range(NB):
            last = nc.vector.scalar_tensor_tensor(out=H[:, b, :], in0=X[:, b, 0:D], scalar=W.mv[:, b, 0:1], in1=weight, op0=ALU.subtract, op1=ALU.mult)
        chain(last)
        for b in range(NB):
            last = nc.vector.scalar_tensor_tensor(out=H[:, b, :], in0=H[:, b, :], scalar=W.rstd[:, b:b + 1], in1=bias, op0=ALU.mult, op1=ALU.add)
        chain(last)
        return
    for b in range(NB):
        last = nc.vector.tensor_scalar(H[:, b, :], X[:, b, 0:D], W.mv[:, b, 0:1], W.rstd[:, b:b + 1], ALU.subtract, ALU.mult)
        if row is not None:
            last.then_inc(row, 1)
    if row is not None:
        dve.wait_ge(row, NB)
    else:
        chain(last)


class Roots:

    def __init__(self, c):
        self.st, self.mv = c.sb("st", [P, NB, 2, 6]), c.sb("mv", [P, NB, 2])
        self.val, self.root, self.rstd, self.sq = (c.sb(x, [P, NB]) for x in ("val", "root", "rstd", "sq"))
        self.s_val, self.s_root, self.n, self.m = c.sem("val"), c.sem("root"), 0, 0


def inverse_roots(nc, dve, chain, W, val, root, out):
    W.n += 1
    dve.sem_inc(W.s_val, 1)
    dve.wait_ge(W.s_root, W.n)
    chain(nc.vector.reciprocal(out[:], root[:]))
    chain(nc.vector.tensor_tensor(W.sq[:], out[:], out[:], ALU.mult))
    chain(nc.vector.tensor_tensor(W.sq[:], W.sq[:], val[:], ALU.mult))
    chain(nc.vector.tensor_scalar(W.sq[:], W.sq[:], -0.5, 1.5, ALU.mult, ALU.add))
    chain(nc.vector.tensor_tensor(out[:], out[:], W.sq[:], ALU.mult))


def square_roots(nc, act, W, val, root):
    W.m += 1
    act.wait_ge(W.s_val, W.m)
    nc.scalar.activation(root[:], val[:], ACT.Sqrt).then_inc(W.s_root, 1)


def setup(nc, R, x, src, dst):
    with Scope(nc, "set") as c:
        rows = c.sb("rows", [QT, 2, 4, P], I32)
        rowsf = c.sb("rowsf", [QT, 2, 4, P])
        first = c.sb("first", [1, GROUPS], I32)
        firstf, start = c.sb("firstf", [1, GROUPS]), c.sb("start", [1, GROUPS])
        steps = c.sb("steps", [1, VISITS])
        before = c.sb("before", [1, VISITS, GROUPS - 1])
        svf = c.sb("svf", [1, VISITS])
        cvf = c.sb("cvf", [1, VISITS])
        ones = c.sb("ones", [P, P])
        blocks = c.sb("blocks", [P, TILES], I32)
        minus_p = c.sb("minus_p", [P, 1])
        turned = c.ps("turned", [P, 2, 4, P])
        spread = c.ps("spread", [P, VISITS])
        s_blocks = c.sem("blocks")
        s_zero, s_x, s_e, s_f, s_p = (c.sem(n) for n in ("zero", "x", "edges", "first", "lists"))
        s_gi, s_id, s_iota, s_cast, s_t, s_v = (c.sem(n) for n in ("gi", "ident", "iota", "cast", "turned", "v"))
        full = EDGES - 3 * QT * P
        block = c.enter_context(nc.Block())

        @block.sync
        def _(sp):
            sp.wait_ge(s_zero, 3)
            sp.dma_start(R.X[:, 0:NB - 1, :], x[0:(NB - 1) * P, :].rearrange("(b p) d -> p b d", p=P)).then_inc(s_x, 16)
            sp.dma_start(R.X[0:LAST, NB - 1, :], x[(NB - 1) * P:NODES, :]).then_inc(s_x, 16)
            for j, e in enumerate((src, dst)):
                whole = full // P
                sp.dma_start(rows[:, j, 0:3, :], e[0:3 * QT * P].rearrange("(q t p) -> t q p", q=3, p=P)).then_inc(s_e, 16)
                sp.dma_start(rows[0:whole, j, 3, :], e[3 * QT * P:3 * QT * P + whole * P].rearrange("(t p) -> t p", p=P)).then_inc(s_e, 16)
                sp.dma_start(rows[whole:whole + 1, j, 3, 0:full - whole * P], e[3 * QT * P + whole * P:EDGES].rearrange("(t p) -> t p", t=1)).then_inc(s_e, 16)
            with nc.allow_non_contiguous_dma("one destination of each group"):
                sp.dma_start(first[:, 0:GROUPS - 1], dst[0:(GROUPS - 1) * P * UN].rearrange("(g e) -> g e", e=P * UN)[:, 0:1].rearrange("g o -> o g")).then_inc(s_f, 16)
                sp.dma_start(first[:, GROUPS - 1:GROUPS], dst[(GROUPS - 1) * P * UN:(GROUPS - 1) * P * UN + 1].rearrange("(a b) -> a b", a=1)).then_inc(s_f, 16)
            sp.wait_ge(s_x, 32)
            sp.wait_ge(s_cast, 1)
            for q in range(4):
                sp.dma_start(R.dst_rows.rearrange("g (u p) -> (g u) p", p=P)[q * QT:(q + 1) * QT, :], rowsf[:, 1, q, :]).then_inc(s_p, 16)
            sp.wait_ge(s_p, 64)

        @block.gpsimd
        def _(pool):
            nc.gpsimd.memset(ones[:], 1.0).then_inc(s_gi, 1)
            nc.gpsimd.iota(R.nodes[:], [[1, ROWS]], 0, 0, allow_small_or_imprecise_dtypes=True).then_inc(s_iota, 1)
            nc.gpsimd.iota(steps[:], [[1, VISITS]], 0, 0, allow_small_or_imprecise_dtypes=True).then_inc(s_iota, 1)
            nc.gpsimd.iota(minus_p[:], [[1, 1]], 0, -1, allow_small_or_imprecise_dtypes=True).then_inc(s_iota, 1)
            pool.wait_ge(s_gi, 1)
            nc.gpsimd.affine_select(out=R.ident[:], in_=ones[:], compare_op=ALU.is_equal, fill=0.0, base=0,
                                    pattern=[[-1, P]], channel_multiplier=1).then_inc(s_id, 1)

        @block.vector
        def _(dve):
            chain = Chain(dve, s_v)
            nc.vector.memset(R.X[:, NB - 1, :], 0.0).then_inc(s_zero, 1)
            nc.vector.memset(rows[:, 0], 0).then_inc(s_zero, 1)
            nc.vector.memset(rows[:, 1], NO_NODE).then_inc(s_zero, 1)
            dve.wait_ge(s_f, 32)
            dve.wait_ge(s_iota, 3)
            chain(nc.vector.tensor_single_scalar(first[:], first[:], 7, ALU.arith_shift_right))
            chain(nc.vector.tensor_copy(firstf[:], first[:]))
            for groups, visits, firsts, to_group, to_block in (
                    (WIDE_GROUPS, WIDE_VISITS, firstf[:, 0:GROUPS:WIDE // UN], R.wide_group, R.wide_block),
                    (GROUPS, VISITS, firstf[:], R.visit_group, R.visit_block)):
                bf, sv, cv = before[:, 0:visits, 0:groups - 1], svf[:, 0:visits], cvf[:, 0:visits]
                chain(nc.vector.tensor_tensor(start[:, 0:groups], firsts, steps[:, 0:groups], ALU.add))
                chain(nc.vector.tensor_tensor(bf, bcast(start[:, 1:groups], 1, visits), bcast(steps[:, 0:visits], 2, groups - 1), ALU.is_le))
                chain(nc.vector.reduce_sum(sv, bf, AX.X))
                chain(nc.vector.tensor_tensor(cv, steps[:, 0:visits], sv, ALU.subtract))
                nc.vector.tensor_copy(to_group[:], sv)
                chain(nc.vector.tensor_copy(to_block[:], cv))
            dve.sem_inc(s_blocks, 1)
            dve.wait_ge(s_e, 96)
            nc.vector.tensor_copy(rowsf[:], rows[:]).then_inc(s_cast, 1)
            dve.wait_ge(s_t, 1)
            for q in range(4):
                nc.vector.tensor_copy(R.src[:, q * QT:(q + 1) * QT], turned[:, 0, q, 0:QT])
                nc.vector.tensor_copy(R.dst[:, q * QT:(q + 1) * QT], turned[:, 1, q, 0:QT])
                chain(nc.vector.tensor_copy(blocks[:, q * QT:(q + 1) * QT], turned[:, 1, q, 0:QT]))
            nc.vector.tensor_copy(R.ends[:, :, :, 1:P + 1], rowsf[:, 1:2])
            nc.vector.tensor_scalar(R.visit_minus[:], spread[:], -1.0, None, ALU.mult)
            nc.vector.tensor_scalar(R.visit_row[:], spread[:], -float(P), minus_p[:], ALU.mult, ALU.add)
            chain(nc.vector.tensor_single_scalar(blocks[:], blocks[:], 7, ALU.arith_shift_right))
            chain(nc.vector.tensor_copy(R.dst_block[:], blocks[:]))
            chain(nc.vector.memset(R.ends[:, :, :, 0:1], -1.0))
            chain(nc.vector.memset(R.ends[:, :, :, P + 1:P + 2], -1.0))

        @block.tensor
        def _(pe):
            pe.wait_ge(s_id, 1)
            pe.wait_ge(s_cast, 1)
            for j in range(2):
                for q in range(4):
                    nc.tensor.transpose(turned[:, j, q, 0:QT], rowsf[:, j, q, :], R.ident[0:QT, 0:QT])
            pe.wait_ge(s_blocks, 1)
            pe.wait_ge(s_gi, 1)
            last = nc.tensor.matmul(spread[:], ones[0:1, :], cvf[:], start=True, stop=True)
            last.then_inc(s_t, 1)


def norm_rows(nc, R, name, l2=False):
    with Scope(nc, name) as c:
        W = Roots(c)
        sq = c.sb("squares", [P, NB, D]) if l2 else None
        s_v, s_row, s_sum = c.sem("v"), c.sem("row"), c.sem("sum")
        block = c.enter_context(nc.Block())

        @block.scalar
        def _(act):
            square_roots(nc, act, W, W.val, W.root)
            if l2:
                for b in range(NB):
                    act.wait_ge(s_row, b + 1)
                    nc.scalar.activation(sq[:, b, :], R.H[:, b, :], ACT.Square, accum_out=W.sq[:, b:b + 1]).then_inc(s_sum, 1)
                square_roots(nc, act, W, W.val, W.root)

        @block.vector
        def _(dve):
            chain = Chain(dve, s_v)
            layer_norms(nc, dve, chain, R.H, R.X, W, row=s_row)
            if l2:
                dve.wait_ge(s_sum, NB)
                chain(nc.vector.tensor_copy(W.val[:], W.sq[:]))
                chain(nc.vector.tensor_scalar(W.val[:], W.val[:], 1e-24, None, ALU.max))
                inverse_roots(nc, dve, chain, W, W.val, W.root, W.rstd)
                for b in range(NB):
                    nc.vector.tensor_scalar(R.H[:, b, :], R.H[:, b, :], W.rstd[:, b:b + 1], None, ALU.mult)


def project(nc, R, name, weights, table, biases, attn, heads):
    hd, he = D // heads, head_width(heads)
    width = heads * he
    with Scope(nc, name) as c:
        w = [c.sb(f"w{j}", [P, KD, D]) for j in range(2)]
        bias = [c.sb(f"bias{j}", [P, D]) for j in range(2)]
        at = c.sb("attn", [P, D])
        rows = c.sb("rows", [P, D])
        rowsT = [c.sb(f"rowsT{s}", [P, KD, P]) for s in range(2)]
        out, dest = c.sb("out", [P, width]), c.sb("dest", [P, D])
        lin = c.sb("lin", [P, heads, 1])
        psT = [c.ps(f"psT{s}", [P, 2, BANK]) for s in range(2)]
        psO = [c.ps(f"psO{j}", [P, 2, BANK]) for j in range(2)]
        s_w, s_b, s_v = [c.sem(f"weights{j}") for j in range(2)], c.sem("biases"), c.sem("v")
        s_rows, s_turn, s_turned, s_mm, s_taken, s_out, s_store = (c.sem(x) for x in ("rows", "turn", "turned", "mm", "taken", "out", "store"))
        block = c.enter_context(nc.Block())

        @block.sync
        def _(sp):
            for j in range(2):
                for k in range(KD):
                    sp.dma_start(w[j][:, k, :], weights[j][k * P:(k + 1) * P, :]).then_inc(s_w[j], 16)
                if j == 0:
                    for n in range(2):
                        sp.dma_start(bias[n][:], biases[n].partition_broadcast(P)).then_inc(s_b, 16)
                    sp.dma_start(at[:], attn.partition_broadcast(P)).then_inc(s_b, 16)
                    sp.wait_ge(s_w[0], 16 * KD)
            with sp.Fori(0, NB) as b:
                sp.wait_ge(s_out, b + 1)
                sp.dma_start(table[ds(b * P, P), :], out[:]).then_inc(s_store, 16)
            sp.wait_ge(s_store, 16 * (1 + NB))

        @block.scalar
        def _(act):
            act.sem_inc(s_store, 16)
            act.sem_inc(s_turn, 1)
            act.sem_inc(s_turned, 2)
            with act.Fori(0, NB // 2) as i:
                for s in range(2):
                    b = i * 2 + s
                    act.wait_ge(s_turn, b + 1)
                    nc.scalar.copy(rows[:], blk(R.H, b)).then_inc(s_rows, 1)
                    act.wait_ge(s_turn, b + 2)
                    act.wait_ge(s_mm, b * 4 + 4)
                    nc.scalar.copy(rowsT[s][:].rearrange("p (a k) q -> p a (k q)", a=2), psT[s][:, :, 0:HALF]).then_inc(s_turned, 1)

        @block.vector
        def _(dve):
            chain = Chain(dve, s_v)
            dve.sem_inc(s_mm, 8)
            dve.sem_inc(s_taken, 4)

            def byhead(t):
                return t.rearrange("p (h e) -> p h e", h=heads)

            outs = byhead(out[:])
            nc.vector.memset(outs[:, :, hd:hd + 1], 1.0)
            if he > hd + 3:
                nc.vector.memset(outs[:, :, hd + 3:he], 0.0)
            for r in (R.fd, R.fdl):
                cols = r[:].bitcast(F32).rearrange("p b (h e) -> p (b h) e", h=heads)
                nc.vector.memset(cols[:, :, hd:hd + 1], 0.0)
                if he > hd + 3:
                    nc.vector.memset(cols[:, :, hd + 3:he], 0.0)
            dve.wait_ge(s_b, 48)

            def linear(low, rows, to):
                for h in range(heads):
                    last = nc.vector.scalar_tensor_tensor(out=low[:, h, 0:hd].bitcast(F32), in0=rows(h), scalar=0.2, in1=at[:, h * hd:(h + 1) * hd],
                                                          op0=ALU.mult, op1=ALU.mult, accum_out=to(h))
                return chain(last)

            with dve.Fori(0, NB) as b:
                chain.loop(b, 6)
                dve.wait_ge(s_store, b * 16 + 16)
                high, low = (byhead(blk(r, b)) for r in (R.fd, R.fdl))
                hh = max(1, heads // 2)
                for a in range(2):
                    cut = slice(a * HALF, (a + 1) * HALF)
                    dve.wait_ge(s_mm, b * 4 + a + 9)
                    o = outs[:, a * hh:(a + 1) * hh, 0:hd] if heads > 1 else outs[:, :, cut]
                    p, q = (t.rearrange("p (h e) -> p h e", h=hh) for t in (psO[0][:, a, 0:HALF], bias[0][:, cut]))
                    nc.vector.tensor_tensor(o, p, q, ALU.add).then_inc(s_taken, 1)
                dve.wait_ge(s_taken, b * 4 + 6)
                linear(low, lambda h: outs[:, h, 0:hd], lambda h: outs[:, h, hd + 1:hd + 2])
                nc.vector.tensor_scalar(outs[:, :, hd + 2:hd + 3], outs[:, :, hd + 1:hd + 2], -1.0, None, ALU.mult).then_inc(s_out, 1)
                for a in range(2):
                    cut = slice(a * HALF, (a + 1) * HALF)
                    dve.wait_ge(s_mm, b * 4 + a + 11)
                    nc.vector.tensor_tensor(dest[:, cut], psO[1][:, a, 0:HALF], bias[1][:, cut], ALU.add).then_inc(s_taken, 1)
                dve.wait_ge(s_taken, b * 4 + 8)
                linear(low, lambda h: dest[:, h * hd:(h + 1) * hd], lambda h: lin[:, h, :])
                nc.vector.tensor_copy(high[:, :, hd + 1:hd + 2], lin[:])
                chain(nc.vector.tensor_copy(high[:, :, 0:hd], byhead(dest[:])))
                nc.vector.tensor_tensor(low[:, :, hd + 1:hd + 2], lin[:], high[:, :, hd + 1:hd + 2].bitcast(F32), ALU.subtract)
                chain(nc.vector.tensor_tensor(low[:, :, 0:hd], byhead(dest[:]), high[:, :, 0:hd].bitcast(F32), ALU.subtract))
                for r in (high, low):
                    chain(nc.vector.tensor_scalar(r[:, :, hd + 2:hd + 3], r[:, :, hd + 1:hd + 2].bitcast(F32), -1.0, None, ALU.mult))
            chain.end(NB)

        @block.tensor
        def _(pe):
            def turn(b, s):
                pe.wait_ge(s_rows, b + 1)
                pe.wait_ge(s_turned, b + 1)
                for k in range(KD):
                    last = nc.tensor.transpose(psT[s][:, k // 3, (k % 3) * P:(k % 3 + 1) * P], rows[:, k * P:(k + 1) * P], R.ident[:])
                last.then_inc(s_turn, 1)

            def multiply(b, s):
                pe.wait_ge(s_turned, b + 3)
                for j in range(2):
                    pe.wait_ge(s_w[j], 16 * KD)
                    for a in range(2):
                        pe.wait_ge(s_taken, b * 4 + j * 2 + a + 1)
                        for k in range(KD):
                            last = nc.tensor.matmul(psO[j][:, a, 0:HALF], rowsT[s][:, k, :], w[j][:, k, a * HALF:(a + 1) * HALF],
                                                    start=(k == 0), stop=(k == KD - 1))
                        last.then_inc(s_mm, 1)

            turn(0, 0)
            with pe.Fori(0, NB // 2 - 1) as i:
                turn(i * 2 + 1, 1)
                multiply(i * 2, 0)
                turn(i * 2 + 2, 0)
                multiply(i * 2 + 1, 1)
            turn(NB - 1, 1)
            multiply(NB - 2, 0)
            multiply(NB - 1, 1)


def logits(nc, R, name, fs, attn, heads):
    hd, he = D // heads, head_width(heads)
    width = heads * he
    half = width // 2
    cuts = [(0, half), (half, width)]
    if heads == 1:
        added = [(0, half)]
        parts = cuts
    else:
        added = [(0, half), (half, half + 2 * he)]
        parts = [(h * he, (h + 1) * he) for h in range(heads)]
    by_pe = added[-1][1]
    with Scope(nc, name) as c:
        at = c.sb("attn", [P, width])
        lists = c.sb("list", [P, 4, UN], I32)
        g = c.sb("g", [P, 2, UN, width])
        dsts, away = c.sb("dsts", [P, 2, UN * P]), c.sb("away", [P, UN * P])
        one = c.sb("one", [P, 1])
        spread = c.sb("spread", [P, 2, UN, P], FR)
        z = c.sb("z", [P, 2, width - by_pe])
        zr = c.sb("zr", [P, 2, width])
        part = c.sb("part", [P, 2, UN, len(parts)])
        inside = c.sb("inside", [P, 2, UN])
        fdc = [[c.sb(f"fdc{s}{t}", [P, width], FR) for t in range(2)] for s in range(2)]
        psZ = [c.ps(f"psZ{k}", [P, 2, BANK]) for k in range(UN)]
        s_at, s_v, s_one, s_list, s_z = c.sem("attn"), c.sem("v"), c.sem("one"), c.sem("list"), c.sem("z")
        s_g = [[c.sem(f"g{s}{k}") for k in range(UN)] for s in range(2)]
        s_d = [c.sem(f"d{s}") for s in range(2)]
        s_away, s_spread, s_rows, s_inside = (c.sem(x) for x in ("away", "spread", "rows", "inside"))
        s_mm, s_part, s_tail, s_sum = c.sem("mm"), c.sem("part"), c.sem("tail"), c.sem("sum")
        block = c.enter_context(nc.Block())

        @block.sync
        def _(sp):
            sp.wait_ge(s_one, 1)
            sp.dma_start(at[:].rearrange("p (h e) -> p h e", h=heads)[:, :, 0:hd], attn.rearrange("(h e) -> h e", h=heads).partition_broadcast(P)).then_inc(s_at, 16)
            with sp.Fori(0, VISITS // 2) as i:
                for s in range(2):
                    v = i * 2 + s
                    grp = sp.value_load(R.visit_group[0:1, ds(v, 1)], min_val=0, max_val=GROUPS - 1)
                    sp.wait_ge(s_spread, v + 1)
                    sp.dma_start(dsts[:, s, :], R.dst_rows[ds(grp, 1), :].squeeze(0).partition_broadcast(P)).then_inc(s_d[s], 16)

        @block.scalar
        def _(act):
            act.sem_inc(s_spread, 2)
            act.sem_inc(s_mm, 4 * UN)
            act.wait_ge(s_one, 1)
            with act.Fori(0, VISITS // 2) as i:
                for s in range(2):
                    v = i * 2 + s
                    b = act.value_load(R.visit_block[0:1, ds(v, 1)], min_val=0, max_val=NB - 1)
                    grp = act.value_load(R.visit_group[0:1, ds(v, 1)], min_val=0, max_val=GROUPS - 1)
                    act.wait_ge(s_d[s], i * 16 + 16)
                    nc.scalar.activation(away[:], dsts[:, s, :], ACT.Abs, bias=R.visit_row[:, ds(v, 1)]).then_inc(s_away, 1)
                    act.wait_ge(s_mm, v * UN + 3 * UN)
                    act.wait_ge(s_away, v + 1)
                    nc.scalar.activation(spread[:, s].rearrange("p k e -> p (k e)"), away[:], ACT.Relu, scale=-1.0, bias=one[:]).then_inc(s_spread, 1)
                    nc.scalar.copy(fdc[s][0][:], blk(R.fd, b).bitcast(F32))
                    nc.scalar.copy(fdc[s][1][:], blk(R.fdl, b).bitcast(F32)).then_inc(s_rows, 1)
                    act.wait_ge(s_sum, v + 1)
                    nc.scalar.activation(inside[:, s, :], R.dst_block[:, ds(grp * UN, UN)], ACT.Abs, bias=R.visit_minus[:, ds(v, 1)]).then_inc(s_inside, 1)
                    act.wait_ge(s_inside, v * 2 + 1)
                    nc.scalar.activation(inside[:, s, :], inside[:, s, :], ACT.Relu, scale=-1.0, bias=one[:]).then_inc(s_inside, 1)

        @block.gpsimd
        def _(pool):
            nc.gpsimd.memset(R.L[:, 0:heads, :], 0.0).then_inc(s_sum, 2)

            def gather(v, q):
                s = q % 2
                """The source rows of the group's edges, v = q mod 4."""
                grp = pool.value_load(R.visit_group[0:1, ds(v, 1)], min_val=0, max_val=GROUPS - 1)
                pool.wait_ge(s_mm, v * UN + UN)
                nc.gpsimd.tensor_copy(lists[:, q, :], R.src[:, ds(grp * UN, UN)]).then_inc(s_list, 1)
                for k in range(UN):
                    pool.wait_ge(s_part, v * UN + k + 1)
                    pool.wait_ge(s_list, v + 1)
                    pool.nop(nofuse=True)
                    nc.gpsimd.indirect_dma_start(
                        out=g[:, s, k, :], out_offset=None, in_=fs,
                        in_offset=bass.IndirectOffsetOnAxis(ap=lists[:, q, k:k + 1], axis=0)).then_inc(s_g[s][k], 16)

            def add(v, s):
                grp = pool.value_load(R.visit_group[0:1, ds(v, 1)], min_val=0, max_val=GROUPS - 1)
                pool.wait_ge(s_part, v * UN + 3 * UN)
                n = 2 if heads == 1 else 1
                if heads == 1:
                    nc.gpsimd.tensor_tensor(part[:, s, :, 0:1], part[:, s, :, 0:1], part[:, s, :, 1:2], ALU.add).then_inc(s_tail, 1)
                    pool.wait_ge(s_tail, v * n + 1)
                pool.wait_ge(s_inside, v * 2 + 2)
                pt = part[:, s, :, 0:heads]
                nc.gpsimd.tensor_tensor(pt, pt, bcast(inside[:, s, :], 2, heads), ALU.mult).then_inc(s_tail, 1)
                pool.wait_ge(s_tail, v * n + n)
                pool.wait_ge(s_sum, v + 2)
                sums = R.L[:, 0:heads, ds(grp * UN, UN)]
                nc.gpsimd.tensor_tensor(sums, sums, pt.rearrange("p k h -> p h k"), ALU.add).then_inc(s_sum, 1)

            gather(0, 0)
            gather(1, 1)
            with pool.Fori(0, VISITS // 4 - 1) as i:
                for q in range(4):
                    gather(i * 4 + q + 2, (q + 2) % 4)
                    add(i * 4 + q, q % 2)
            for q in range(4):
                if q < 2:
                    gather(VISITS - 2 + q, q + 2)
                add(VISITS - 4 + q, q % 2)
            pool.wait_ge(s_sum, VISITS + 2)

        @block.vector
        def _(dve):
            chain = Chain(dve, s_v)
            dve.sem_inc(s_part, 2 * UN)
            chain(nc.vector.memset(one[:], 1.0))
            chain(nc.vector.memset(at[:], 0.0))
            dve.sem_inc(s_one, 1)
            dve.wait_ge(s_at, 16)
            ah = at[:].rearrange("p (h e) -> p h e", h=heads)
            nc.vector.memset(ah[:, :, hd + 1:hd + 2], 1.0)
            nc.vector.memset(ah[:, :, hd + 2:hd + 3], -1.0)
            chain(nc.vector.tensor_scalar(ah[:, :, 0:hd], ah[:, :, 0:hd], 0.8, None, ALU.mult))
            with dve.Fori(0, VISITS // 2) as i:
                for s in range(2):
                    v = i * 2 + s
                    dve.wait_ge(s_sum, v + 1)
                    for k in range(UN):
                        n, j = v * UN + k, k % 2
                        dve.wait_ge(s_mm, n + 4 * UN + 1)
                        nc.vector.tensor_tensor(z[:, j, :], psZ[k][:, 1, by_pe - half:half], g[:, s, k, by_pe:width], ALU.add).then_inc(s_z, 1)
                        waited = False
                        for m, (lo, hi) in enumerate(parts):
                            own = lo >= by_pe
                            if own and not waited:
                                dve.wait_ge(s_z, n + 1)
                                waited = True
                            src = z[:, j, lo - by_pe:hi - by_pe] if own else psZ[k][:, lo // half, lo % half:lo % half + hi - lo]
                            last = nc.vector.scalar_tensor_tensor(out=zr[:, j, lo:hi], in0=src, scalar=0.0, in1=at[:, lo:hi], op0=ALU.max, op1=ALU.mult,
                                                                  accum_out=part[:, s, k, m:m + 1])
                        last.then_inc(s_part, 1)

        @block.tensor
        def _(pe):
            with pe.Fori(0, VISITS // 2) as i:
                for s in range(2):
                    v = i * 2 + s
                    pe.wait_ge(s_spread, v + 3)
                    pe.wait_ge(s_rows, v + 1)
                    for k in range(UN):
                        pe.wait_ge(s_part, v * UN + k + UN + 1)
                        for a, (lo, hi) in enumerate(cuts):
                            for t in range(2):
                                nc.tensor.matmul(psZ[k][:, a, 0:half], spread[:, s, k, :], fdc[s][t][:, lo:hi], start=(t == 0), stop=(t == 1))
                        pe.wait_ge(s_g[s][k], i * 16 + 16)
                        for a, (lo, hi) in enumerate(added):
                            last = nc.tensor.matmul(psZ[k][:, a, 0:hi - lo], R.ident[:], g[:, s, k, lo:hi], start=False, stop=True, skip_group_check=True)
                        last.then_inc(s_mm, 1)


def edge_softmax(nc, R, name, heads):
    W = P + 2
    with Scope(nc, name) as c:
        S = c.sb("S", [QT, 4, heads, W])
        pen = c.sb("pen", [QT, 2, 4, heads, W])
        run = c.sb("run", [QT, 2, heads, W])
        sides = c.sb("sides", [QT, 4, 4, heads])
        rowsd = c.sb("rowsd", [heads, 4, TILES])
        a = c.sb("a", [heads, 6, TILES])
        seen = c.sb("seen", [heads, 2, TILES])
        carry = c.sb("carry", [heads, 2, TILES])
        psS = c.ps("psS", [P, 2, 4, P])
        psR = c.ps("psR", [heads, 4, BANK])
        psC = c.ps("psC", [P, BANK])
        s_v, s_turn, s_copied, s_side, s_rows, s_carry, s_back = (c.sem(x) for x in ("v", "turn", "copied", "side", "rows", "carry", "back"))
        s_exp, s_exped, s_ret, s_retd = c.sem("exp"), c.sem("exped"), c.sem("ret"), c.sem("retd")
        block = c.enter_context(nc.Block())

        @block.tensor
        def _(pe):
            for q in range(4):
                for h in range(heads):
                    n = q * heads + h
                    if n >= 8 and n % 4 == 0:
                        pe.wait_ge(s_copied, n // 4 - 1)
                    t = nc.tensor.transpose(psS[0:QT, n // 4 % 2, n % 4, :], R.L[:, h, q * QT:(q + 1) * QT], R.ident[:])
                    if n % 4 == 3:
                        t.then_inc(s_turn, 1)
            pe.wait_ge(s_side, 1)
            for j in range(4):
                for q in range(4):
                    last = nc.tensor.transpose(psR[:, j, q * QT:(q + 1) * QT], sides[:, q, j, :], R.ident[0:QT, 0:QT])
            last.then_inc(s_rows, 1)
            pe.wait_ge(s_carry, 1)
            for j in range(2):
                for q in range(4):
                    last = nc.tensor.transpose(psC[0:QT, (j * 4 + q) * heads:(j * 4 + q + 1) * heads], carry[:, j, q * QT:(q + 1) * QT], R.ident[0:heads, 0:heads])
            last.then_inc(s_back, 1)
            for h in range(heads):
                if h == 0:
                    pe.wait_ge(s_exped, 4)
                if h >= 2:
                    pe.wait_ge(s_retd, h - 1)
                for q in range(4):
                    last = nc.tensor.transpose(psS[:, h % 2, :, :].rearrange("p a b -> p (a b)")[:, q * QT:(q + 1) * QT], S[:, q, h, 1:P + 1], R.ident[0:QT, 0:QT])
                last.then_inc(s_ret, 1)

        @block.scalar
        def _(act):
            for n in range(heads):
                act.wait_ge(s_turn, n + 1)
                for k in range(4):
                    m = n * 4 + k
                    last = nc.scalar.copy(S[:, m // heads, m % heads, 1:P + 1], psS[0:QT, n % 2, k, :])
                last.then_inc(s_copied, 1)
            for q in range(4):
                act.wait_ge(s_exp, q + 1)
                nc.scalar.activation(S[:, q, :, 1:P + 1], S[:, q, :, 1:P + 1], ACT.Exp).then_inc(s_exped, 1)
            for h in range(heads):
                act.wait_ge(s_ret, h + 1)
                nc.scalar.copy(R.L[:, h, :], psS[:, h % 2, :, :].rearrange("p a b -> p (a b)")[:, 0:TILES]).then_inc(s_retd, 1)

        @block.vector
        def _(dve):
            chain = Chain(dve, s_v)
            flat = "p h w -> p (h w)"

            def scans():
                for q in range(4):
                    yield q
                    chain(nc.vector.tensor_tensor_scan(run[:, 0].rearrange(flat), pen[:, 0, q].rearrange(flat), S[:, q].rearrange(flat), NEG, ALU.add, ALU.max))
                    chain(nc.vector.tensor_tensor_scan(run[:, 1].rearrange(flat)[:, ::-1], pen[:, 1, q].rearrange(flat)[:, ::-1], S[:, q].rearrange(flat)[:, ::-1], NEG, ALU.add, ALU.max))
                    yield q

            chain(nc.vector.memset(pen[:], 0.0))
            for q in range(4):
                same = run[:, 0, 0, 0:P - 1]
                e = R.ends[:, 0, q]
                chain(nc.vector.tensor_tensor(same, e[:, 2:P + 1], e[:, 1:P], ALU.not_equal))
                chain(nc.vector.tensor_scalar(same, same, NEG, None, ALU.mult))
                nc.vector.tensor_copy(pen[:, 0, q, :, 2:P + 1], bcast(same, 1, heads))
                chain(nc.vector.tensor_copy(pen[:, 1, q, :, 1:P], bcast(same, 1, heads)))
            nc.vector.memset(pen[:, 0, :, :, 0:1], NEG)
            chain(nc.vector.memset(pen[:, 1, :, :, P + 1:W], NEG))
            nc.vector.memset(S[:, :, :, 0:1], NEG)
            chain(nc.vector.memset(S[:, :, :, P + 1:W], NEG))
            for q in range(4):
                nc.vector.tensor_copy(sides[:, q, 2, :], R.ends[:, 0, q, 1:2].broadcast_to([QT, heads]))
                chain(nc.vector.tensor_copy(sides[:, q, 3, :], R.ends[:, 0, q, P:P + 1].broadcast_to([QT, heads])))
            dve.wait_ge(s_copied, heads)
            it = scans()
            for q in it:
                next(it)
                nc.vector.tensor_copy(sides[:, q, 0, :], run[:, 0, :, P:P + 1].squeeze(2))
                chain(nc.vector.tensor_copy(sides[:, q, 1, :], run[:, 1, :, 1:2].squeeze(2)))
            dve.sem_inc(s_side, 1)
            dve.wait_ge(s_rows, 1)
            chain(nc.vector.tensor_copy(rowsd[:], psR[:, :, 0:TILES]))
            last, first, dfirst, dlast = (rowsd[:, j, :] for j in range(4))
            whole, cont, nocont = a[:, 0, :], a[:, 1, :], a[:, 2, :]
            T1 = TILES - 1
            nc.vector.tensor_tensor(whole, dfirst, dlast, ALU.is_equal)
            nc.vector.tensor_tensor(cont[:, 0:T1], dfirst[:, 1:TILES], dlast[:, 0:T1], ALU.is_equal)
            chain(nc.vector.memset(cont[:, T1:TILES], 0.0))
            chain(nc.vector.tensor_scalar(nocont[:, 0:T1], cont[:, 0:T1], -NEG, NEG, ALU.mult, ALU.add))
            nc.vector.tensor_tensor(a[:, 3, 1:TILES], whole[:, 1:TILES], cont[:, 0:T1], ALU.mult)
            nc.vector.tensor_tensor(a[:, 4, 0:TILES], whole, cont, ALU.mult)
            chain(nc.vector.memset(a[:, 3, 0:1], 0.0))
            chain(nc.vector.tensor_scalar(a[:, 3:5, :], a[:, 3:5, :], -NEG, NEG, ALU.mult, ALU.add))
            nc.vector.tensor_tensor_scan(seen[:, 0, :], a[:, 3, :], last, NEG, ALU.add, ALU.max)
            chain(nc.vector.tensor_tensor_scan(seen[:, 1, ::-1], a[:, 4, ::-1], first[:, ::-1], NEG, ALU.add, ALU.max))
            nc.vector.memset(carry[:, 0, 0:1], NEG)
            chain(nc.vector.memset(carry[:, 1, T1:TILES], NEG))
            nc.vector.tensor_tensor(carry[:, 0, 1:TILES], seen[:, 0, 0:T1], a[:, 2, 0:T1], ALU.add)
            chain(nc.vector.tensor_tensor(carry[:, 1, 0:T1], seen[:, 1, 1:TILES], a[:, 2, 0:T1], ALU.add))
            dve.sem_inc(s_carry, 1)
            dve.wait_ge(s_back, 1)
            back = psC[0:QT, 0:8 * heads].rearrange("p (j q h) -> p j q h", j=2, q=4)
            nc.vector.tensor_copy(S[:, :, :, 0:1], back[:, 0].unsqueeze(3))
            chain(nc.vector.tensor_copy(S[:, :, :, P + 1:W], back[:, 1].unsqueeze(3)))
            it = scans()
            for q in it:
                next(it)
                chain(nc.vector.tensor_tensor(run[:, 0], run[:, 0], run[:, 1], ALU.max))
                chain(nc.vector.tensor_tensor(S[:, q, :, 1:P + 1], S[:, q, :, 1:P + 1], run[:, 0, :, 1:P + 1], ALU.subtract))
                dve.sem_inc(s_exp, 1)


def aggregate(nc, R, name, table, width, heads=0, count=False):
    cols = width + bool(count)
    cuts = [(0, width // 2), (width // 2, cols)]
    he = width // heads
    SPLIT = 2 if heads == 1 else 0
    by_dve = () if heads == 1 else range(SPLIT, UN - 1)
    with Scope(nc, name) as c:
        lists = c.sb("list", [P, 4, UN], I32)
        g = c.sb("g", [P, 2, UN, cols])
        sel = c.sb("sel", [P, 2, UN, P], FR)
        high, low = (c.sb(x, [P, 2, SPLIT, cols], FR) if SPLIT else None for x in ("high", "low"))
        psO = [c.ps(f"psO{s}", [P, 2, BANK]) for s in range(2)]
        s_v, s_list, s_zero = c.sem("v"), c.sem("list"), c.sem("zero")
        s_g = [[c.sem(f"g{s}{k}") for k in range(UN)] for s in range(2)]
        s_w = [[c.sem(f"w{s}{k}") for k in range(UN)] for s in range(2)]
        s_mm = [[c.sem(f"mm{s}{k}") for k in range(UN)] for s in range(2)]
        s_high = [[c.sem(f"high{s}{k}") for k in range(SPLIT)] for s in range(2)]
        s_sel, s_add = c.sem("sel"), c.sem("add")
        block = c.enter_context(nc.Block())

        @block.gpsimd
        def _(pool):
            pool.wait_ge(s_zero, 1)
            with pool.Fori(0, VISITS // 4) as i:
                for q in range(4):
                    v, s, pair = i * 4 + q, q % 2, i * 2 + q // 2
                    grp = pool.value_load(R.visit_group[0:1, ds(v, 1)], min_val=0, max_val=GROUPS - 1)
                    pool.wait_ge(s_mm[s][UN - 1], pair + 1)
                    nc.gpsimd.tensor_copy(lists[:, q, :], R.src[:, ds(grp * UN, UN)]).then_inc(s_list, 1)
                    for k in range(UN):
                        pool.wait_ge(s_mm[s][k], pair + (1 if k < UN - 1 else 2))
                        pool.wait_ge(s_list, v + 1)
                        pool.nop(nofuse=True)
                        nc.gpsimd.indirect_dma_start(
                            out=g[:, s, k, 0:width], out_offset=None, in_=table,
                            in_offset=bass.IndirectOffsetOnAxis(ap=lists[:, q, k:k + 1], axis=0)).then_inc(s_g[s][k], 16)

        @block.vector
        def _(dve):
            chain = Chain(dve, s_v)
            chain(nc.vector.memset(R.acc[:], 0.0))
            if count:
                chain(nc.vector.memset(g[:, :, :, width:cols], 1.0))
            for s in range(2):
                for k in range(UN):
                    dve.sem_inc(s_mm[s][k], 1 if k < UN - 1 else 2)
            dve.sem_inc(s_zero, 1)
            dve.sem_inc(s_add, 4)

            def make(i, s):
                v = i * 2 + s
                grp = dve.value_load(R.visit_group[0:1, ds(v, 1)], min_val=0, max_val=GROUPS - 1)
                blk = dve.value_load(R.visit_block[0:1, ds(v, 1)], min_val=0, max_val=NB - 1)
                dve.wait_ge(s_mm[s][UN - 1], i + 2)
                nc.vector.tensor_tensor(sel[:, s], bcast(R.nodes[:, ds(blk * P, P)], 1, UN), bcast(R.dst[:, ds(grp * UN, UN)], 2, P), ALU.is_equal).then_inc(s_sel, 1)
                for k in range(UN):
                    rows = g[:, s, k, 0:width].rearrange("p (h e) -> p h e", h=heads)
                    if k in by_dve:
                        dve.wait_ge(s_g[s][k], i * 16 + 16)
                        nc.vector.tensor_tensor(rows, rows, R.L[:, :, ds(grp * UN + k, 1)].broadcast_to([P, heads, he]), ALU.mult).then_inc(s_w[s][k], 1)
                for k in range(SPLIT):
                    dve.wait_ge(s_high[s][k], i + 1)
                    for h in range(heads):
                        cut = slice(h * he, (h + 1) * he)
                        last = nc.vector.scalar_tensor_tensor(out=low[:, s, k, cut], in0=g[:, s, k, cut], scalar=R.L[:, h, ds(grp * UN + k, 1)],
                                                              in1=high[:, s, k, cut].bitcast(F32), op0=ALU.mult, op1=ALU.subtract)
                    last.then_inc(s_w[s][k], 1)

            def add(i, s):
                v = i * 2 + s
                blk = dve.value_load(R.visit_block[0:1, ds(v, 1)], min_val=0, max_val=NB - 1)
                dve.wait_ge(s_add, v * 2 + 4)
                dve.wait_ge(s_mm[s][UN - 1], i + 3)
                for a, (lo, hi) in enumerate(cuts):
                    acc = R.acc[:, ds(blk, 1), lo:hi].squeeze(1)
                    nc.vector.tensor_tensor(acc, acc, psO[s][:, a, 0:hi - lo], ALU.add).then_inc(s_add, 1)

            make(0, 0)
            with dve.Fori(0, VISITS // 2 - 1) as i:
                make(i, 1)
                add(i, 0)
                make(i + 1, 0)
                add(i, 1)
            last = VISITS // 2 - 1
            make(last, 1)
            add(last, 0)
            add(last, 1)

        @block.scalar
        def _(act):
            with act.Fori(0, VISITS // 2) as i:
                for s in range(2):
                    v = i * 2 + s
                    grp = act.value_load(R.visit_group[0:1, ds(v, 1)], min_val=0, max_val=GROUPS - 1)
                    for k in range(UN):
                        if k not in by_dve:
                            act.wait_ge(s_g[s][k], i * 16 + 16)
                            act.nop(nofuse=True)
                            for h in range(heads):
                                cut = slice(h * he, (h + 1) * he)
                                to = high[:, s, k, cut] if k < SPLIT else g[:, s, k, cut]
                                last = nc.scalar.activation(to, g[:, s, k, cut], ACT.Copy, scale=R.L[:, h, ds(grp * UN + k, 1)])
                            last.then_inc((s_high if k < SPLIT else s_w)[s][k], 1)

        @block.tensor
        def _(pe):
            with pe.Fori(0, VISITS // 2) as i:
                for s in range(2):
                    v = i * 2 + s
                    pe.wait_ge(s_add, v * 2 + 2)
                    pe.wait_ge(s_sel, v + 1)
                    for k in range(UN):
                        pe.wait_ge(s_w[s][k], i + 1)
                        parts = (high, low) if k < SPLIT else (g,)
                        one = sel[:, s, k, :] if k < SPLIT else sel[:, s, k, :].bitcast(F32)
                        for a, (lo, hi) in enumerate(cuts):
                            for t, rows in enumerate(parts):
                                last = nc.tensor.matmul(psO[s][:, a, 0:hi - lo], one, rows[:, s, k, lo:hi],
                                                        start=(k == 0 and t == 0), stop=(k == UN - 1))
                        last.then_inc(s_mm[s][k], 1)


def finish_gat(nc, R, name, heads, weight, bias, first):
    hd, he = D // heads, head_width(heads)
    with Scope(nc, name) as c:
        W = Roots(c)
        wt, bs = c.sb("weight", [P, D]), c.sb("bias", [P, D])
        den = c.sb("den", [P, NB, heads, 1])
        v, e = c.sb("values", [P, 2, D]), c.sb("e", [P, 2, D])
        s_w, s_v, s_low, s_exp = c.sem("weights"), c.sem("v"), c.sem("low"), c.sem("exp")
        block = c.enter_context(nc.Block())

        @block.sync
        def _(sp):
            sp.dma_start(wt[:], weight.partition_broadcast(P)).then_inc(s_w, 16)
            sp.dma_start(bs[:], bias.partition_broadcast(P)).then_inc(s_w, 16)

        @block.scalar
        def _(act):
            for b in range(NB):
                act.wait_ge(s_low, b + 1)
                nc.scalar.activation(e[:, b % 2, :], e[:, b % 2, :], ACT.Exp).then_inc(s_exp, 1)
            if first:
                square_roots(nc, act, W, W.val, W.root)
            square_roots(nc, act, W, W.val, W.root)

        @block.vector
        def _(dve):
            chain = Chain(dve, s_v)

            if first:
                chain(nc.vector.tensor_scalar(W.val[:], R.acc[:, :, heads * he:heads * he + 1].squeeze(2), 1.0, None, ALU.add))
            acc = R.acc[:, :, 0:heads * he].rearrange("p b (h e) -> p b h e", h=heads)
            chain(nc.vector.tensor_scalar(den[:], acc[:, :, :, hd:hd + 1], 1e-30, None, ALU.max))
            chain(nc.vector.reciprocal(den[:], den[:]))
            for b in range(NB + 1):
                if b < NB:
                    vb, eb = v[:, b % 2, :], e[:, b % 2, :]
                    chain(nc.vector.tensor_tensor(vb.rearrange("p (h e) -> p h e", h=heads), acc[:, b, :, 0:hd], den[:, b].broadcast_to([P, heads, hd]), ALU.mult))
                    nc.vector.tensor_scalar(eb, vb, 0.0, None, ALU.min).then_inc(s_low, 1)
                if b:
                    vb, eb = v[:, (b - 1) % 2, :], e[:, (b - 1) % 2, :]
                    dve.wait_ge(s_exp, b)
                    chain(nc.vector.scalar_tensor_tensor(out=vb, in0=vb, scalar=0.0, in1=eb, op0=ALU.max, op1=ALU.add))
                    y = R.acc[:, b - 1, 0:D]
                    if first:
                        chain(nc.vector.scalar_tensor_tensor(out=y, in0=vb, scalar=-1.0, in1=R.H[:, b - 1, :], op0=ALU.add, op1=ALU.add))
                    else:
                        chain(nc.vector.tensor_scalar(y, vb, -1.0, None, ALU.add))
            if first:
                inverse_roots(nc, dve, chain, W, W.val, W.root, R.dinv)
            dve.wait_ge(s_w, 32)
            layer_norms(nc, dve, chain, R.H, R.acc, W, wt[:], bs[:])
            if not first:
                nc.vector.tensor_tensor(R.X[:], R.X[:], R.H[:], ALU.add)


EXPERTS, SLOTS, HID = 32, 32, 192
SE = EXPERTS * SLOTS
KS = SE // P
HC = HID // 2


def soft_logits(nc, R, name, phi, scale, disp, comb, ph):
    with Scope(nc, name) as c:
        sq = c.sb("sq", [P, 2, SE])
        f = c.sb("f", [P, 2, SE])
        ones, sc = c.sb("ones", [P, P]), c.sb("scale", [P, 1])
        rows = [c.sb(f"rows{s}", [P, D]) for s in range(2)]
        rowsT = [c.sb(f"rowsT{s}", [P, KD, P]) for s in range(2)]
        gm, rm, gs, rs = c.sb("gm", [P, 2, EXPERTS, 1]), c.sb("rm", [P, 2]), c.sb("gs", [P, 2, EXPERTS, 1]), c.sb("rs", [P, 2])
        psT = [c.ps(f"psT{s}", [P, 2, BANK]) for s in range(2)]
        psO = [c.ps(f"psO{s}", [P, 2, BANK]) for s in range(2)]
        s_w = [c.sem(f"weights{k}") for k in range(KD)]
        s_sc, s_v, s_sq, s_n, s_clip, s_root = (c.sem(x) for x in ("scale", "v", "sq", "n", "clip", "root"))
        s_rows, s_turn, s_turned, s_mm, s_scaled, s_exp, s_sub = (c.sem(x) for x in ("rows", "turn", "turned", "mm", "scaled", "exp", "sub"))
        block = c.enter_context(nc.Block())

        @block.sync
        def _(sp):
            for k in range(KD):
                sp.dma_start(ph[:, k, :], phi[k * P:(k + 1) * P].rearrange("p e s -> p (e s)")).then_inc(s_w[k], 16)
            sp.dma_start(sc[:], scale.partition_broadcast(P)).then_inc(s_sc, 16)

        @block.vector
        def _(dve):
            chain = Chain(dve, s_v)
            chain(nc.vector.memset(ones[:], 1.0))
            dve.sem_inc(s_scaled, 1)
            dve.wait_ge(s_n, KD)
            n2, r = f[:, 0, :], f[:, 1, :]
            chain(nc.vector.tensor_scalar(n2.rearrange("p (a b) -> p a b", a=2), psO[1][:], 1e-24, None, ALU.max))
            dve.sem_inc(s_scaled, 1)
            dve.sem_inc(s_clip, 1)
            dve.wait_ge(s_root, 1)
            chain(nc.vector.reciprocal(r, sq[:, 0, :]))
            chain(nc.vector.tensor_tensor(sq[:, 1, :], r, r, ALU.mult))
            chain(nc.vector.tensor_tensor(sq[:, 1, :], sq[:, 1, :], n2, ALU.mult))
            chain(nc.vector.tensor_scalar(sq[:, 1, :], sq[:, 1, :], -0.5, 1.5, ALU.mult, ALU.add))
            chain(nc.vector.tensor_tensor(r, r, sq[:, 1, :], ALU.mult))
            dve.wait_ge(s_sc, 16)
            chain(nc.vector.tensor_scalar(r, r, sc[:], None, ALU.mult))

            with dve.Fori(0, NB // 2) as i:
                chain.loop(i, 14)
                for s in range(2):
                    b = i * 2 + s
                    dve.wait_ge(s_mm, b + 3)
                    nc.vector.tensor_tensor(sq[:, s, :].rearrange("p (a e) -> p a e", a=2), psO[s][:], r.rearrange("p (a e) -> p a e", a=2), ALU.mult).then_inc(s_scaled, 1)
                    dve.wait_ge(s_scaled, b + 3)
                    lg = sq[:, s, :].rearrange("p (e s) -> p e s", e=EXPERTS)
                    dsp = blk(disp, b).rearrange("p (e s) -> p e s", e=EXPERTS)
                    chain(nc.vector.tensor_reduce(gm[:, s], lg, AX.X, ALU.max))
                    chain(nc.vector.tensor_reduce(rm[:, s:s + 1], gm[:, s].squeeze(2), AX.X, ALU.max))
                    chain(nc.vector.tensor_scalar(rm[:, s:s + 1], rm[:, s:s + 1], -1.0, None, ALU.mult))
                    nc.vector.tensor_tensor(dsp, lg, gm[:, s].broadcast_to([P, EXPERTS, SLOTS]), ALU.subtract).then_inc(s_sub, 1)
                    dve.wait_ge(s_exp, b * 2 + 2)
                    dve.nop(nofuse=True)
                    chain(nc.vector.tensor_reduce(gs[:, s], dsp, AX.X, ALU.add))
                    chain(nc.vector.reciprocal(gs[:, s], gs[:, s]))
                    nc.vector.tensor_tensor(dsp, dsp, gs[:, s].broadcast_to([P, EXPERTS, SLOTS]), ALU.mult)
                    chain(nc.vector.reciprocal(rs[:, s:s + 1], rs[:, s:s + 1]))
                    chain(nc.vector.tensor_scalar(blk(comb, b), blk(comb, b), rs[:, s:s + 1], None, ALU.mult))
            chain.end(NB // 2)

        @block.scalar
        def _(act):
            act.sem_inc(s_turn, 2)
            act.sem_inc(s_mm, 2)
            for k in range(KD):
                act.wait_ge(s_w[k], 16)
                if k >= 2:
                    act.wait_ge(s_n, k - 1)
                nc.scalar.activation(sq[:, k % 2, :], ph[:, k, :], ACT.Square).then_inc(s_sq, 1)

            def turn(b, s):
                act.wait_ge(s_turn, b + 1)
                nc.scalar.copy(rows[s][:], blk(R.H, b)).then_inc(s_rows, 1)
                act.wait_ge(s_turn, b + 3)
                act.wait_ge(s_mm, b + 1)
                nc.scalar.copy(rowsT[s][:].rearrange("p (a k) q -> p a (k q)", a=2), psT[s][:, :, 0:HALF]).then_inc(s_turned, 1)

            def exponentials(b, s):
                act.wait_ge(s_sub, b + 1)
                nc.scalar.activation(blk(comb, b), sq[:, s, :], ACT.Exp, bias=rm[:, s:s + 1], accum_out=rs[:, s:s + 1]).then_inc(s_exp, 1)
                nc.scalar.activation(blk(disp, b), blk(disp, b), ACT.Exp).then_inc(s_exp, 1)

            turn(0, 0)
            turn(1, 1)
            act.wait_ge(s_clip, 1)
            nc.scalar.activation(sq[:, 0, :], f[:, 0, :], ACT.Sqrt).then_inc(s_root, 1)
            with act.Fori(0, NB // 2 - 1) as i:
                for s in range(2):
                    turn(i * 2 + s + 2, s)
                    exponentials(i * 2 + s, s)
            for s in range(2):
                exponentials(NB - 2 + s, s)

        @block.tensor
        def _(pe):
            pe.wait_ge(s_v, 1)
            for k in range(KD):
                pe.wait_ge(s_sq, k + 1)
                for a in range(2):
                    last = nc.tensor.matmul(psO[1][:, a, :], ones[:], sq[:, k % 2, a * BANK:(a + 1) * BANK], start=(k == 0), stop=(k == KD - 1))
                last.then_inc(s_n, 1)

            def turn(b, s):
                pe.wait_ge(s_rows, b + 1)
                for k in range(KD):
                    last = nc.tensor.transpose(psT[s][:, k // 3, (k % 3) * P:(k % 3 + 1) * P], rows[s][:, k * P:(k + 1) * P], R.ident[:])
                last.then_inc(s_turn, 1)

            def multiply(b, s):
                pe.wait_ge(s_turned, b + 1)
                pe.wait_ge(s_scaled, b + 1)
                for a in range(2):
                    for k in range(KD):
                        last = nc.tensor.matmul(psO[s][:, a, :], rowsT[s][:, k, :], ph[:, k, a * BANK:(a + 1) * BANK], start=(k == 0), stop=(k == KD - 1))
                last.then_inc(s_mm, 1)

            turn(0, 0)
            with pe.Fori(0, NB // 2 - 1) as i:
                turn(i * 2 + 1, 1)
                multiply(i * 2, 0)
                turn(i * 2 + 2, 0)
                multiply(i * 2 + 1, 1)
            turn(NB - 1, 1)
            multiply(NB - 2, 0)
            multiply(NB - 1, 1)


def soft_slots(nc, R, name, disp, slotsT):
    with Scope(nc, name) as c:
        ps = [c.ps(f"ps{j}", [P, BANK]) for j in range(4)]
        s_mm, s_copy = c.sem("mm"), c.sem("copy")
        block = c.enter_context(nc.Block())

        @block.tensor
        def _(pe):
            for n in range(2 * KD):
                k, a = n // 2, n % 2
                if n >= 4:
                    pe.wait_ge(s_copy, n - 3)
                for b in range(NB):
                    m = P if b < NB - 1 else LAST
                    last = nc.tensor.matmul(ps[n % 4][:], R.H[0:m, b, k * P:(k + 1) * P], disp[0:m, b, a * BANK:(a + 1) * BANK], start=(b == 0), stop=(b == NB - 1))
                last.then_inc(s_mm, 1)

        @block.scalar
        def _(act):
            for n in range(2 * KD):
                act.wait_ge(s_mm, n + 1)
                nc.scalar.copy(slotsT[:, n // 2, n % 2 * BANK:(n % 2 + 1) * BANK], ps[n % 4][:]).then_inc(s_copy, 1)


def soft_experts(nc, R, name, w1, b1, w2, b2, slotsT, eo):
    with Scope(nc, name) as c:
        w1t = [c.sb(f"w1{s}", [P, 2, KD, HID]) for s in range(2)]
        w2t = [c.sb(f"w2{s}", [HC, 2, 2, D]) for s in range(2)]
        b1r, b1t = c.sb("b1r", [EXPERTS, HID]), c.sb("b1t", [HC, 2, EXPERTS])
        b2t = c.sb("b2t", [P, EXPERTS // 4, D])
        hT = c.sb("hT", [HC, 4, 2, SLOTS])
        psB = c.ps("psB", [HC, 2, EXPERTS])
        psH = [c.ps(f"psH{j}", [HC, 2, SLOTS]) for j in range(2)]
        psE = [c.ps(f"psE{j}", [P, 2, BANK]) for j in range(2)]
        s_b, s_bt, s_bc, s_h, s_gelu, s_e, s_out = (c.sem(x) for x in ("b", "bt", "bc", "h", "gelu", "e", "out"))
        s_w1, s_w2, s_free = ([c.sem(f"{x}{s}") for s in range(2)] for x in ("w1", "w2", "free"))
        G = EXPERTS // 4
        block = c.enter_context(nc.Block())

        @block.sync
        def _(sp):
            sp.dma_start(b1r[:], b1).then_inc(s_b, 16)

            def load(g, s):
                sp.wait_ge(s_free[s], g + 1)
                for j in range(2):
                    e = g * 4 + 2 * s + j
                    sp.dma_start(w1t[s][:, j], w1[ds(e, 1)].squeeze(0).rearrange("(k p) h -> p k h", p=P)).then_inc(s_w1[s], 16)
                    sp.dma_start(w2t[s][:, j], w2[ds(e, 1)].squeeze(0).rearrange("(m p) d -> p m d", p=HC)).then_inc(s_w2[s], 16)

            load(0, 0)
            sp.wait_ge(s_w1[0], 32)
            load(0, 1)
            with sp.Fori(0, G - 1) as g:
                for s in range(2):
                    load(g + 1, s)

        @block.scalar
        def _(act):
            for j in range(4):
                act.dma_start(b2t[32 * j:32 * j + 32], b2.rearrange("(g j) d -> j g d", j=4)[j].partition_broadcast(32)).then_inc(s_b, 16)
            act.wait_ge(s_bt, 1)
            nc.scalar.copy(b1t[:], psB[:]).then_inc(s_bc, 1)
            act.wait_ge(s_bc, 1)
            with act.Fori(0, G) as g:
                for j in range(4):
                    act.wait_ge(s_h, g * 4 + j + 1)
                    if j == 0:
                        act.wait_ge(s_e, g + 1)
                    for m in range(2):
                        last = nc.scalar.activation(hT[:, j, m, :], psH[j % 2][:, m, :], ACT.Gelu, bias=b1t[:, m, ds(g * 4 + j, 1)])
                    last.then_inc(s_gelu, 1)

        @block.vector
        def _(dve):
            for s in range(2):
                dve.sem_inc(s_free[s], 1)
            dve.sem_inc(s_e, 1)
            dve.sem_inc(s_out, 2)
            dve.wait_ge(s_b, 80)
            with dve.Fori(0, G // 2) as i:
                for s in range(2):
                    g = i * 2 + s
                    dve.wait_ge(s_e, g + 2)
                    nc.vector.tensor_tensor(blk(eo, g).rearrange("p (a d) -> p a d", a=2), psE[s][:, :, 0:HALF],
                                            blk(b2t, g).rearrange("p (a d) -> p a d", a=2), ALU.add).then_inc(s_out, 1)

        @block.tensor
        def _(pe):
            pe.wait_ge(s_b, 80)
            for m in range(2):
                last = nc.tensor.transpose(psB[:, m, :], b1r[:, m * HC:(m + 1) * HC], R.ident[0:EXPERTS, 0:EXPERTS])
            last.then_inc(s_bt, 1)
            with pe.Fori(0, G // 2) as i:
                for t in range(2):
                    g = i * 2 + t

                    def hidden(j):
                        if j % 2 == 0:
                            pe.wait_ge(s_w1[j // 2], g * 32 + 32)
                        for m in range(2):
                            for k in range(KD):
                                last = nc.tensor.matmul(psH[j % 2][:, m, :], w1t[j // 2][:, j % 2, k, m * HC:(m + 1) * HC],
                                                        slotsT[:, k, ds(g * P + j * SLOTS, SLOTS)], start=(k == 0), stop=(k == KD - 1))
                        last.then_inc(s_h, 1)

                    def outer(j):
                        if j == 0:
                            pe.wait_ge(s_out, g + 1)
                        if j % 2 == 0:
                            pe.wait_ge(s_w2[j // 2], g * 32 + 32)
                        pe.wait_ge(s_gelu, g * 4 + j + 1)
                        for a in range(2):
                            for m in range(2):
                                last = nc.tensor.matmul(psE[t][32 * j:32 * j + 32, a, 0:HALF], hT[:, j, m, :], w2t[j // 2][:, j % 2, m, a * HALF:(a + 1) * HALF],
                                                        start=(m == 0), stop=(m == 1))
                        if j % 2:
                            last.then_inc(s_free[j // 2], 1)

                    hidden(0)
                    hidden(1)
                    outer(0)
                    outer(1)
                    hidden(2)
                    hidden(3)
                    outer(2)
                    outer(3)
                    pe.wait_ge(s_free[1], g + 2)
                    pe.sem_inc(s_e, 1)


def soft_combine(nc, R, name, comb, eo):
    with Scope(nc, name) as c:
        rows = [c.sb(f"rows{s}", [P, SE]) for s in range(2)]
        rowsT = [c.sb(f"rowsT{s}", [P, KS, P]) for s in range(2)]
        psT = [c.ps(f"psT{s}", [P, 2, BANK]) for s in range(2)]
        psO = [c.ps(f"psO{s}", [P, 2, BANK]) for s in range(2)]
        s_rows, s_turn, s_turned, s_mm, s_add = (c.sem(x) for x in ("rows", "turn", "turned", "mm", "add"))
        block = c.enter_context(nc.Block())

        @block.scalar
        def _(act):
            act.sem_inc(s_turn, 2)
            act.sem_inc(s_mm, 2)
            with act.Fori(0, NB // 2) as i:
                for s in range(2):
                    b = i * 2 + s
                    act.wait_ge(s_turn, b + 1)
                    nc.scalar.copy(rows[s][:], blk(comb, b)).then_inc(s_rows, 1)
                    act.wait_ge(s_turn, b + 3)
                    act.wait_ge(s_mm, b + 1)
                    nc.scalar.copy(rowsT[s][:].rearrange("p (a k) q -> p a (k q)", a=2), psT[s][:]).then_inc(s_turned, 1)

        @block.vector
        def _(dve):
            dve.sem_inc(s_add, 2)
            with dve.Fori(0, NB // 2) as i:
                for s in range(2):
                    b = i * 2 + s
                    dve.wait_ge(s_mm, b + 3)
                    x = blk(R.X, b).rearrange("p (a d) -> p a d", a=2)
                    nc.vector.tensor_tensor(x, x, psO[s][:, :, 0:HALF], ALU.add).then_inc(s_add, 1)

        @block.tensor
        def _(pe):
            def turn(b, s):
                pe.wait_ge(s_rows, b + 1)
                for k in range(KS):
                    last = nc.tensor.transpose(psT[s][:, k // 4, (k % 4) * P:(k % 4 + 1) * P], rows[s][:, k * P:(k + 1) * P], R.ident[:])
                last.then_inc(s_turn, 1)

            def multiply(b, s):
                pe.wait_ge(s_add, b + 1)
                pe.wait_ge(s_turned, b + 1)
                for a in range(2):
                    for k in range(KS):
                        last = nc.tensor.matmul(psO[s][:, a, 0:HALF], rowsT[s][:, k, :], eo[:, k, a * HALF:(a + 1) * HALF], start=(k == 0), stop=(k == KS - 1))
                last.then_inc(s_mm, 1)

            turn(0, 0)
            with pe.Fori(0, NB // 2 - 1) as i:
                turn(i * 2 + 1, 1)
                multiply(i * 2, 0)
                turn(i * 2 + 2, 0)
                multiply(i * 2 + 1, 1)
            turn(NB - 1, 1)
            multiply(NB - 2, 0)
            multiply(NB - 1, 1)


def edge_counts(nc, R, name):
    BY_ACT = 2
    PAIRS = WIDE_VISITS // 2
    with Scope(nc, name) as c:
        nodes = c.sb("nodes", [P, ROWS], F16)
        srcf, minus = c.sb("src", [P, TILES]), c.sb("minus", [P, TILES])
        one = c.sb("one", [P, 1])
        away = c.sb("away", [P, 2, BY_ACT, ROWS], F16)
        pick = c.sb("pick", [P, 2, WIDE, ROWS], BF16)
        sel = c.sb("sel", [P, 2, WIDE, P], BF16)
        psC = [c.ps(f"psC{s}", [P, 3 * BANK]) for s in range(2)]
        s_v, s_zero, s_cast, s_sel, s_pick, s_mm, s_add = (c.sem(x) for x in ("v", "zero", "cast", "sel", "pick", "mm", "add"))
        s_minus, s_away = c.sem("minus"), c.sem("away")
        block = c.enter_context(nc.Block())

        def visits(eng, one):
            with eng.Fori(0, PAIRS) as i:
                for s in range(2):
                    one(i, s)
            if WIDE_VISITS % 2:
                one(PAIRS, 0)

        @block.gpsimd
        def _(pool):
            nc.gpsimd.memset(R.CT[:], 0.0).then_inc(s_zero, 1)

        @block.scalar
        def _(act):
            act.wait_ge(s_cast, 1)
            nc.scalar.mul(minus[:], srcf[:], -1.0).then_inc(s_minus, 1)
            act.wait_ge(s_minus, 1)

            def make(i, s):
                v = i * 2 + s
                grp = act.value_load(R.wide_group[0:1, ds(v, 1)], min_val=0, max_val=WIDE_GROUPS - 1)
                act.wait_ge(s_mm, v + 1)
                for n in range(BY_ACT):
                    k = WIDE - BY_ACT + n
                    nc.scalar.activation(away[:, s, n, :], nodes[:], ACT.Abs, bias=minus[:, ds(grp * WIDE + k, 1)]).then_inc(s_away, 1)
                for n in range(BY_ACT):
                    act.wait_ge(s_away, v * BY_ACT + n + 1)
                    last = nc.scalar.activation(pick[:, s, WIDE - BY_ACT + n, :], away[:, s, n, :], ACT.Relu, scale=-1.0, bias=one[:])
                last.then_inc(s_pick, 1)

            visits(act, make)

        @block.vector
        def _(dve):
            chain = Chain(dve, s_v)
            chain(nc.vector.memset(one[:], 1.0))
            chain(nc.vector.tensor_copy(nodes[:], R.nodes[:]))
            chain(nc.vector.tensor_copy(srcf[:], R.src[:]))
            dve.sem_inc(s_cast, 1)
            dve.sem_inc(s_mm, 2)
            dve.sem_inc(s_add, 2)

            def make(i, s):
                v = i * 2 + s
                grp = dve.value_load(R.wide_group[0:1, ds(v, 1)], min_val=0, max_val=WIDE_GROUPS - 1)
                blk_ = dve.value_load(R.wide_block[0:1, ds(v, 1)], min_val=0, max_val=NB - 1)
                dve.wait_ge(s_mm, v + 1)
                nc.vector.tensor_tensor(sel[:, s], bcast(R.nodes[:, ds(blk_ * P, P)], 1, WIDE), bcast(R.dst[:, ds(grp * WIDE, WIDE)], 2, P), ALU.is_equal)
                for k in range(WIDE - BY_ACT):
                    last = nc.vector.tensor_scalar(pick[:, s, k, :], nodes[:], srcf[:, ds(grp * WIDE + k, 1)], None, ALU.is_equal)
                last.then_inc(s_sel, 1)

            def add(i, s):
                v = i * 2 + s
                blk_ = dve.value_load(R.wide_block[0:1, ds(v, 1)], min_val=0, max_val=NB - 1)
                dve.wait_ge(s_mm, v + 3)
                dve.wait_ge(s_add, v + 2)
                cols = R.CT[:, :, ds(blk_ * P, P)]
                nc.vector.tensor_tensor(cols, cols, psC[s][:, 0:ROWS].rearrange("p (c i) -> p c i", c=NB), ALU.add).then_inc(s_add, 1)

            make(0, 0)
            dve.wait_ge(s_zero, 1)
            whole = (WIDE_VISITS - 1) // 2
            with dve.Fori(0, whole) as i:
                make(i, 1)
                add(i, 0)
                make(i + 1, 0)
                add(i, 1)
            if WIDE_VISITS % 2 == 0:
                make(whole, 1)
            add(whole, 0)
            if WIDE_VISITS % 2 == 0:
                add(whole, 1)
            dve.wait_ge(s_add, WIDE_VISITS + 2)
            for b in range(NB):
                own = R.CT[:, b, b * P:(b + 1) * P]
                nc.vector.tensor_tensor(own, own, R.ident[:], ALU.add)

        @block.tensor
        def _(pe):
            def multiply(i, s):
                v = i * 2 + s
                pe.wait_ge(s_add, v + 1)
                pe.wait_ge(s_sel, v + 1)
                pe.wait_ge(s_pick, v + 1)
                for b in range(NB):
                    for k in range(WIDE):
                        last = nc.tensor.matmul(psC[s][:, b * P:(b + 1) * P], pick[:, s, k, b * P:(b + 1) * P], sel[:, s, k, :],
                                                start=(k == 0), stop=(k == WIDE - 1))
                last.then_inc(s_mm, 1)

            visits(pe, multiply)


def gcn_layer(nc, R, name, rows, weight, bias, first):
    CH = 2 * P
    with Scope(nc, name) as c:
        w, bs = c.sb("w", [P, KD, D]), c.sb("bias", [P, D])
        sumT = [c.sb(f"sumT{s}", [P, KD, CH]) for s in range(2)]
        y = c.sb("y", [P, 2, HALF])
        psY = [c.ps(f"psY{s}", [P, KD // 2, BANK]) for s in range(2)]
        psO = c.ps("psO", [P, 2, BANK])
        s_w, s_b, s_rows, s_mix, s_copied, s_mm, s_taken, s_y = (c.sem(x) for x in ("weights", "bias", "rows", "mix", "copied", "mm", "taken", "y"))
        block = c.enter_context(nc.Block())

        @block.sync
        def _(sp):
            sp.dma_start(w[:], weight.rearrange("(k p) d -> p k d", p=P)).then_inc(s_w, 16)
            sp.dma_start(bs[:], bias.partition_broadcast(P)).then_inc(s_b, 16)

        @block.scalar
        def _(act):
            def copy(c_, s):
                act.wait_ge(s_mm, c_ * 4 + 4)
                for a in range(KD // 2):
                    act.wait_ge(s_mix, c_ * 3 + a + 1)
                    nc.scalar.copy(sumT[s][:, 2 * a:2 * a + 2, :].rearrange("p k i -> p (k i)"), psY[s][:, a, :]).then_inc(s_copied, 1)

            copy(0, 0)
            with act.Fori(0, NB // 4) as i:
                copy(i * 2 + 1, 1)
                copy(i * 2 + 2, 0)

        @block.vector
        def _(dve):
            dve.sem_inc(s_mm, 8)
            dve.sem_inc(s_copied, 6)
            dve.sem_inc(s_taken, 2)
            if first:
                for b in range(NB):
                    nc.vector.tensor_scalar(rows[:, b, :], rows[:, b, :], R.dinv[:, b:b + 1], None, ALU.mult).then_inc(s_rows, 1)
            dve.wait_ge(s_b, 16)
            with dve.Fori(0, NB) as b:
                for a in range(2):
                    cut = slice(a * HALF, (a + 1) * HALF)
                    dve.wait_ge(s_mm, b * 2 + a + 9)
                    nc.vector.scalar_tensor_tensor(out=y[:, a, :], in0=psO[:, a, 0:HALF], scalar=R.dinv[:, ds(b, 1)], in1=bs[:, cut],
                                                   op0=ALU.mult, op1=ALU.add).then_inc(s_taken, 1)
                    dve.wait_ge(s_taken, b * 2 + a + 3)
                    if first:
                        nc.vector.tensor_scalar(R.out[:, ds(b, 1), cut].squeeze(1), y[:, a, :], 0.0, R.dinv[:, ds(b, 1)], ALU.max, ALU.mult).then_inc(s_y, 1)
                    else:
                        xb = R.X[:, ds(b, 1), cut].squeeze(1)
                        nc.vector.tensor_tensor(xb, xb, y[:, a, :], ALU.add).then_inc(s_y, 1)
            dve.wait_ge(s_y, 2 * NB)

        @block.tensor
        def _(pe):
            def mix(c_, s, start=False):
                pe.wait_ge(s_copied, c_ * 3 + 3)
                for k in range(KD):
                    for b in range(NB):
                        if start and k == 0:
                            pe.wait_ge(s_rows, b + 1)
                        last = nc.tensor.matmul(psY[s][:, k // 2, (k % 2) * CH:(k % 2 + 1) * CH], rows[:, b, k * P:(k + 1) * P],
                                                R.CT[:, b, ds(c_ * CH, CH)], start=(b == 0), stop=(b == NB - 1))
                    if k % 2:
                        last.then_inc(s_mix, 1)

            def multiply(c_, s):
                pe.wait_ge(s_copied, c_ * 3 + 9)
                for q in range(2):
                    for a in range(2):
                        pe.wait_ge(s_taken, c_ * 4 + q * 2 + a + 1)
                        for k in range(KD):
                            last = nc.tensor.matmul(psO[:, a, 0:HALF], sumT[s][:, k, q * P:(q + 1) * P], w[:, k, a * HALF:(a + 1) * HALF],
                                                    start=(k == 0), stop=(k == KD - 1))
                        last.then_inc(s_mm, 1)

            mix(0, 0, first)
            pe.wait_ge(s_w, 16)
            with pe.Fori(0, NB // 4) as i:
                mix(i * 2 + 1, 1)
                multiply(i * 2, 0)
                mix(i * 2 + 2, 0)
                multiply(i * 2 + 1, 1)
            multiply(NB // 2 - 1, 0)


ME, MHID, TOP = 8, 1152, 2
MB = (TOP * NODES - ME) // P + ME
MSLOTS = MB * P
KH = MHID // P
SPARE = MSLOTS + TOP * P


def route(nc, R, name, wr, br, rows_table, slot_table):
    with Scope(nc, name) as c:
        w, bias, one = c.sb("w", [P, KD, ME]), c.sb("bias", [1, ME]), c.sb("one", [1, P])
        rows = [c.sb(f"rows{s}", [P, D]) for s in range(2)]
        rowsT = [c.sb(f"rowsT{s}", [P, KD, P]) for s in range(2)]
        pr, best = c.sb("probs", [P, NB, ME]), c.sb("best", [P, NB, ME])
        which, whichf = c.sb("which", [P, NB, ME], U32), c.sb("whichf", [P, NB, TOP])
        red = c.sb("red", [P, NB, 1])
        eight, rown, valid = c.sb("eight", [P, ME]), c.sb("rown", [P, NB]), c.sb("valid", [P, NB])
        spare, tri, ones = c.sb("spare", [P, NB, TOP]), c.sb("tri", [P, P]), c.sb("ones", [P, P])
        hot, member = c.sb("hot", [P, NB, TOP, ME]), c.sb("member", [P, NB, ME])
        off = c.sb("off", [P, NB + 1, ME])
        blocks, blocksi = c.sb("blocks", [P, ME]), c.sb("blocksi", [P, ME], I32)
        start = c.sb("start", [P, ME + 1])
        place, placed = c.sb("place", [P, NB, ME]), c.sb("placed", [P, NB, TOP, ME])
        slotf = c.sb("slotf", [P, NB, TOP, 1])
        nodei, none = c.sb("nodei", [P, NB], I32), c.sb("none", [P, SPARE // P], I32)
        mb, ends, exf = c.sb("mb", [1, MB]), c.sb("ends", [1, MB, ME]), c.sb("exf", [1, MB])
        fresh = c.sb("fresh", [1, MB])
        psT = [c.ps(f"psT{s}", [P, 2, BANK]) for s in range(2)]
        psL = [c.ps(f"psL{s}", [P, BANK]) for s in range(2)]
        psC = c.ps("psC", [P, 2, NB, ME])
        s_w, s_v, s_c, s_rows, s_turn, s_turned, s_mm = (c.sem(x) for x in ("weights", "v", "consts", "rows", "turn", "turned", "mm"))
        s_logit, s_sub, s_exp, s_member, s_rank, s_slot, s_st, s_init, s_sc, s_ld = (
            c.sem(x) for x in ("logit", "sub", "exp", "member", "rank", "slot", "st", "init", "sc", "ld"))
        block = c.enter_context(nc.Block())

        @block.sync
        def _(sp):
            sp.dma_start(w[:], wr.rearrange("(k p) e -> p k e", p=P)).then_inc(s_w, 16)
            sp.dma_start(bias[:], br.rearrange("(o e) -> o e", o=1)).then_inc(s_w, 16)
            sp.dma_start(rows_table.rearrange("(b p) d -> p b d", p=P), R.H[:]).then_inc(s_st, 16)
            sp.wait_ge(s_c, 7)
            sp.dma_start(slot_table.rearrange("(p j) o -> p (j o)", p=P), none[:]).then_inc(s_init, 16)
            sp.wait_ge(s_sc, 16 * TOP * NB)
            sp.dma_start(R.slot_node[:], slot_table[0:MSLOTS, :].rearrange("(j p) o -> p (j o)", p=P), allow_slow_non_contiguous=True).then_inc(s_ld, 16)
            sp.wait_ge(s_ld, 16)
            sp.wait_ge(s_st, 16)

        @block.gpsimd
        def _(pool):
            lax = dict(allow_small_or_imprecise_dtypes=True)
            nc.gpsimd.iota(eight[:], [[1, ME]], 0, 0, **lax).then_inc(s_c, 1)
            nc.gpsimd.iota(rown[:], [[P, NB]], 0, 1, **lax).then_inc(s_c, 1)
            nc.gpsimd.iota(nodei[:], [[P, NB]], 0, 1).then_inc(s_c, 1)
            nc.gpsimd.iota(spare[:], [[0, NB], [1, TOP]], MSLOTS, TOP, **lax).then_inc(s_c, 1)
            nc.gpsimd.iota(mb[:], [[1, MB]], 0, 0, **lax).then_inc(s_c, 1)
            nc.gpsimd.memset(ones[:], 1.0).then_inc(s_c, 1)
            nc.gpsimd.memset(none[:], ROWS - 1).then_inc(s_c, 1)
            pool.wait_ge(s_c, 7)
            nc.gpsimd.affine_select(out=tri[:], in_=ones[:], compare_op=ALU.is_gt, fill=0.0, base=0, pattern=[[1, P]], channel_multiplier=-1).then_inc(s_c, 1)
            pool.wait_ge(s_init, 16)
            pool.wait_ge(s_slot, 1)
            for b in range(NB):
                for k in range(TOP):
                    nc.gpsimd.indirect_dma_start(out=slot_table, out_offset=bass.IndirectOffsetOnAxis(ap=R.slot[:, b, k:k + 1], axis=0),
                                                 in_=nodei[:, b:b + 1], in_offset=None).then_inc(s_sc, 16)

        @block.scalar
        def _(act):
            act.sem_inc(s_turn, 2)
            with act.Fori(0, NB // 2) as i:
                for s in range(2):
                    b = i * 2 + s
                    act.wait_ge(s_turn, b + 1)
                    nc.scalar.copy(rows[s][:], blk(R.H, b)).then_inc(s_rows, 1)
            act.wait_ge(s_sub, 1)
            nc.scalar.activation(pr[:], pr[:], ACT.Exp).then_inc(s_exp, 1)

        @block.vector
        def _(dve):
            chain = Chain(dve, s_v)
            dve.sem_inc(s_mm, 2)
            chain(nc.vector.memset(one[:], 1.0))
            dve.sem_inc(s_logit, 2)

            def turned(b, s):
                dve.wait_ge(s_turn, b + 3)
                dve.wait_ge(s_mm, b + 1)
                nc.vector.tensor_copy(rowsT[s][:].rearrange("p (a k) q -> p a (k q)", a=2), psT[s][:, :, 0:HALF]).then_inc(s_turned, 1)

            def logit(b, s):
                dve.wait_ge(s_mm, b + 3)
                nc.vector.tensor_copy(blk(pr, b), psL[s][:, 0:ME]).then_inc(s_logit, 1)

            turned(0, 0)
            with dve.Fori(0, NB // 2 - 1) as i:
                turned(i * 2 + 1, 1)
                logit(i * 2, 0)
                turned(i * 2 + 2, 0)
                logit(i * 2 + 1, 1)
            turned(NB - 1, 1)
            logit(NB - 2, 0)
            logit(NB - 1, 1)
            dve.wait_ge(s_logit, NB + 2)
            chain(nc.vector.tensor_reduce(red[:], pr[:], AX.X, ALU.max))
            chain(nc.vector.tensor_tensor(pr[:], pr[:], red[:].broadcast_to([P, NB, ME]), ALU.subtract))
            dve.sem_inc(s_sub, 1)
            dve.wait_ge(s_exp, 1)
            chain(nc.vector.tensor_reduce(red[:], pr[:], AX.X, ALU.add))
            chain(nc.vector.reciprocal(red[:], red[:]))
            chain(nc.vector.tensor_tensor(pr[:], pr[:], red[:].broadcast_to([P, NB, ME]), ALU.mult))
            for b in range(NB):
                last = nc.vector.max(best[:, b, :], pr[:, b, :])
            chain(last)
            for b in range(NB):
                last = nc.vector.max_index(which[:, b, :], best[:, b, :], pr[:, b, :])
            chain(last)
            nc.vector.tensor_copy(R.gate[:], best[:, :, 0:TOP])
            chain(nc.vector.tensor_copy(whichf[:], which[:, :, 0:TOP]))
            dve.wait_ge(s_c, 8)
            chain(nc.vector.tensor_scalar(valid[:], rown[:], float(NODES), None, ALU.is_lt))
            for k in range(TOP):
                last = nc.vector.tensor_tensor(hot[:, :, k, :], bcast(whichf[:, :, k], 2, ME), bcast(eight[:], 1, NB), ALU.is_equal)
            chain(last)
            chain(nc.vector.tensor_tensor(member[:], hot[:, :, 0, :], hot[:, :, 1, :], ALU.add))
            chain(nc.vector.tensor_tensor(member[:], member[:], bcast(valid[:], 2, ME), ALU.mult))
            dve.sem_inc(s_member, 1)
            dve.wait_ge(s_rank, 1)
            chain(nc.vector.memset(off[:, 0, :], 0.0))
            for b in range(NB):
                chain(nc.vector.tensor_tensor(off[:, b + 1, :], off[:, b, :], psC[:, 1, b, :], ALU.add))
            chain(nc.vector.tensor_scalar(blocks[:], off[:, NB, :], float(P - 1), None, ALU.add))
            chain(nc.vector.tensor_copy(blocksi[:], blocks[:]))
            chain(nc.vector.tensor_single_scalar(blocksi[:], blocksi[:], 7, ALU.arith_shift_right))
            chain(nc.vector.tensor_copy(blocks[:], blocksi[:]))
            chain(nc.vector.memset(start[:, 0:1], 0.0))
            for e in range(ME):
                chain(nc.vector.tensor_tensor(start[:, e + 1:e + 2], start[:, e:e + 1], blocks[:, e:e + 1], ALU.add))
            chain(nc.vector.tensor_tensor(place[:], off[:, 0:NB, :], psC[:, 0], ALU.add))
            chain(nc.vector.tensor_scalar(blocks[:], start[:, 0:ME], float(P), None, ALU.mult))
            chain(nc.vector.tensor_tensor(place[:], place[:], bcast(blocks[:], 1, NB), ALU.add))
            for k in range(TOP):
                last = nc.vector.tensor_tensor(placed[:, :, k, :], hot[:, :, k, :], place[:], ALU.mult)
            chain(last)
            chain(nc.vector.tensor_reduce(slotf[:], placed[:], AX.X, ALU.add))
            sf = slotf[:].squeeze(3)
            chain(nc.vector.tensor_tensor(sf, sf, spare[:], ALU.subtract))
            chain(nc.vector.tensor_tensor(sf, sf, bcast(valid[:], 2, TOP), ALU.mult))
            chain(nc.vector.tensor_tensor(sf, sf, spare[:], ALU.add))
            chain(nc.vector.tensor_copy(R.slot[:], sf))
            dve.sem_inc(s_slot, 1)
            chain(nc.vector.tensor_tensor(ends[:], bcast(start[0:1, 1:ME + 1], 1, MB), bcast(mb[:], 2, ME), ALU.is_le))
            chain(nc.vector.reduce_sum(exf[:], ends[:], AX.X))
            chain(nc.vector.tensor_scalar(exf[:], exf[:], float(ME - 1), None, ALU.min))
            chain(nc.vector.tensor_copy(R.block_expert[:], exf[:]))
            chain(nc.vector.memset(fresh[:, 0:2], 1.0))
            chain(nc.vector.tensor_tensor(fresh[:, 2:MB], exf[:, 2:MB], exf[:, 0:MB - 2], ALU.not_equal))
            chain(nc.vector.tensor_copy(R.block_fresh[:], fresh[:]))

        @block.tensor
        def _(pe):
            pe.wait_ge(s_w, 32)
            pe.wait_ge(s_v, 1)

            def turn(b, s):
                pe.wait_ge(s_rows, b + 1)
                for k in range(KD):
                    last = nc.tensor.transpose(psT[s][:, k // 3, (k % 3) * P:(k % 3 + 1) * P], rows[s][:, k * P:(k + 1) * P], R.ident[:])
                last.then_inc(s_turn, 1)

            def multiply(b, s):
                pe.wait_ge(s_turned, b + 1)
                pe.wait_ge(s_logit, b + 1)
                for k in range(KD):
                    nc.tensor.matmul(psL[s][:, 0:ME], rowsT[s][:, k, :], w[:, k, :], start=(k == 0), stop=False)
                nc.tensor.matmul(psL[s][:, 0:ME], one[:], bias[:], start=False, stop=True).then_inc(s_mm, 1)

            turn(0, 0)
            with pe.Fori(0, NB // 2 - 1) as i:
                turn(i * 2 + 1, 1)
                multiply(i * 2, 0)
                turn(i * 2 + 2, 0)
                multiply(i * 2 + 1, 1)
            turn(NB - 1, 1)
            multiply(NB - 2, 0)
            multiply(NB - 1, 1)
            pe.wait_ge(s_member, 1)
            m = member[:].rearrange("p b e -> p (b e)")
            nc.tensor.matmul(psC[:, 0].rearrange("p b e -> p (b e)"), tri[:], m, start=True, stop=True)
            nc.tensor.matmul(psC[:, 1].rearrange("p b e -> p (b e)"), ones[:], m, start=True, stop=True).then_inc(s_rank, 1)


def experts(nc, R, name, rows_table, w1, b1, w2, b2, out_table):
    with Scope(nc, name) as c:
        w1t = [c.sb(f"w1{s}", [P, KD, MHID]) for s in range(2)]
        w2t = [c.sb(f"w2{s}", [P, KH, D]) for s in range(2)]
        b1r, b1t = c.sb("b1r", [ME, MHID]), c.sb("b1t", [P, KH, ME])
        rows = [R.H[:, s, :] for s in range(2)]
        y = [R.H[:, 2 + s, :] for s in range(2)]
        b2t = [R.H[:, 4 + s, :] for s in range(2)]
        rowsT = [c.sb(f"rowsT{s}", [P, KD, P]) for s in range(2)]
        hT = [c.sb(f"hT{s}", [P, KH, P]) for s in range(2)]
        psT = c.ps("psT", [P, 2, BANK])
        psH = [c.ps(f"psH{j}", [P, BANK]) for j in range(4)]
        psY = c.ps("psY", [P, 2, BANK])
        s_b, s_bt, s_bc, s_turn, s_turned, s_h, s_gelu, s_y, s_add = (c.sem(x) for x in ("b", "bt", "bc", "turn", "turned", "h", "gelu", "y", "add"))
        s_w1, s_w2, s_b2, s_rows, s_st = ([c.sem(f"{x}{s}") for s in range(2)] for x in ("w1", "w2", "b2", "rows", "st"))
        block = c.enter_context(nc.Block())
        PAIRS = MB // 2
        assert MB % 2

        def blocks(eng, one, last=None):
            with eng.Fori(0, PAIRS) as i:
                for s in range(2):
                    one(i, s)
            (last or one)(PAIRS, 0)

        @block.sync
        def _(sp):
            sp.dma_start(b1r[:], b1).then_inc(s_b, 16)

            def load(i, s, first=False):
                j = i * 2 + s
                e = sp.value_load(R.block_expert[0:1, ds(j, 1)], min_val=0, max_val=ME - 1)
                fresh = sp.value_load(R.block_fresh[0:1, ds(j, 1)], min_val=0, max_val=1)
                sp.wait_ge(s_h, j * KH + KH)
                sp.dma_start(w1t[s][:], w1[ds(e, 1)].squeeze(0).rearrange("(k p) h -> p k h", p=P), cond=fresh, cond_hint=True).then_inc(s_w1[s], 16)
                if first:
                    sp.wait_ge(s_w1[0], 16)
                sp.wait_ge(s_add, j + 1)
                sp.dma_start(w2t[s][:], w2[ds(e, 1)].squeeze(0).rearrange("(k p) d -> p k d", p=P), cond=fresh, cond_hint=True).then_inc(s_w2[s], 16)
                sp.dma_start(b2t[s], b2[ds(e, 1)].squeeze(0).partition_broadcast(P)).then_inc(s_b2[s], 16)

            def store(i, s):
                sp.wait_ge(s_add, i * 2 + s + 3)
                sp.dma_start(out_table[ds((i * 2 + s) * P, P), :], y[s]).then_inc(s_st[s], 16)

            load(0, 0, first=True)
            sp.wait_ge(s_w2[0], 16)
            load(0, 1)
            with sp.Fori(0, PAIRS - 1) as i:
                for s in range(2):
                    store(i, s)
                    load(i + 1, s)
            store(PAIRS - 1, 0)
            load(PAIRS, 0)
            store(PAIRS - 1, 1)
            store(PAIRS, 0)
            for s in range(2):
                sp.wait_ge(s_st[s], 16 * (1 + PAIRS + (1 - s)))

        @block.gpsimd
        def _(pool):
            def gather(i, s):
                pool.wait_ge(s_turn, i * 2 + s + 1)
                nc.gpsimd.tensor_copy(R.list[:, s:s + 1], R.slot_node[:, ds(i * 2 + s, 1)]).then_inc(s_bc, 1)
                pool.wait_ge(s_bc, i * 2 + s + 1)
                pool.nop(nofuse=True)
                nc.gpsimd.indirect_dma_start(out=rows[s], out_offset=None, in_=rows_table,
                                             in_offset=bass.IndirectOffsetOnAxis(ap=R.list[:, s:s + 1], axis=0)).then_inc(s_rows[s], 16)

            blocks(pool, gather)

        @block.scalar
        def _(act):
            act.wait_ge(s_bt, 1)
            nc.scalar.copy(b1t[:], psY[:, 0, 0:KH * ME].rearrange("p (k e) -> p k e", e=ME)).then_inc(s_b, 1)
            act.wait_ge(s_b, 17)

            def gelus(i, s):
                j = i * 2 + s
                e = act.value_load(R.block_expert[0:1, ds(j, 1)], min_val=0, max_val=ME - 1)
                act.wait_ge(s_y, j + 1)
                for m in range(KH):
                    act.wait_ge(s_h, (j + 2) * KH + m + 1)
                    nc.scalar.activation(hT[s][:, m, :], psH[m % 4][:, 0:P], ACT.Gelu, bias=b1t[:, m, ds(e, 1)]).then_inc(s_gelu, 1)

            blocks(act, gelus)

        @block.vector
        def _(dve):
            dve.sem_inc(s_turn, 2)
            dve.sem_inc(s_h, 2 * KH)
            dve.sem_inc(s_y, 2)
            dve.sem_inc(s_add, 2)
            for s in range(2):
                dve.sem_inc(s_st[s], 16)

            def turned(j, s):
                dve.wait_ge(s_turn, j + 3)
                nc.vector.tensor_copy(rowsT[s][:].rearrange("p (a k) q -> p a (k q)", a=2), psT[:, :, 0:HALF]).then_inc(s_turned, 1)

            def finish(i, s):
                j = i * 2 + s
                dve.wait_ge(s_y, j + 3)
                dve.wait_ge(s_b2[s], i * 16 + 16)
                dve.wait_ge(s_st[s], i * 16 + 16)
                nc.vector.tensor_tensor(y[s].rearrange("p (a d) -> p a d", a=2), psY[:, :, 0:HALF], b2t[s].rearrange("p (a d) -> p a d", a=2), ALU.add).then_inc(s_add, 1)

            def both(i, s):
                turned(i * 2 + s + 1, 1 - s)
                finish(i, s)

            turned(0, 0)
            blocks(dve, both, finish)

        @block.tensor
        def _(pe):
            pe.wait_ge(s_b, 16)
            for k in range(KH):
                last = nc.tensor.transpose(psY[:, 0, k * ME:(k + 1) * ME], b1r[:, k * P:(k + 1) * P], R.ident[0:ME, 0:ME])
            last.then_inc(s_bt, 1)
            pe.wait_ge(s_b, 17)

            def turn(j, s):
                pe.wait_ge(s_rows[s], (j - s) * 8 + 16)
                for k in range(KD):
                    last = nc.tensor.transpose(psT[:, k // 3, (k % 3) * P:(k % 3 + 1) * P], rows[s][:, k * P:(k + 1) * P], R.ident[:])
                last.then_inc(s_turn, 1)

            def one(i, s, last_one=False):
                j = i * 2 + s
                pe.wait_ge(s_turned, j + 1)
                pe.wait_ge(s_w1[s], i * 16 + 16)
                for m in range(KH):
                    if m >= 4:
                        pe.wait_ge(s_gelu, j * KH + m - 3)
                    for k in range(KD):
                        last = nc.tensor.matmul(psH[m % 4][:, 0:P], w1t[s][:, k, m * P:(m + 1) * P], rowsT[s][:, k, :],
                                                start=(k == 0), stop=(k == KD - 1))
                    last.then_inc(s_h, 1)
                if not last_one:
                    turn(j + 1, 1 - s)
                pe.wait_ge(s_w2[s], i * 16 + 16)
                pe.wait_ge(s_add, j + 2)
                for m in range(KH):
                    pe.wait_ge(s_gelu, j * KH + m + 1)
                    for a in range(2):
                        last = nc.tensor.matmul(psY[:, a, 0:HALF], hT[s][:, m, :], w2t[s][:, m, a * HALF:(a + 1) * HALF], start=(m == 0), stop=(m == KH - 1))
                last.then_inc(s_y, 1)

            turn(0, 0)
            blocks(pe, one, lambda i, s: one(i, s, last_one=True))


def combine(nc, R, name, out_table, out):
    with Scope(nc, name) as c:
        g = [[R.H[:, 2 * s + k, :] for k in range(TOP)] for s in range(4)]
        s_v, s_done, s_st = c.sem("v"), c.sem("done"), c.sem("st")
        s_g = [c.sem(f"g{s}") for s in range(4)]
        block = c.enter_context(nc.Block())

        @block.gpsimd
        def _(pool):
            for b in range(NB):
                if b >= 4:
                    pool.wait_ge(s_done, b - 3)
                m = P if b < NB - 1 else LAST
                for k in range(TOP):
                    nc.gpsimd.indirect_dma_start(out=g[b % 4][k][0:m], out_offset=None, in_=out_table,
                                                 in_offset=bass.IndirectOffsetOnAxis(ap=R.slot[0:m, b, k:k + 1], axis=0)).then_inc(s_g[b % 4], 16)

        @block.vector
        def _(dve):
            chain = Chain(dve, s_v)
            for b in range(NB):
                dve.wait_ge(s_g[b % 4], 32 * (b // 4 + 1))
                m = P if b < NB - 1 else LAST
                x = R.X[0:m, b, :]
                chain(nc.vector.scalar_tensor_tensor(out=x, in0=g[b % 4][0][0:m], scalar=R.gate[0:m, b, 0:1], in1=x, op0=ALU.mult, op1=ALU.add))
                nc.vector.scalar_tensor_tensor(out=x, in0=g[b % 4][1][0:m], scalar=R.gate[0:m, b, 1:2], in1=x, op0=ALU.mult, op1=ALU.add).then_inc(s_done, 1)

        @block.sync
        def _(sp):
            for b in range(NB):
                m = P if b < NB - 1 else LAST
                sp.wait_ge(s_done, b + 1)
                sp.dma_start(out[b * P:b * P + m, :], R.X[0:m, b, :]).then_inc(s_st, 16)
            sp.wait_ge(s_st, 16 * NB)


def program(nc, A, out):
    with ExitStack() as ctx:
        def sb(name, shape, dt=F32):
            return ctx.enter_context(nc.sbuf_tensor(name, shape, dt))

        class R:
            pass

        R.ident = sb("ident", [P, P])
        R.nodes = sb("nodes", [P, ROWS])
        R.X = sb("X", [P, NB, D])
        R.H = sb("H", [P, NB, D])
        R.src = sb("src", [P, TILES], I32)
        R.dst_block = sb("dst_block", [P, TILES])
        R.dst = sb("dst", [P, TILES])
        R.ends = sb("ends", [QT, 1, 4, P + 2])
        R.visit_group = sb("visit_group", [1, VISITS], I32)
        R.visit_block = sb("visit_block", [1, VISITS], I32)
        R.wide_group, R.wide_block = sb("wide_group", [1, WIDE_VISITS], I32), sb("wide_block", [1, WIDE_VISITS], I32)
        R.visit_minus, R.visit_row = sb("visit_minus", [P, VISITS]), sb("visit_row", [P, VISITS])
        R.dinv = sb("dinv", [P, NB])
        R.dst_rows = nc.dram_tensor("dst_rows", (TILES // UN, UN * P), F32, kind="Internal").ap()

        def table(name, width, rows=ROWS):
            return nc.dram_tensor(name, (rows, width), F32, kind="Internal").ap()

        setup(nc, R, A["x"], A["src"], A["dst"])
        norm_rows(nc, R, "ln0")
        with ExitStack() as gat:
            R.L = gat.enter_context(nc.sbuf_tensor("L", [P, HEADS, TILES], F32))
            layers = ((1, HEADS, "W1s", "W1d", "b1s", "b1d", "attn1", "ln1_w", "ln1_b"),
                      (2, 1, "Wos", "Wod", "bos", "bod", "attno", "lno_w", "lno_b"))
            for n, heads, ws, wd, bs, bd, at, lw, lb in layers:
                ws, wd, bs, bd, at, lw, lb = (A["L0_gnn_" + x] for x in (ws, wd, bs, bd, at, lw, lb))
                at = at.rearrange("h d -> (h d)")
                width = heads * head_width(heads)
                fs = table(f"fs{n}", width)
                with nc.sbuf_tensor(f"fd{n}", [P, NB, width], FR) as R.fd, nc.sbuf_tensor(f"fdl{n}", [P, NB, width], FR) as R.fdl:
                    project(nc, R, f"p{n}", [ws, wd], fs, [bs, bd], at, heads)
                    logits(nc, R, f"l{n}", fs, at, heads)
                edge_softmax(nc, R, f"s{n}", heads)
                with nc.sbuf_tensor(f"acc{n}", [P, NB, width + (n == 1)], F32) as R.acc:
                    aggregate(nc, R, f"a{n}", fs, width, heads, count=(n == 1))
                    finish_gat(nc, R, f"f{n}", heads, lw, lb, n == 1)
        norm_rows(nc, R, "ln1", l2=True)
        with ExitStack() as soft:
            comb = soft.enter_context(nc.sbuf_tensor("comb", [P, NB, SE], F32))
            slotsT = soft.enter_context(nc.sbuf_tensor("slotsT", [P, KD, SE], F32))
            with nc.sbuf_tensor("disp", [P, NB, SE], F32) as disp:
                soft_logits(nc, R, "m1", A["L0_ffn_phi"], A["L0_ffn_scale"], disp, comb, slotsT)
                soft_slots(nc, R, "m2", disp, slotsT)
            eo = R.H
            soft_experts(nc, R, "m3", A["L0_ffn_w1"], A["L0_ffn_b1"], A["L0_ffn_w2"], A["L0_ffn_b2"], slotsT, eo)
            soft_combine(nc, R, "m4", comb, eo)
        norm_rows(nc, R, "ln2")
        with ExitStack() as gcn:
            R.CT = gcn.enter_context(nc.sbuf_tensor("CT", [P, NB, ROWS], F32))
            edge_counts(nc, R, "ec")
            R.out = gcn.enter_context(nc.sbuf_tensor("gcn_out", [P, NB, D], F32))
            gcn_layer(nc, R, "gc1", R.H, A["L1_gnn_W1"], A["L1_gnn_b1"], True)
            gcn_layer(nc, R, "gc2", R.out, A["L1_gnn_W2"], A["L1_gnn_b2"], False)
        norm_rows(nc, R, "ln3")
        R.gate, R.slot = sb("gate", [P, NB, TOP]), sb("slot", [P, NB, TOP], I32)
        R.slot_node, R.block_expert = sb("slot_node", [P, MB], I32), sb("block_expert", [1, MB], I32)
        R.block_fresh = sb("block_fresh", [1, MB], I32)
        R.list = sb("list", [P, 2], I32)
        rows_table, out_table = table("moe_rows", D), table("moe_out", D, MSLOTS)
        slot_table = nc.dram_tensor("moe_slots", (SPARE, 1), I32, kind="Internal").ap()
        route(nc, R, "r1", A["L1_ffn_router_w"], A["L1_ffn_router_b"], rows_table, slot_table)
        experts(nc, R, "r2", rows_table, A["L1_ffn_w1"], A["L1_ffn_b1"], A["L1_ffn_w2"], A["L1_ffn_b2"], out_table)
        combine(nc, R, "r3", out_table, out)


_INS = ["x", "src", "dst", "L0_gnn_W1s", "L0_gnn_b1s", "L0_gnn_W1d", "L0_gnn_b1d", "L0_gnn_attn1", "L0_gnn_ln1_w", "L0_gnn_ln1_b",
        "L0_gnn_Wos", "L0_gnn_bos", "L0_gnn_Wod", "L0_gnn_bod", "L0_gnn_attno", "L0_gnn_lno_w", "L0_gnn_lno_b",
        "L0_ffn_phi", "L0_ffn_scale", "L0_ffn_w1", "L0_ffn_b1", "L0_ffn_w2", "L0_ffn_b2",
        "L1_gnn_W1", "L1_gnn_b1", "L1_gnn_W2", "L1_gnn_b2",
        "L1_ffn_router_w", "L1_ffn_router_b", "L1_ffn_w1", "L1_ffn_b1", "L1_ffn_w2", "L1_ffn_b2"]


def kernel(**inputs):
    import numpy as np
    import concourse.bacc as bacc
    from concourse.bass_utils import run_bass_kernel_spmd as run

    nc = bacc.Bacc("TRN2", target_bir_lowering=False, num_devices=1)
    arrays, args = {}, {}
    for name in _INS:
        a = np.ascontiguousarray(inputs[name])
        arrays[f"in_{name}"] = a
        args[name] = nc.dram_tensor(f"in_{name}", a.shape, mybir.dt.from_np(a.dtype), kind="ExternalInput").ap()
    out = nc.dram_tensor("out", (NODES, D), F32, kind="ExternalOutput").ap()
    program(nc, args, out)
    r = run(nc, [arrays], core_ids=[0])
    return r.results[0]["out"]
```
